# Optimizing a Trainium2 kernel written in Bass

```python
import numpy as np
import jax
import jax.numpy as jnp

def _softmax(x, axis=-1):
    return jax.nn.softmax(x, axis=axis)

def _gelu(x):
    return jax.nn.gelu(x, approximate=True)

def _silu(x):
    return jax.nn.silu(x)

def _sigmoid(x):
    return jax.nn.sigmoid(x)

def _layernorm(x, axis=-1, eps=1e-05):
    m = jnp.mean(x, axis=axis, keepdims=True)
    v = jnp.var(x, axis=axis, keepdims=True)
    return (x - m) / jnp.sqrt(v + eps)

def _scatter_add(tgt, idx, src, axis=0):
    return tgt.at[idx].add(src)

def _segment_sum(src, seg, n):
    return jax.ops.segment_sum(src, seg, n)
kernel_name = 'mk_gnn_ffn_d2_gnn_r32_5ab20e'

def setup_inputs(seed: int=0):
    np.random.seed(seed)
    _w = jnp.asarray

    def _rec_inputs():
        import jax
        import jax.numpy as jnp
        _gk = jax.random.key(seed)
        x = -0.0002117 + 1 * jax.random.normal(jax.random.fold_in(_gk, 1), (3125, 256), jnp.float32)
        src = jax.random.randint(jax.random.fold_in(_gk, 2), (50000,), 0, 3125, jnp.int32)
        dst = jnp.minimum((3125 * jax.random.uniform(jax.random.fold_in(_gk, 3), (50000,)) ** 2.0).astype(jnp.int32), 99999)
        _o = jnp.argsort(dst, stable=True)
        src = src[_o]
        dst = dst[_o]
        edge_attr_5 = jax.random.uniform(jax.random.fold_in(_gk, 12), (50000, 5), jnp.float32, 0.0, 99.9996)
        edge_weight = jax.random.uniform(jax.random.fold_in(_gk, 14), (50000,), jnp.float32, 0.0, 1)
        node_type_19 = jax.random.randint(jax.random.fold_in(_gk, 15), (3125,), 0, 19, jnp.int32)
        return (x, src, dst, edge_attr_5, edge_weight, node_type_19)
    x, src, dst, edge_attr_5, edge_weight, node_type_19 = _rec_inputs()

    def _L0_gnn_setup():
        import jax, jax.numpy as jnp
        import numpy as np
        N = 3125
        D_IN = 256
        D_OUT = 256
        E = 100000
        key = jax.random.key(seed)
        ks = jax.random.split(key, 9)
        x = jax.random.normal(ks[0], (N, D_IN), dtype=jnp.float32)
        edge_src = jax.random.randint(ks[1], (E,), 0, N, dtype=jnp.int32)
        edge_dst = jax.random.randint(ks[2], (E,), 0, N, dtype=jnp.int32)
        edge_weight = jax.random.uniform(ks[3], (E,), dtype=jnp.float32)
        eps = jnp.zeros((1,), dtype=jnp.float32)
        lim1 = 1.0 / np.sqrt(D_IN)
        w1 = jax.random.uniform(ks[4], (D_IN, D_OUT), minval=-lim1, maxval=lim1, dtype=jnp.float32)
        b1 = jax.random.uniform(ks[5], (D_OUT,), minval=-lim1, maxval=lim1, dtype=jnp.float32)
        lim2 = 1.0 / np.sqrt(D_OUT)
        w2 = jax.random.uniform(ks[6], (D_OUT, D_OUT), minval=-lim2, maxval=lim2, dtype=jnp.float32)
        b2 = jax.random.uniform(ks[7], (D_OUT,), minval=-lim2, maxval=lim2, dtype=jnp.float32)
        return {'x': x, 'edge_src': edge_src, 'edge_dst': edge_dst, 'edge_weight': edge_weight, 'eps': eps, 'w1': w1, 'b1': b1, 'w2': w2, 'b2': b2}
    _L0_gnn_all = _L0_gnn_setup()
    _L0_gnn_in = {k: v for k, v in _L0_gnn_all.items() if k in ('eps', 'w1', 'b1', 'w2', 'b2')}
    del _L0_gnn_all

    def _L0_ffn_setup():
        import math
        import jax, jax.numpy as jnp
        import numpy as np
        CAPACITY_FACTOR = 1.25
        key = jax.random.key(seed)
        ks = jax.random.split(key, 5)
        B, L, D, F, E = (8, 256, 256, 1024, 8)
        h = jax.random.normal(ks[0], (B, L, D), dtype=jnp.float32)
        gate_w = jax.random.normal(ks[1], (D, E), dtype=jnp.float32) * 0.02
        gate_b = jnp.zeros((E,), dtype=jnp.float32)
        w1 = jax.random.normal(ks[2], (E, D, F), dtype=jnp.float32) * (1.0 / math.sqrt(D))
        b1 = jnp.zeros((E, F), dtype=jnp.float32)
        w2 = jax.random.normal(ks[3], (E, F, D), dtype=jnp.float32) * (1.0 / math.sqrt(F))
        b2 = jnp.zeros((E, D), dtype=jnp.float32)
        return {'h': h, 'gate_w': gate_w, 'gate_b': gate_b, 'w1': w1, 'b1': b1, 'w2': w2, 'b2': b2}
    _L0_ffn_all = _L0_ffn_setup()
    _L0_ffn_in = {k: v for k, v in _L0_ffn_all.items() if k in ('gate_w', 'gate_b', 'w1', 'b1', 'w2', 'b2')}
    del _L0_ffn_all

    def _L1_gnn_setup():
        import jax, jax.numpy as jnp
        import numpy as np
        N = 1024
        E = 4096
        IN = 256
        OUT = 256
        TD = 32
        H = 4
        T = 19
        PROJ = OUT - 2 * TD
        DK = (OUT - TD) // H
        SQRT_DK = float(np.sqrt(DK))
        LN_EPS = 1e-05

        def time_emb(t, w, b):
            return jnp.cos(jnp.log(t + 1.0)[:, None] * w[None, :] + b[None, :])

        def typed_linear(x, W, b, node_type):
            out = jnp.zeros((x.shape[0], W.shape[2]), x.dtype)
            for t in range(W.shape[0]):
                out = jnp.where((node_type == t)[:, None], x @ W[t] + b[t], out)
            return out

        def seg_softmax(att, idx, n):
            m = jax.ops.segment_max(att, idx, num_segments=n)
            e = jnp.exp(att - m[idx])
            s = jax.ops.segment_sum(e, idx, num_segments=n)
            return e / (s[idx] + 1e-16)
        key = jax.random.key(seed)
        ks = jax.random.split(key, 8)
        x = jax.random.normal(ks[0], (N, IN), jnp.float32)
        node_type = jax.random.randint(ks[1], (N,), 0, T, jnp.int32)
        edge_index = jax.random.randint(ks[2], (2, E), 0, N, jnp.int32)
        times = jax.random.uniform(ks[3], (E, 3), jnp.float32, 0.0, 100.0)
        edge_attr = jnp.concatenate([times, node_type[edge_index[0]][:, None].astype(jnp.float32), node_type[edge_index[1]][:, None].astype(jnp.float32)], axis=1)
        s = 0.02
        Wk = jax.random.normal(ks[4], (T, IN, PROJ), jnp.float32) * s
        Wq = jax.random.normal(ks[5], (T, IN, PROJ), jnp.float32) * s
        Wv = jax.random.normal(ks[6], (T, IN, PROJ), jnp.float32) * s
        bk = jnp.zeros((T, PROJ), jnp.float32)
        bq = jnp.zeros((T, PROJ), jnp.float32)
        bv = jnp.zeros((T, PROJ), jnp.float32)
        Wa = jax.random.normal(ks[7], (T, 2 * OUT, IN), jnp.float32) * s
        ba = jnp.zeros((T, IN), jnp.float32)
        gamma = jnp.ones((T, IN), jnp.float32)
        beta = jnp.zeros((T, IN), jnp.float32)
        w_time = jnp.asarray(1.0 / 10 ** np.linspace(0, 1.5, TD), jnp.float32)
        b_time = jnp.zeros((TD,), jnp.float32)
        return dict(x=x, node_type=node_type, edge_index=edge_index, edge_attr=edge_attr, Wk=Wk, bk=bk, Wq=Wq, bq=bq, Wv=Wv, bv=bv, Wa=Wa, ba=ba, gamma=gamma, beta=beta, w_time=w_time, b_time=b_time)
    _L1_gnn_all = _L1_gnn_setup()
    _L1_gnn_in = {k: v for k, v in _L1_gnn_all.items() if k in ('Wk', 'bk', 'Wq', 'bq', 'Wv', 'bv', 'Wa', 'ba', 'gamma', 'beta', 'w_time', 'b_time')}
    del _L1_gnn_all

    def _L1_ffn_setup():
        import jax, jax.numpy as jnp
        import numpy as np
        DIM = 256
        H = 8
        D = 64
        G = 64
        INNER = H * D
        SCALE = D ** (-0.5)
        key = jax.random.key(seed)
        ks = jax.random.split(key, 12)
        B, N = (4, 512)
        x = jax.random.normal(ks[0], (B, N, DIM), dtype=jnp.float32)
        s = lambda fan_in: 1.0 / np.sqrt(fan_in)
        W_fx = jax.random.normal(ks[1], (DIM, INNER), dtype=jnp.float32) * s(DIM)
        b_fx = jnp.zeros((INNER,), dtype=jnp.float32)
        W_x = jax.random.normal(ks[2], (DIM, INNER), dtype=jnp.float32) * s(DIM)
        b_x = jnp.zeros((INNER,), dtype=jnp.float32)
        A = jax.random.normal(ks[3], (G, D), dtype=jnp.float32)
        Q, _ = jnp.linalg.qr(A.T)
        W_slice = Q[:, :G].astype(jnp.float32)
        b_slice = jnp.zeros((G,), dtype=jnp.float32)
        W_q = jax.random.normal(ks[4], (D, D), dtype=jnp.float32) * s(D)
        W_k = jax.random.normal(ks[5], (D, D), dtype=jnp.float32) * s(D)
        W_v = jax.random.normal(ks[6], (D, D), dtype=jnp.float32) * s(D)
        W_out = jax.random.normal(ks[7], (INNER, DIM), dtype=jnp.float32) * s(INNER)
        b_out = jnp.zeros((DIM,), dtype=jnp.float32)
        temperature = jnp.ones((1, H, 1, 1), dtype=jnp.float32) * 0.5
        return {'x': x, 'W_fx': W_fx, 'b_fx': b_fx, 'W_x': W_x, 'b_x': b_x, 'W_slice': W_slice, 'b_slice': b_slice, 'W_q': W_q, 'W_k': W_k, 'W_v': W_v, 'W_out': W_out, 'b_out': b_out, 'temperature': temperature}
    _L1_ffn_all = _L1_ffn_setup()
    _L1_ffn_in = {k: v for k, v in _L1_ffn_all.items() if k in ('W_fx', 'b_fx', 'W_x', 'b_x', 'W_slice', 'b_slice', 'W_q', 'W_k', 'W_v', 'W_out', 'b_out', 'temperature')}
    del _L1_ffn_all
    return {'x': x, 'src': src, 'dst': dst, 'edge_attr_5': edge_attr_5, 'edge_weight': edge_weight, 'node_type_19': node_type_19, 'L0_gnn_eps': _L0_gnn_in['eps'], 'L0_gnn_w1': _L0_gnn_in['w1'], 'L0_gnn_b1': _L0_gnn_in['b1'], 'L0_gnn_w2': _L0_gnn_in['w2'], 'L0_gnn_b2': _L0_gnn_in['b2'], 'L0_ffn_gate_w': _L0_ffn_in['gate_w'], 'L0_ffn_gate_b': _L0_ffn_in['gate_b'], 'L0_ffn_w1': _L0_ffn_in['w1'], 'L0_ffn_b1': _L0_ffn_in['b1'], 'L0_ffn_w2': _L0_ffn_in['w2'], 'L0_ffn_b2': _L0_ffn_in['b2'], 'L1_gnn_Wk': _L1_gnn_in['Wk'], 'L1_gnn_bk': _L1_gnn_in['bk'], 'L1_gnn_Wq': _L1_gnn_in['Wq'], 'L1_gnn_bq': _L1_gnn_in['bq'], 'L1_gnn_Wv': _L1_gnn_in['Wv'], 'L1_gnn_bv': _L1_gnn_in['bv'], 'L1_gnn_Wa': _L1_gnn_in['Wa'], 'L1_gnn_ba': _L1_gnn_in['ba'], 'L1_gnn_gamma': _L1_gnn_in['gamma'], 'L1_gnn_beta': _L1_gnn_in['beta'], 'L1_gnn_w_time': _L1_gnn_in['w_time'], 'L1_gnn_b_time': _L1_gnn_in['b_time'], 'L1_ffn_W_fx': _L1_ffn_in['W_fx'], 'L1_ffn_b_fx': _L1_ffn_in['b_fx'], 'L1_ffn_W_x': _L1_ffn_in['W_x'], 'L1_ffn_b_x': _L1_ffn_in['b_x'], 'L1_ffn_W_slice': _L1_ffn_in['W_slice'], 'L1_ffn_b_slice': _L1_ffn_in['b_slice'], 'L1_ffn_W_q': _L1_ffn_in['W_q'], 'L1_ffn_W_k': _L1_ffn_in['W_k'], 'L1_ffn_W_v': _L1_ffn_in['W_v'], 'L1_ffn_W_out': _L1_ffn_in['W_out'], 'L1_ffn_b_out': _L1_ffn_in['b_out'], 'L1_ffn_temperature': _L1_ffn_in['temperature']}

def reference(x, src, dst, edge_attr_5, edge_weight, node_type_19, L0_gnn_eps, L0_gnn_w1, L0_gnn_b1, L0_gnn_w2, L0_gnn_b2, L0_ffn_gate_w, L0_ffn_gate_b, L0_ffn_w1, L0_ffn_b1, L0_ffn_w2, L0_ffn_b2, L1_gnn_Wk, L1_gnn_bk, L1_gnn_Wq, L1_gnn_bq, L1_gnn_Wv, L1_gnn_bv, L1_gnn_Wa, L1_gnn_ba, L1_gnn_gamma, L1_gnn_beta, L1_gnn_w_time, L1_gnn_b_time, L1_ffn_W_fx, L1_ffn_b_fx, L1_ffn_W_x, L1_ffn_b_x, L1_ffn_W_slice, L1_ffn_b_slice, L1_ffn_W_q, L1_ffn_W_k, L1_ffn_W_v, L1_ffn_W_out, L1_ffn_b_out, L1_ffn_temperature):
    import jax
    import jax.numpy as jnp

    def _L0_gnn_ref(x, edge_src, edge_dst, edge_weight, eps, w1, b1, w2, b2):
        import jax, jax.numpy as jnp
        import numpy as np
        N = 3125
        D_IN = 256
        D_OUT = 256
        E = 100000
        msgs = edge_weight[:, None] * x[edge_src]
        agg = jax.ops.segment_sum(msgs, edge_dst, num_segments=N)
        h = (1.0 + eps[0]) * x + agg
        h = jax.nn.relu(h @ w1 + b1)
        return h @ w2 + b2

    def _L0_ffn_ref(h, gate_w, gate_b, w1, b1, w2, b2):
        import math
        import jax, jax.numpy as jnp
        import numpy as np
        CAPACITY_FACTOR = 1.25
        B, L, D = h.shape
        E = gate_w.shape[1]
        T = B * L
        C = max(1, math.ceil(CAPACITY_FACTOR * T / E))
        x = h.reshape(T, D)
        logits = x @ gate_w + gate_b
        probs = jax.nn.softmax(logits, axis=-1)
        idx = jnp.argmax(probs, axis=-1)
        prb = jnp.take_along_axis(probs, idx[:, None], axis=1)[:, 0]
        one_hot = jax.nn.one_hot(idx, E, dtype=jnp.float32)
        pos = (jnp.cumsum(one_hot, axis=0) * one_hot).sum(-1).astype(jnp.int32) - 1
        kept = pos < C
        pos_safe = jnp.where(kept, pos, C)
        buf = jnp.zeros((E, C, D), dtype=h.dtype).at[idx, pos_safe].set(x, mode='drop')
        hmid = jax.nn.relu(jnp.einsum('ecd,edf->ecf', buf, w1) + b1[:, None, :])
        ybuf = jnp.einsum('ecf,efd->ecd', hmid, w2) + b2[:, None, :]
        pos_g = jnp.minimum(pos, C - 1)
        y_tok = ybuf[idx, pos_g] * (prb * kept)[:, None]
        y = y_tok.reshape(B, L, D)
        y = jnp.nan_to_num(y, nan=0.0, posinf=10000.0, neginf=-10000.0)
        return y

    def _L1_gnn_ref(x, node_type, edge_index, edge_attr, Wk, bk, Wq, bq, Wv, bv, Wa, ba, gamma, beta, w_time, b_time):
        import jax, jax.numpy as jnp
        import numpy as np
        N = 1024
        E = 4096
        IN = 256
        OUT = 256
        TD = 32
        H = 4
        T = 19
        PROJ = OUT - 2 * TD
        DK = (OUT - TD) // H
        SQRT_DK = float(np.sqrt(DK))
        LN_EPS = 1e-05

        def time_emb(t, w, b):
            return jnp.cos(jnp.log(t + 1.0)[:, None] * w[None, :] + b[None, :])

        def typed_linear(x, W, b, node_type):
            out = jnp.zeros((x.shape[0], W.shape[2]), x.dtype)
            for t in range(W.shape[0]):
                out = jnp.where((node_type == t)[:, None], x @ W[t] + b[t], out)
            return out

        def seg_softmax(att, idx, n):
            m = jax.ops.segment_max(att, idx, num_segments=n)
            e = jnp.exp(att - m[idx])
            s = jax.ops.segment_sum(e, idx, num_segments=n)
            return e / (s[idx] + 1e-16)
        row, col = (edge_index[0], edge_index[1])
        n = x.shape[0]
        K = typed_linear(x, Wk, bk, node_type)
        Q = typed_linear(x, Wq, bq, node_type)
        V = typed_linear(x, Wv, bv, node_type)
        e0 = time_emb(edge_attr[:, 0], w_time, b_time)
        e1 = time_emb(edge_attr[:, 1], w_time, b_time)
        e2 = time_emb(edge_attr[:, 2], w_time, b_time)

        def edge_msgs(Kn, Qn, Vn, ek, eq):
            k = jnp.concatenate([Kn, ek], axis=1).reshape(-1, H, DK)
            q = jnp.concatenate([Qn, eq], axis=1).reshape(-1, H, DK)
            att = jnp.einsum('ehd,ed->eh', k, q.sum(axis=1)) / SQRT_DK
            v = jnp.concatenate([Vn, ek], axis=1).reshape(-1, H, DK)
            return (att, v)
        att, v = edge_msgs(K[row], Q[col], V[row], e1, e2)
        att_i, v_i = edge_msgs(K[col], Q[row], V[col], e2, e1)
        att = seg_softmax(att, col, n)
        att_i = seg_softmax(att_i, row, n)
        res = (v * att[:, :, None]).reshape(-1, H * DK)
        res = jnp.concatenate([res, e0], axis=1)
        res_i = (v_i * att_i[:, :, None]).reshape(-1, H * DK)
        res_i = jnp.concatenate([res_i, e0], axis=1)
        agg = jax.ops.segment_sum(res, col, num_segments=n) + jax.ops.segment_sum(res_i, row, num_segments=n)
        h = jnp.concatenate([agg, agg], axis=1)
        o = typed_linear(h, Wa, ba, node_type)
        y = o + x
        mu = y.mean(axis=-1, keepdims=True)
        var = y.var(axis=-1, keepdims=True)
        yn = (y - mu) / jnp.sqrt(var + LN_EPS)
        return yn * gamma[node_type] + beta[node_type]

    def _L1_ffn_ref(x, W_fx, b_fx, W_x, b_x, W_slice, b_slice, W_q, W_k, W_v, W_out, b_out, temperature):
        import jax, jax.numpy as jnp
        import numpy as np
        DIM = 256
        H = 8
        D = 64
        G = 64
        INNER = H * D
        SCALE = D ** (-0.5)
        B, N, _ = x.shape
        fx_mid = (x @ W_fx + b_fx).reshape(B, N, H, D).transpose(0, 2, 1, 3)
        x_mid = (x @ W_x + b_x).reshape(B, N, H, D).transpose(0, 2, 1, 3)
        temp = jnp.clip(temperature, 0.1, 5.0)
        slice_weights = jax.nn.softmax((x_mid @ W_slice + b_slice) / temp, axis=-1)
        slice_norm = slice_weights.sum(axis=2)
        slice_token = jnp.einsum('bhnc,bhng->bhgc', fx_mid, slice_weights)
        slice_token = slice_token / (slice_norm[..., None] + 1e-05)
        q = slice_token @ W_q
        k = slice_token @ W_k
        v = slice_token @ W_v
        attn = jax.nn.softmax(jnp.einsum('bhgc,bhkc->bhgk', q, k) * SCALE, axis=-1)
        out_slice = jnp.einsum('bhgk,bhkc->bhgc', attn, v)
        out_x = jnp.einsum('bhgc,bhng->bhnc', out_slice, slice_weights)
        out_x = out_x.transpose(0, 2, 1, 3).reshape(B, N, INNER)
        return out_x @ W_out + b_out
    edge_index = jnp.stack([src, dst])
    x = x + _L0_gnn_ref(_layernorm(x, axis=-1), src, dst, edge_weight, L0_gnn_eps, L0_gnn_w1, L0_gnn_b1, L0_gnn_w2, L0_gnn_b2)
    x = x + _L0_ffn_ref(_layernorm(x, axis=-1)[None], L0_ffn_gate_w, L0_ffn_gate_b, L0_ffn_w1, L0_ffn_b1, L0_ffn_w2, L0_ffn_b2)[0]
    x = x + _L1_gnn_ref(_layernorm(x, axis=-1), node_type_19, edge_index, edge_attr_5, L1_gnn_Wk, L1_gnn_bk, L1_gnn_Wq, L1_gnn_bq, L1_gnn_Wv, L1_gnn_bv, L1_gnn_Wa, L1_gnn_ba, L1_gnn_gamma, L1_gnn_beta, L1_gnn_w_time, L1_gnn_b_time)
    x = x + _L1_ffn_ref(_layernorm(x, axis=-1)[None], L1_ffn_W_fx, L1_ffn_b_fx, L1_ffn_W_x, L1_ffn_b_x, L1_ffn_W_slice, L1_ffn_b_slice, L1_ffn_W_q, L1_ffn_W_k, L1_ffn_W_v, L1_ffn_W_out, L1_ffn_b_out, L1_ffn_temperature)[0]
    return x

_drawn_inputs = setup_inputs


def setup_inputs(seed=0):
    import zlib

    import numpy as np

    out = dict(_drawn_inputs(seed))
    spreads = {'L0_ffn_gate_b': (0.0, 0.1),
     'L0_ffn_b1': (0.0, 0.8),
     'L0_ffn_b2': (0.0, 0.619),
     'L1_gnn_bk': (0.0, 0.8),
     'L1_gnn_bq': (0.0, 0.8),
     'L1_gnn_bv': (0.0, 0.8),
     'L1_gnn_ba': (0.0, 0.488),
     'L1_gnn_gamma': (1.0, 0.2),
     'L1_gnn_beta': (0.0, 0.1),
     'L1_gnn_b_time': (0.0, 0.1),
     'L1_ffn_b_fx': (0.0, 0.1),
     'L1_ffn_b_x': (0.0, 0.8),
     'L1_ffn_b_slice': (0.0, 0.8),
     'L1_ffn_b_out': (0.0, 0.1),
     'L1_ffn_temperature': (0.5, 0.6)}
    factors = {'L0_gnn_b1': 3.349,
     'L1_gnn_Wk': 8.0,
     'L1_gnn_Wq': 8.0,
     'L1_gnn_Wv': 5.894,
     'L1_ffn_W_x': 8.0,
     'L1_ffn_W_slice': 8.0,
     'L1_ffn_W_q': 8.0,
     'L1_ffn_W_k': 8.0}
    for name, (base, spread) in spreads.items():
        noise = np.random.default_rng([zlib.crc32(name.encode()), seed]).standard_normal(out[name].shape)
        drawn = base * np.exp(spread * noise) if base else spread * noise
        out[name] = jnp.asarray(drawn.astype(out[name].dtype))
    for name, factor in factors.items():
        out[name] = (out[name] * factor).astype(out[name].dtype)
    return out
```

```python
from contextlib import ExitStack

import concourse.bass as bass
from concourse import mybir

ALU = mybir.AluOpType
ACT = mybir.ActivationFunctionType
AX = mybir.AxisListType
F32 = mybir.dt.float32
BF16 = mybir.dt.bfloat16
I32 = mybir.dt.int32
U32 = mybir.dt.uint32
ds = bass.ds

P = 128
N, D = 3125, 256
NT = 26
TAIL = N - 24 * P
E = 50000
EP, EC = 125, 400
W = 25
NB = 416
U = 4
NIT = NB // U // 2
REC = 128
R_EQ, R_META = 64, 96
CC = 10
PROJ, TD, H1, DK = 192, 32, 4, 56
KV = 2 * PROJ
ROW = KV + 2 * TD
VROW = PROJ + 2 * TD
SROW = D + H1
T1 = 19
TT = 44
EX, F = 8, 1024
CAP = 489
CAPP = 512
H2, G = 8, 64
LN_EPS = 1e-5
BIG = 2.0 ** 100
TWO_PI = 6.283185307179586
MAGIC = 12582912.0
FAR = float(1 << 20)


def build(nc, A, out):
    ctx = ExitStack()
    with ctx:
        ctx.enter_context(nc.allow_non_contiguous_dma(reason="small tables of biases and types"))
        sems = {}

        def sem(name):
            if name not in sems:
                sems[name] = ctx.enter_context(nc.semaphore(name))
            return sems[name]

        def sb(name, shape, dt=F32):
            return ctx.enter_context(nc.sbuf_tensor(name, shape, dt))

        def dram(name, rows, cols):
            return nc.dram_tensor(name, (rows, cols), F32).ap()

        xn_tab = dram("xn_tab", NT * P, D)
        kv_tab = dram("kv_tab", NT * P, KV)
        rec_tab = [dram("rec_dst", NB * P, REC), dram("rec_src", NB * P, REC)]
        v_tab = [dram("v_dst", NB * P, VROW), dram("v_src", NB * P, VROW)]
        moe_in = dram("moe_in", EX * CAPP, D)
        moe_out = dram("moe_out", EX * CAPP, D)
        typ_x = dram("typ_x", TT * P, D)
        typ_agg = dram("typ_agg", TT * P, D)
        typ_kvq = dram("typ_kvq", TT * P, KV + DK)
        typ_y = dram("typ_y", TT * P, D)

        X = sb("X", [P, NT, D])
        XN = sb("XN", [P, NT, D])
        BIGR = sb("BIGR", [P, NT * (SROW + D)])
        ACC = BIGR[:, 0:NT * SROW].rearrange("p (t c) -> p t c", c=SROW)
        AGG = BIGR[:, NT * SROW:].rearrange("p (t c) -> p t c", c=D)
        AR = sb("AR", [P, 15600])
        QS = sb("QS", [P, NT, DK])
        M = sb("M", [P, NT, H1])
        META = [sb("META0", [P, NB, 4]), sb("META1", [P, NB, 4])]
        ident = sb("ident", [P, P])
        identb = sb("identb", [P, P], BF16)
        tri = sb("tri", [P, P])
        ones = sb("ones", [P, P])
        iota1 = sb("iota1", [P, P])
        iotaz = sb("iotaz", [P, P])
        pcol = sb("pcol", [P, 1])
        valid = sb("valid", [P, NT])
        win = [sb("win0", [1, NB], I32), sb("win1", [1, NB], I32)]
        slot_e = [sb("slot_e0", [P, EC], I32), sb("slot_e1", [P, EC], I32)]
        mv = sb("mv", [P, NT, 2])
        rs = sb("rs", [P, 4, NT])
        bst = sb("bst", [P, 2, 6])
        slot_m = sb("slot_m", [P, NT], I32)
        rowof_m = sb("rowof_m", [P, NT], I32)
        gate_p = sb("gate_p", [P, NT])
        slot_t = sb("slot_t", [P, NT], I32)
        rowof_t = sb("rowof_t", [P, NT], I32)
        ttype = sb("ttype", [1, TT], I32)

        def ar(off, *shape, dt=F32):
            n = 1
            for k in shape:
                n *= k
            v = AR[:, off:off + n]
            if dt is not F32:
                v = AR[:, off:off + (n // 2 if dt is BF16 else n)].bitcast(dt)
            if len(shape) == 2:
                v = v.rearrange("p (a b) -> p a b", b=shape[1])
            if len(shape) == 3:
                v = v.rearrange("p (a b c) -> p a b c", b=shape[1], c=shape[2])
            return v

        PS = [ctx.enter_context(nc.psum_tensor(f"ps{k}", [P, 512], F32)) for k in range(8)]

        ids = [ar(0, EC, dt=I32), ar(400, EC, dt=I32)]
        wgt = ar(800, EC)
        lo1 = [ar(1200, EC), ar(1600, EC)]
        attr = ar(2000, EC, 5)
        logt = ar(4000, EC * 3)
        SCAN = ar(5200, W, EC)
        MASK = BIGR[:, 0:W * EC].rearrange("p (a b) -> p a b", b=EC)
        hi_i = ar(15200, EC, dt=I32)
        rk = sb("rk", [P, 5, 32])
        rk_i = sb("rk_i", [P, 32], I32)
        tmpf = BIGR[:, 10400:10816]
        jrow = BIGR[0:1, 12000:12416]
        wt_row = sb("wt_row", [P, 2, TD])
        Z0, Z1 = ar(5200, CC * 3, TD), ar(6160, CC * 3, TD)
        RD = [[ar(7200 + 2560 * s + 1280 * o, CC, REC) for o in range(2)] for s in range(2)]
        scst = [[sb(f"scst{s}{o}", [P, CC], I32) for o in range(2)] for s in range(2)]

        def loads_of(eng, ap_row, maxv, etype):
            _, vals = nc.values_load_multi_w_load_instructions(
                ap_row, engines=[etype], min_val=0, max_val=maxv,
                skip_runtime_bounds_check_because="clamped when the table was computed")
            return vals

        ET = mybir.EngineType
        block = ctx.enter_context(nc.Block())

        def bc(ap, shape):
            return ap.to_broadcast(shape)

        def ln_vector(ve, tag):
            for t in range(NT):
                ve.bn_stats(bst[:, t % 2, :], X[:, t, :])
                ve.drain()
                ve.bn_aggr(mv[:, t, :], bst[:, t % 2, :])
            ve.drain()
            ve.tensor_scalar(rs[:, 0, :], mv[:, :, 1], LN_EPS, None, ALU.add).then_inc(sem("var"), 1)
            ve.wait_ge(sem("sd"), tag)
            newton(ve, rs, slice(0, NT))
            for t in range(NT):
                ve.tensor_scalar(XN[:, t, :], X[:, t, :], mv[:, t, 0:1], rs[:, 3, t:t + 1],
                                 ALU.subtract, ALU.mult).then_inc(sem("xn"), 1)
            ve.drain()

        def newton(ve, r, sl):
            ve.reciprocal(r[:, 2, sl], r[:, 1, sl])
            ve.drain()
            ve.tensor_tensor(r[:, 2, sl], r[:, 2, sl], r[:, 0, sl], ALU.mult)
            ve.drain()
            ve.tensor_tensor(r[:, 2, sl], r[:, 2, sl], r[:, 1, sl], ALU.add)
            ve.drain()
            ve.tensor_scalar(r[:, 2, sl], r[:, 2, sl], 0.5, None, ALU.mult)
            ve.drain()
            ve.reciprocal(r[:, 3, sl], r[:, 2, sl])
            ve.drain()

        def ln_scalar(act, tag):
            act.wait_ge(sem("var"), tag)
            act.activation(rs[:, 1, :], rs[:, 0, :], ACT.Sqrt).then_inc(sem("sd"), 1)

        def consts_pool(pool):
            pool.memset(ident[:, :], 0.0)
            pool.memset(tri[:, :], 1.0)
            pool.memset(ones[:, :], 1.0)
            pool.iota(iota1[:, :], [[1, P]], base=1, channel_multiplier=0, allow_small_or_imprecise_dtypes=True)
            pool.iota(iotaz[:, :], [[1, P]], base=0, channel_multiplier=0, allow_small_or_imprecise_dtypes=True)
            pool.iota(pcol[:, :], [[0, 1]], base=0, channel_multiplier=1, allow_small_or_imprecise_dtypes=True)
            pool.iota(jrow, [[1, NB]], base=0, channel_multiplier=0, allow_small_or_imprecise_dtypes=True)
            pool.drain()
            pool.affine_select(out=ident[:, :], in_=ident[:, :], compare_op=ALU.not_equal, fill=1.0, base=0,
                               pattern=[[-1, P]], channel_multiplier=1)
            pool.affine_select(out=tri[:, :], in_=tri[:, :], compare_op=ALU.is_gt, fill=0.0, base=0,
                               pattern=[[1, P]], channel_multiplier=-1)
            pool.drain()
            pool.tensor_copy(identb[:, :], ident[:, :]).then_inc(sem("consts"), 1)

        ZR = BIGR[:, 10900:11924]

        def zero_view(tab, rows, cols):
            return tab.rearrange("(p c) w -> p (c w)", p=P).rearrange("p (k n) -> p k n", n=1024)

        def loads_sync(sp):
            sp.dma_start(ids[0][0:EP], A["dst"].rearrange("(p c) -> p c", p=EP)).then_inc(sem("ids"), 16)
            sp.dma_start(ids[1][0:EP], A["src"].rearrange("(p c) -> p c", p=EP)).then_inc(sem("ids"), 16)
            sp.wait_ge(sem("xpad"), 1)
            sp.dma_start(X[:, 0:24, :], A["x"][0:24 * P, :].rearrange("(t p) d -> p t d", p=P)).then_inc(sem("x_in"), 16)
            sp.dma_start(X[0:TAIL, 24, :], A["x"][24 * P:N, :]).then_inc(sem("x_in"), 16)
            sp.dma_start(attr[0:EP], A["edge_attr_5"].rearrange("(p c) k -> p c k", p=EP)).then_inc(sem("edges_in"), 16)
            sp.dma_start(wgt[0:EP], A["edge_weight"].rearrange("(p c) -> p c", p=EP)).then_inc(sem("edges_in"), 16)
            for k, name in enumerate(("L1_gnn_w_time", "L1_gnn_b_time")):
                sp.dma_start(wt_row[:, k, :], A[name].rearrange("(a n) -> a n", a=1).to_broadcast([P, TD])).then_inc(sem("edges_in"), 16)
            sp.wait_ge(sem("zeros"), 1)
            for tab, rows, cols in ((rec_tab[0], NB * P, REC), (rec_tab[1], NB * P, REC), (moe_in, EX * CAPP, D),
                                    (typ_x, TT * P, D), (typ_agg, TT * P, D)):
                v = zero_view(tab, rows, cols)
                sp.dma_start(v, ZR.unsqueeze(1).to_broadcast([P, v.shape[1], 1024])).then_inc(sem("zeroed"), 16)
            for t in range(NT):
                sp.wait_ge(sem("xn"), t + 1)
            sp.dma_start(xn_tab.rearrange("(t p) d -> p t d", p=P), XN[:, :, :]).then_inc(sem("xn_tab"), 16)

        def rank_vector(ve, o):
            ve.tensor_scalar(hi_i[0:EP], ids[o][0:EP], 7, None, ALU.arith_shift_right)
            ve.drain()
            ve.tensor_copy(tmpf[0:EP, 0:EC], hi_i[0:EP])
            ve.drain()
            ve.tensor_scalar(hi_i[0:EP], ids[o][0:EP], 127, None, ALU.bitwise_and)
            ve.tensor_tensor(MASK[0:EP], tmpf[0:EP, 0:EC].unsqueeze(1).to_broadcast([EP, W, EC]),
                             iotaz[0:EP, 0:W].unsqueeze(2).to_broadcast([EP, W, EC]), ALU.is_equal)
            ve.drain()
            ve.tensor_scalar(lo1[o][0:EP], hi_i[0:EP], 1.0, None, ALU.add)
            ve.tensor_reduce(rk[0:EP, 0, 0:W], MASK[0:EP], AX.X, ALU.add).then_inc(sem("tot_e"), 1)
            ve.wait_ge(sem("cross_e"), o + 1)
            ve.tensor_scalar(rk_i[:, 0:W], PS[0][:, 32:32 + W], 127.0, None, ALU.add)
            ve.drain()
            ve.tensor_scalar(rk_i[:, 0:W], rk_i[:, 0:W], 7, None, ALU.arith_shift_right)
            ve.drain()
            ve.tensor_copy(rk[:, 1, 0:W], rk_i[:, 0:W])
            ve.drain()
            ve.tensor_tensor_scan(rk[:, 2, 0:W], ones[:, 0:W], rk[:, 1, 0:W], 0.0, ALU.mult, ALU.add)
            ve.drain()
            ve.tensor_tensor(rk[:, 3, 0:W], rk[:, 2, 0:W], rk[:, 1, 0:W], ALU.subtract)
            ve.drain()
            ve.scalar_tensor_tensor(out=rk[0:EP, 4, 0:W], in0=rk[0:EP, 3, 0:W], scalar=128.0, in1=PS[0][0:EP, 0:W],
                                    op0=ALU.mult, op1=ALU.add)
            ve.drain()
            for w in range(W):
                ve.tensor_tensor_scan(SCAN[0:EP, w, :], bc(ones[0:EP, 0:1], [EP, EC]), MASK[0:EP, w, :],
                                      rk[0:EP, 4, w:w + 1], ALU.mult, ALU.add)
            ve.drain()
            ve.tensor_tensor(MASK[0:EP], MASK[0:EP], SCAN[0:EP], ALU.mult)
            ve.drain()
            ve.tensor_reduce(tmpf[0:EP, 0:EC], MASK[0:EP].rearrange("p w j -> p j w"), AX.X, ALU.add)
            ve.drain()
            ve.tensor_scalar(slot_e[o][0:EP], tmpf[0:EP, 0:EC], -1.0, None, ALU.add)
            cmp = MASK[0:1].rearrange("p a b -> p (a b)")[:, 0:208 * W].rearrange("p (j w) -> p j w", w=W)
            for half in range(2):
                js = slice(208 * half, 208 * half + 208)
                ve.drain()
                ve.tensor_tensor(cmp, rk[0:1, 2, 0:W].unsqueeze(1).to_broadcast([1, 208, W]),
                                 jrow[:, js].unsqueeze(2).to_broadcast([1, 208, W]), ALU.is_le)
                ve.drain()
                ve.tensor_reduce(tmpf[0:1, js], cmp, AX.X, ALU.add)
            ve.drain()
            ve.tensor_scalar(win[o][:, :], tmpf[0:1, 0:NB], float(W - 1), None, ALU.min).then_inc(sem("win"), 1)
            ve.drain()

        def rank_tensor(pe, o):
            pe.wait_ge(sem("consts"), 1)
            pe.wait_ge(sem("tot_e"), o + 1)
            pe.matmul(PS[0][0:EP, 0:W], tri[0:EP, 0:EP], rk[0:EP, 0, 0:W], start=True, stop=True)
            pe.matmul(PS[0][:, 32:32 + W], ones[0:EP, :], rk[0:EP, 0, 0:W], start=True, stop=True).then_inc(sem("cross_e"), 1)


        def run(eng, n, body):
            body(0, True)
            with eng.Fori(1, n) as i:
                body(i, False)

        NCH = EC // CC // 2

        def embed_vector(ve):
            ve.wait_ge(sem("edges_in"), 64)
            ve.tensor_scalar(wt_row[:, 1, :], wt_row[:, 1, :], TWO_PI / 4, None, ALU.add)
            for s in range(2):
                for o in range(2):
                    ve.memset(RD[s][o], 0.0)
            ve.drain()
            ve.wait_ge(sem("logt"), 1)

            def body(i, first):
                for s in range(2):
                    c = 2 * i + s
                    if not first:
                        ve.wait_ge(sem(f"rd_sent{s}"), 16 * 2 * CC * i)
                        ve.wait_ge(sem("sin_done"), 2 * i + s)
                    elif s:
                        ve.wait_ge(sem("sin_done"), 1)
                    ve.tensor_tensor(Z0[0:EP], logt[0:EP, ds(c * 3 * CC, 3 * CC)].unsqueeze(2).to_broadcast([EP, 3 * CC, TD]),
                                     wt_row[0:EP, 0, :].unsqueeze(1).to_broadcast([EP, 3 * CC, TD]), ALU.mult)
                    ve.drain()
                    ve.tensor_tensor(Z0[0:EP], Z0[0:EP], wt_row[0:EP, 1, :].unsqueeze(1).to_broadcast([EP, 3 * CC, TD]), ALU.add)
                    ve.drain()
                    ve.tensor_scalar(Z1[0:EP], Z0[0:EP], 1.0 / TWO_PI, MAGIC, ALU.mult, ALU.add)
                    ve.drain()
                    ve.tensor_scalar(Z1[0:EP], Z1[0:EP], MAGIC, -TWO_PI, ALU.subtract, ALU.mult)
                    ve.drain()
                    ve.tensor_tensor(Z0[0:EP], Z0[0:EP], Z1[0:EP], ALU.add)
                    ve.drain()
                    ve.tensor_scalar(Z0[0:EP], Z0[0:EP], 3.1415925, -3.1415925, ALU.min, ALU.max).then_inc(sem("z_ready"), 1)
                    for o in range(2):
                        r = RD[s][o]
                        ve.tensor_copy(r[0:EP, :, R_META].bitcast(I32), ids[1 - o][0:EP, ds(c * CC, CC)])
                        ve.tensor_copy(r[0:EP, :, R_META + 1], lo1[o][0:EP, ds(c * CC, CC)])
                        ve.tensor_copy(r[0:EP, :, R_META + 2], wgt[0:EP, ds(c * CC, CC)]).then_inc(sem("rd_meta"), 1)

            run(ve, NCH, body)
            ve.drain()

        def embed_scalar(act):
            act.wait_ge(sem("edges_in"), 64)
            act.activation(logt[0:EP].rearrange("p (j k) -> p j k", k=3), attr[0:EP, :, 0:3], ACT.Ln, bias=1.0).then_inc(sem("logt"), 1)

            def body(i, first):
                for s in range(2):
                    act.wait_ge(sem("z_ready"), 2 * i + s + 1)
                    z = Z0.rearrange("p (j k) n -> p j k n", k=3)
                    for o, order in enumerate(((1, 0, 2), (2, 0, 1))):
                        for q, k in enumerate(order):
                            ins = act.activation(RD[s][o][0:EP, :, q * TD:(q + 1) * TD], z[0:EP, :, k, :], ACT.Sin)
                    ins.then_inc(sem("sin_done"), 1)

            run(act, NCH, body)

        def scatter_pool(pool):
            pool.wait_ge(sem("win"), 2)
            pool.wait_ge(sem("zeroed"), 16 * 5)

            def body(i, first):
                for s in range(2):
                    c = 2 * i + s
                    if not first:
                        pool.wait_ge(sem(f"rd_sent{s}"), 16 * 2 * CC * i)
                    for o in range(2):
                        pool.tensor_copy(scst[s][o][:, :], slot_e[o][:, ds(c * CC, CC)]).then_inc(sem("scst"), 1)
                    pool.wait_ge(sem("scst"), 4 * i + 2 * s + 2)
                    pool.wait_ge(sem("sin_done"), 2 * i + s + 1)
                    pool.wait_ge(sem("rd_meta"), 4 * i + 2 * s + 2)
                    pool.nop(nofuse=True)
                    for o in range(2):
                        for k in range(CC):
                            pool.indirect_dma_start(
                                rec_tab[o], bass.IndirectOffsetOnAxis(ap=scst[s][o][:, k:k + 1].bitcast(U32), axis=0),
                                RD[s][o][:, k, :], None, bounds_check=NB * P - 1, oob_is_err=False,
                            ).then_inc(sem(f"rd_sent{s}"), 16)

            run(pool, NCH, body)

        def meta_sync(sp):
            for s in range(2):
                sp.wait_ge(sem(f"rd_sent{s}"), 16 * 2 * CC * NCH)
            for o in range(2):
                v = rec_tab[o].rearrange("(b p) c -> p b c", p=P)
                for q in range(4):
                    bs = slice(104 * q, 104 * q + 104)
                    sp.dma_start(META[o][:, bs, :], v[:, bs, R_META:R_META + 4]).then_inc(sem(f"meta{o}"), 16)

        GA = [ar(1024 * s, U, D) for s in range(2)]
        OW = [ar(2048 + 512 * s, U, P) for s in range(2)]
        MST = [sb(f"mst{s}", [P, U, 4]) for s in range(2)]
        IST = [sb(f"ist{s}", [P, U], I32) for s in range(2)]

        def l0_ps(s, u):
            return PS[2 * s + u // 2][:, (u % 2) * D:(u % 2) * D + D]

        def l0_pool(pool):
            pool.wait_ge(sem("meta0"), 64)
            pool.wait_ge(sem("xn_tab"), 16)

            def body(i, first):
                for s in range(2):
                    b = (2 * i + s) * U
                    if not first:
                        pool.wait_ge(sem("l0_mm"), 2 * i + s - 1)
                    pool.tensor_copy(IST[s][:, :], META[0][:, ds(b, U), 0].bitcast(I32)).then_inc(sem("ist"), 1)
                    pool.wait_ge(sem("ist"), 2 * i + s + 1)
                    pool.nop(nofuse=True)
                    for u in range(U):
                        pool.indirect_dma_start(GA[s][:, u, :], None, xn_tab,
                                                bass.IndirectOffsetOnAxis(ap=IST[s][:, u:u + 1].bitcast(U32), axis=0)
                                                ).then_inc(sem(f"l0_rows{s}"), 16)

            run(pool, NIT, body)

        def l0_vector(ve):
            ve.wait_ge(sem("meta0"), 64)
            ve.wait_ge(sem("zeroed"), 80)
            ve.memset(BIGR[:, 0:NT * SROW], 0.0)
            ve.drain()

            def body(i, first):
                for s in range(2):
                    b = (2 * i + s) * U
                    if not first:
                        ve.wait_ge(sem("l0_mm"), 2 * i + s - 1)
                    ve.tensor_copy(MST[s][:, :, :], META[0][:, ds(b, U), :])
                    ve.drain()
                    for u in range(U):
                        ins = ve.tensor_scalar(OW[s][:, u, :], iota1[:, :], MST[s][:, u, 1:2], MST[s][:, u, 2:3],
                                               ALU.is_equal, ALU.mult)
                    ins.then_inc(sem("l0_ow"), 1)
                for s in range(2):
                    b = (2 * i + s) * U
                    ws = loads_of(ve, win[0][0:1, ds(b, U)], W - 1, ET.DVE)
                    ve.wait_ge(sem("l0_mm"), 2 * i + s + 1)
                    for u in range(U):
                        a = ACC[:, ds(ws[u], 1), 0:D].rearrange("p t d -> p (t d)")
                        ins = ve.tensor_tensor(a, a, l0_ps(s, u), ALU.add)
                        ve.drain()
                    ins.then_inc(sem("l0_add"), 1)

            run(ve, NIT, body)

        def l0_tensor(pe):
            def body(i, first):
                for s in range(2):
                    pe.wait_ge(sem("l0_ow"), 2 * i + s + 1)
                    pe.wait_ge(sem(f"l0_rows{s}"), 64 * (i + 1))
                    if not first:
                        pe.wait_ge(sem("l0_add"), 2 * i + s - 1)
                    for u in range(U):
                        ins = pe.matmul(l0_ps(s, u), OW[s][:, u, :], GA[s][:, u, :], start=True, stop=True)
                    ins.then_inc(sem("l0_mm"), 1)

            run(pe, NIT, body)


        NH = NT // 2
        w1_sb, w2_sb = ar(3100, 2, D), ar(3612, 2, D)
        b1c, b2r, epsc = ar(4124, 2), ar(4126, 1, D), ar(4382, 1)
        HS = [ar(4400 + 256 * s, D) for s in range(2)]
        HTS = [ar(4912 + 256 * s, 2, P) for s in range(2)]
        ZTS = [ar(5424 + 256 * s, 2, P) for s in range(2)]

        def mlp_sync(sp):
            for s in range(2):
                sp.wait_ge(sem(f"rd_sent{s}"), 16 * 2 * CC * NCH)
            sp.dma_start(w1_sb, A["L0_gnn_w1"].rearrange("(k p) n -> p k n", p=P)).then_inc(sem("mlp_w"), 16)
            sp.dma_start(w2_sb, A["L0_gnn_w2"].rearrange("(k p) n -> p k n", p=P)).then_inc(sem("mlp_w"), 16)
            sp.dma_start(b1c, A["L0_gnn_b1"].rearrange("(k p) -> p k", p=P)).then_inc(sem("mlp_w"), 16)
            sp.dma_start(b2r[0:1, 0, :], A["L0_gnn_b2"].rearrange("(a n) -> a n", a=1)).then_inc(sem("mlp_w"), 16)
            sp.dma_start(epsc, A["L0_gnn_eps"].rearrange("(a n) -> a n", a=1).to_broadcast([P, 1])).then_inc(sem("mlp_w"), 16)

        def mlp_vector(ve):
            ve.wait_ge(sem("mlp_w"), 80)
            ve.tensor_scalar(epsc, epsc, 1.0, None, ALU.add)
            ve.drain()

            def body(i, first):
                for s in range(2):
                    t = 2 * i + s
                    if not first:
                        ve.wait_ge(sem("mlp_ht"), 2 * i + s - 1)
                    ve.scalar_tensor_tensor(out=HS[s], in0=XN[:, ds(t, 1), :].rearrange("p t d -> p (t d)"), scalar=epsc,
                                            in1=ACC[:, ds(t, 1), 0:D].rearrange("p t d -> p (t d)"),
                                            op0=ALU.mult, op1=ALU.add).then_inc(sem("mlp_h"), 1)
                for s in range(2):
                    t = 2 * i + s
                    ve.wait_ge(sem("mlp_y"), 2 * i + s + 1)
                    x = X[:, ds(t, 1), :].rearrange("p t d -> p (t d)")
                    ve.tensor_tensor(x, x, PS[4 + s][:, 0:D], ALU.add).then_inc(sem("mlp_x"), 1)

            run(ve, NH, body)
            ve.drain()

        def mlp_tensor(pe):
            pe.wait_ge(sem("mlp_w"), 80)

            def body(i, first):
                for s in range(2):
                    pe.wait_ge(sem("mlp_h"), 2 * i + s + 1)
                    for k in range(2):
                        ins = pe.transpose(PS[s][:, k * P:(k + 1) * P], HS[s][:, k * P:(k + 1) * P], ident[:, :])
                    ins.then_inc(sem("mlp_ht"), 1)
                for s in range(2):
                    pe.wait_ge(sem("mlp_hts"), 2 * i + s + 1)
                    for f in range(2):
                        for k in range(2):
                            ins = pe.matmul(PS[2 + s][:, f * P:(f + 1) * P], w1_sb[:, k, f * P:(f + 1) * P], HTS[s][:, k, :],
                                            start=(k == 0), stop=(k == 1))
                    ins.then_inc(sem("mlp_z"), 1)
                for s in range(2):
                    pe.wait_ge(sem("mlp_zs"), 2 * (2 * i + s + 1))
                    if not first:
                        pe.wait_ge(sem("mlp_x"), 2 * i + s - 1)
                    for k in range(2):
                        pe.matmul(PS[4 + s][:, 0:D], ZTS[s][:, k, :], w2_sb[:, k, :], start=(k == 0), stop=False)
                    pe.matmul(PS[4 + s][:, 0:D], ones[0:1, :], b2r[0:1, 0, :], start=False, stop=True).then_inc(sem("mlp_y"), 1)

            run(pe, NH, body)

        def mlp_scalar(act):
            act.wait_ge(sem("mlp_w"), 80)

            def body(i, first):
                for s in range(2):
                    act.wait_ge(sem("mlp_ht"), 2 * i + s + 1)
                    act.activation(HTS[s].rearrange("p k n -> p (k n)"), PS[s][:, 0:D], ACT.Copy).then_inc(sem("mlp_hts"), 1)
                for s in range(2):
                    act.wait_ge(sem("mlp_z"), 2 * i + s + 1)
                    for f in range(2):
                        act.activation(ZTS[s][:, f, :], PS[2 + s][:, f * P:(f + 1) * P], ACT.Relu,
                                       bias=b1c[:, f:f + 1]).then_inc(sem("mlp_zs"), 1)

            run(act, NH, body)

        def place_tensor(pe, tag, OH, n):
            pe.wait_ge(sem(f"oh_{tag}"), 1)
            pe.matmul(PS[0][:, 0:NT * n], tri[:, :], OH, start=True, stop=True)
            pe.matmul(PS[1][:, 0:NT * n], ones[:, :], OH, start=True, stop=True).then_inc(sem(f"cnt_{tag}"), 1)

        def place_vector(ve, tag, OH, n, TOT, INC, EXC):
            ve.wait_ge(sem(f"cnt_{tag}"), 1)
            ve.tensor_copy(TOT, PS[1][:, 0:NT * n].rearrange("p (t g) -> p t g", g=n))
            ve.drain()
            for g in range(n):
                ve.tensor_tensor_scan(INC[:, :, g], ones[:, 0:NT], TOT[:, :, g], 0.0, ALU.mult, ALU.add)
            ve.drain()
            ve.tensor_tensor(EXC, INC, TOT, ALU.subtract)
            ve.drain()
            ve.tensor_tensor(EXC, EXC, PS[0][:, 0:NT * n].rearrange("p (t g) -> p t g", g=n), ALU.add)
            ve.drain()

        gw_sb, gb_row = ar(0, 2, EX), ar(16, 1, EX)
        XTG = [ar(32 + 256 * s, 2, P) for s in range(2)]
        LG, OHm, T8a, T8b, T8c = (ar(600 + 208 * k, NT, EX) for k in range(5))
        R26 = ar(1700, 8, NT)
        b1T = ar(2000, EX * F // P)
        b2e = ar(2064, EX * D)
        b1raw = ar(4112, P)
        ME = 4300
        XE = [ar(ME + 1024 * s, 4, D) for s in range(2)]
        XET = ar(ME + 2048, 2, 4 * P)
        YB = ar(ME + 3072, 4, D)
        MW = [[BIGR[:, 4096 * s:4096 * s + 2048].rearrange("p (k n) -> p k n", k=2),
               BIGR[:, 4096 * s + 2048:4096 * s + 4096].rearrange("p (k n) -> p k n", k=8)] for s in range(2)]
        HM = BIGR[:, 8192:12288].rearrange("p (f n) -> p f n", f=8)
        b1s = [sb(f"b1s{s}", [P, 8]) for s in range(2)]

        def route_sync(sp):
            sp.wait_ge(sem("mlp_x"), NT)
            sp.dma_start(gw_sb, A["L0_ffn_gate_w"].rearrange("(k p) n -> p k n", p=P)).then_inc(sem("gw"), 16)
            sp.dma_start(gb_row[0:1, 0, :], A["L0_ffn_gate_b"].rearrange("(a n) -> a n", a=1)).then_inc(sem("gw"), 16)
            sp.dma_start(b1raw[0:64, :], A["L0_ffn_b1"].rearrange("e (f p) -> (e f) p", p=P)).then_inc(sem("gw"), 16)
            sp.dma_start(b2e[0:1, :], A["L0_ffn_b2"].rearrange("(a e) n -> a (e n)", a=1)).then_inc(sem("gw"), 16)

        def route_tensor(pe):
            pe.wait_ge(sem("gw"), 64)
            pe.transpose(PS[7][:, 0:64], b1raw[0:64, :], ident[0:64, 0:64]).then_inc(sem("b1T"), 1)
            for t in range(NT):
                pe.wait_ge(sem("xn"), NT + t + 1)
                if t >= 2:
                    pe.wait_ge(sem("xtg"), t - 1)
                for k in range(2):
                    ins = pe.transpose(PS[t % 2][:, k * P:(k + 1) * P], XN[:, t, k * P:(k + 1) * P], ident[:, :])
                ins.then_inc(sem("xtg_ps"), 1)
                pe.wait_ge(sem("xtg"), t + 1)
                lg = PS[6][:, t * EX:(t + 1) * EX]
                for k in range(2):
                    pe.matmul(lg, XTG[t % 2][:, k, :], gw_sb[:, k, :], start=(k == 0), stop=False)
                ins = pe.matmul(lg, ones[0:1, :], gb_row[0:1, 0, :], start=False, stop=True)
                if t == NT - 1:
                    ins.then_inc(sem("gate_lg"), 1)
                else:
                    ins.then_inc(sem("gate_mm"), 1)
            place_tensor(pe, "m", OHm.rearrange("p t g -> p (t g)"), EX)

        def route_scalar(act):
            act.wait_ge(sem("b1T"), 1)
            act.activation(b1T, PS[7][:, 0:64], ACT.Copy).then_inc(sem("b1T_sb"), 1)
            for t in range(NT):
                act.wait_ge(sem("xtg_ps"), t + 1)
                if t >= 2:
                    act.wait_ge(sem("gate_mm"), t - 1)
                act.activation(XTG[t % 2].rearrange("p k n -> p (k n)"), PS[t % 2][:, 0:D], ACT.Copy).then_inc(sem("xtg"), 1)
            act.wait_ge(sem("gate_sub"), 1)
            act.activation(T8a, T8a, ACT.Exp).then_inc(sem("gate_exp"), 1)

        def route_vector(ve):
            e_row = iotaz[:, 0:EX].unsqueeze(1).to_broadcast([P, NT, EX])
            ve.tensor_scalar(valid[:, 24:25], pcol[:, :], float(TAIL), None, ALU.is_lt)
            ve.memset(valid[:, 0:24], 1.0)
            ve.memset(valid[:, 25:26], 0.0)
            ve.wait_ge(sem("gate_lg"), 1)
            ve.tensor_copy(LG, PS[6][:, 0:NT * EX].rearrange("p (t g) -> p t g", g=EX))
            ve.drain()
            ve.tensor_reduce(R26[:, 0, :], LG, AX.X, ALU.max)
            ve.drain()
            ve.tensor_tensor(T8a, LG, R26[:, 0, :].unsqueeze(2).to_broadcast([P, NT, EX]), ALU.subtract).then_inc(sem("gate_sub"), 1)
            ve.tensor_tensor(T8b, LG, R26[:, 0, :].unsqueeze(2).to_broadcast([P, NT, EX]), ALU.is_equal)
            ve.tensor_scalar(T8c, e_row, -100.0, None, ALU.add)
            ve.drain()
            ve.tensor_tensor(T8b, T8b, T8c, ALU.mult)
            ve.drain()
            ve.tensor_reduce(R26[:, 1, :], T8b, AX.X, ALU.min)
            ve.drain()
            ve.tensor_scalar(R26[:, 1, :], R26[:, 1, :], 100.0, None, ALU.add)
            ve.drain()
            ve.tensor_tensor(OHm, e_row, R26[:, 1, :].unsqueeze(2).to_broadcast([P, NT, EX]), ALU.is_equal)
            ve.drain()
            ve.tensor_tensor(OHm, OHm, valid[:, :].unsqueeze(2).to_broadcast([P, NT, EX]), ALU.mult).then_inc(sem("oh_m"), 1)
            ve.wait_ge(sem("gate_exp"), 1)
            ve.tensor_reduce(R26[:, 2, :], T8a, AX.X, ALU.add)
            ve.drain()
            ve.reciprocal(R26[:, 3, :], R26[:, 2, :])
            place_vector(ve, "m", OHm, EX, T8b, T8c, T8a)
            ve.tensor_tensor(T8b, T8a, OHm, ALU.mult)
            ve.drain()
            ve.tensor_reduce(R26[:, 4, :], T8b, AX.X, ALU.add)
            ve.drain()
            ve.tensor_scalar(R26[:, 5, :], R26[:, 4, :], float(CAP), None, ALU.is_lt)
            ve.drain()
            ve.tensor_tensor(R26[:, 5, :], R26[:, 5, :], valid[:, :], ALU.mult)
            ve.scalar_tensor_tensor(out=R26[:, 4, :], in0=R26[:, 1, :], scalar=float(CAPP), in1=R26[:, 4, :],
                                    op0=ALU.mult, op1=ALU.add)
            ve.drain()
            ve.tensor_tensor(gate_p[:, :], R26[:, 3, :], R26[:, 5, :], ALU.mult)
            ve.tensor_tensor(R26[:, 6, :], R26[:, 4, :], R26[:, 5, :], ALU.mult)
            ve.tensor_scalar(R26[:, 7, :], R26[:, 5, :], -FAR, FAR, ALU.mult, ALU.add)
            ve.drain()
            ve.tensor_copy(rowof_m[:, :], R26[:, 6, :])
            ve.tensor_tensor(R26[:, 7, :], R26[:, 7, :], R26[:, 6, :], ALU.add)
            ve.drain()
            ve.tensor_copy(slot_m[:, :], R26[:, 7, :]).then_inc(sem("slot_m"), 1)
            ve.drain()

        def route_pool(pool):
            pool.wait_ge(sem("slot_m"), 1)
            for t in range(25):
                pool.indirect_dma_start(moe_in, bass.IndirectOffsetOnAxis(ap=slot_m[:, t:t + 1].bitcast(U32), axis=0),
                                        XN[:, t, :], None, bounds_check=EX * CAPP - 1, oob_is_err=False
                                        ).then_inc(sem("moe_in"), 16)

        def experts_sync(sp):
            sp.wait_ge(sem("moe_in"), 16 * 25)
            w1 = A["L0_ffn_w1"].rearrange("e (k p) n -> p (e k) n", p=P)
            w2 = A["L0_ffn_w2"].rearrange("e (k p) n -> p (e k) n", p=P)
            xin = moe_in.rearrange("(b p) d -> p b d", p=P)
            yout = moe_out.rearrange("(b p) d -> p b d", p=P)

            def body(i, first):
                for s in range(2):
                    e = 2 * i + s
                    if not first:
                        sp.wait_ge(sem("ex_y"), 4 * (2 * i + s - 1))
                        sp.nop(nofuse=True)
                    sp.dma_start(XE[s], xin[:, ds(4 * e, 4), :]).then_inc(sem(f"ex_in{s}"), 16)
                    sp.dma_start(MW[s][0], w1[:, ds(2 * e, 2), :]).then_inc(sem(f"ex_in{s}"), 16)
                    sp.dma_start(MW[s][1], w2[:, ds(8 * e, 8), :]).then_inc(sem(f"ex_in{s}"), 16)
                for s in range(2):
                    e = 2 * i + s
                    sp.wait_ge(sem("ex_ys"), 4 * (e + 1))
                    sp.nop(nofuse=True)
                    sp.dma_start(yout[:, ds(4 * e, 4), :], YB).then_inc(sem("ex_out"), 16)

            run(sp, EX // 2, body)

        def experts_tensor(pe):
            def body(i, first):
                for s in range(2):
                    e = 2 * i + s
                    pe.wait_ge(sem(f"ex_in{s}"), 48 * (i + 1))
                    for k in range(2):
                        for t in range(4):
                            ins = pe.transpose(PS[k][:, t * P:(t + 1) * P], XE[s][:, t, k * P:(k + 1) * P], ident[:, :])
                        ins.then_inc(sem("ex_xt"), 1)
                    pe.wait_ge(sem("ex_xts"), e + 1)
                    pe.wait_ge(sem("ex_xts2"), e + 1)
                    for f in range(8):
                        if f >= 2 or s or not first:
                            pe.wait_ge(sem("ex_hs"), 8 * e + f - 1)
                        for k in range(2):
                            ins = pe.matmul(PS[2 + f % 2][:, :], MW[s][0][:, k, f * P:(f + 1) * P], XET[:, k, :],
                                            start=(k == 0), stop=(k == 1))
                        ins.then_inc(sem("ex_h"), 1)
                    pe.wait_ge(sem("ex_hs"), 8 * (e + 1))
                    if s or not first:
                        pe.wait_ge(sem("ex_ys"), 4 * e)
                    for t in range(4):
                        y = PS[4 + t][:, 0:D]
                        for f in range(8):
                            pe.matmul(y, HM[:, f, t * P:(t + 1) * P], MW[s][1][:, f, :], start=(f == 0), stop=False)
                        pe.matmul(y, ones[0:1, :], b2e[0:1, ds(e * D, D)], start=False, stop=True).then_inc(sem("ex_y"), 1)

            run(pe, EX // 2, body)

        def experts_scalar(act):
            act.wait_ge(sem("b1T_sb"), 1)

            def body(i, first):
                for s in range(2):
                    e = 2 * i + s
                    act.activation(b1s[s][:, :], b1T[:, ds(8 * e, 8)], ACT.Copy)
                    act.wait_ge(sem("ex_xt"), 2 * e + 1)
                    if s or not first:
                        act.wait_ge(sem("ex_h"), 8 * e)
                    act.activation(XET[:, 0, :], PS[0][:, :], ACT.Copy).then_inc(sem("ex_xts"), 1)
                    act.drain()
                    for f in range(8):
                        act.wait_ge(sem("ex_h"), 8 * e + f + 1)
                        if f == 0 and (s or not first):
                            act.wait_ge(sem("ex_y"), 4 * e)
                        act.activation(HM[:, f, :], PS[2 + f % 2][:, :], ACT.Relu, bias=b1s[s][:, f:f + 1]).then_inc(sem("ex_hs"), 1)

            run(act, EX // 2, body)

        def experts_vector(ve):
            def body(i, first):
                for s in range(2):
                    e = 2 * i + s
                    ve.wait_ge(sem("ex_xt"), 2 * e + 2)
                    if s or not first:
                        ve.wait_ge(sem("ex_h"), 8 * e)
                    ve.tensor_copy(XET[:, 1, :], PS[1][:, :]).then_inc(sem("ex_xts2"), 1)
                    if s or not first:
                        ve.wait_ge(sem("ex_out"), 16 * e)
                    for t in range(4):
                        ve.wait_ge(sem("ex_y"), 4 * e + t + 1)
                        ve.tensor_copy(YB[:, t, :], PS[4 + t][:, 0:D]).then_inc(sem("ex_ys"), 1)

            run(ve, EX // 2, body)

        YG = BIGR[:, 0:NT * D].rearrange("p (t d) -> p t d", d=D)
        NG = ar(0, NT * D, dt=I32)
        TENK = ar(NT * D, 2)

        def expert_rows_pool(pool):
            pool.wait_ge(sem("ex_out"), 16 * EX)
            for t in range(NT):
                pool.indirect_dma_start(YG[:, t, :], None, moe_out,
                                        bass.IndirectOffsetOnAxis(ap=rowof_m[:, t:t + 1].bitcast(U32), axis=0)
                                        ).then_inc(sem("moe_rows"), 16)

        def expert_rows_vector(ve):
            ve.wait_ge(sem("ex_out"), 16 * EX)
            ve.memset(TENK[:, 0:1], 10000.0)
            ve.memset(TENK[:, 1:2], -10000.0)
            ve.wait_ge(sem("moe_rows"), 16 * NT)
            for t in range(NT):
                ve.tensor_scalar(YG[:, t, :], YG[:, t, :], gate_p[:, t:t + 1], None, ALU.mult)
            ve.drain()
            y = BIGR[:, 0:NT * D]
            for q, (op, lim) in enumerate(((ALU.is_gt, 3.4028234663852886e38), (ALU.is_lt, -3.4028234663852886e38))):
                ve.tensor_scalar(NG, y, lim, None, op)
                ve.drain()
                ve.copy_predicated(y, NG, TENK[:, q:q + 1].to_broadcast([P, NT * D]))
                ve.drain()
            ve.tensor_tensor(NG, y, y, ALU.not_equal)
            ve.drain()
            ve.copy_predicated(y, NG, valid[:, 25:26].to_broadcast([P, NT * D]))
            ve.drain()
            for t in range(25):
                ins = ve.tensor_tensor(X[:, t, :], X[:, t, :], YG[:, t, :], ALU.add)
            ins.then_inc(sem("x2"), 1)
            ve.drain()


        NTY = ar(6000, NT, dt=I32)
        NTF = ar(6040, NT)
        OHt, TOTt, INCt, EXCt = (ar(6100 + 500 * k, NT, T1) for k in range(4))
        TB = ar(8200, 8, T1)
        TBI = ar(8400, T1, dt=I32)
        TCM = ar(8500, TT, T1)
        TR = ar(9400, 3, NT)
        TTF = ar(9500, TT)

        def types_sync(sp):
            sp.wait_ge(sem("types_pad"), 1)
            nt = A["node_type_19"]
            sp.dma_start(NTY[:, 0:24], nt[0:24 * P].rearrange("(t p) -> p t", p=P)).then_inc(sem("types_in"), 16)
            sp.dma_start(NTY[0:TAIL, 24:25], nt[24 * P:N].rearrange("(p t) -> p t", t=1)).then_inc(sem("types_in"), 16)

        def types_vector(ve):
            t_row = iotaz[:, 0:T1]
            ve.memset(NTY[:, 24:26], 0).then_inc(sem("types_pad"), 1)
            ve.wait_ge(sem("types_in"), 32)
            ve.tensor_copy(NTF, NTY)
            ve.drain()
            ve.tensor_tensor(OHt, t_row.unsqueeze(1).to_broadcast([P, NT, T1]), NTF.unsqueeze(2).to_broadcast([P, NT, T1]), ALU.is_equal)
            ve.drain()
            ve.tensor_tensor(OHt, OHt, valid[:, :].unsqueeze(2).to_broadcast([P, NT, T1]), ALU.mult).then_inc(sem("oh_t"), 1)
            place_vector(ve, "t", OHt, T1, TOTt, INCt, EXCt)
            ve.tensor_scalar(TBI, INCt[:, NT - 1, :], 127.0, None, ALU.add)
            ve.drain()
            ve.tensor_scalar(TBI, TBI, 7, None, ALU.arith_shift_right)
            ve.drain()
            ve.tensor_copy(TB[:, 0, :], TBI)
            ve.drain()
            ve.tensor_tensor_scan(TB[:, 1, :], ones[:, 0:T1], TB[:, 0, :], 0.0, ALU.mult, ALU.add)
            ve.drain()
            ve.tensor_tensor(TB[:, 2, :], TB[:, 1, :], TB[:, 0, :], ALU.subtract)
            ve.drain()
            ve.tensor_scalar(TB[:, 2, :], TB[:, 2, :], 128.0, None, ALU.mult)
            ve.drain()
            ve.tensor_tensor(EXCt, EXCt, TB[:, 2, :].unsqueeze(1).to_broadcast([P, NT, T1]), ALU.add)
            ve.drain()
            ve.tensor_tensor(EXCt, EXCt, OHt, ALU.mult)
            ve.drain()
            ve.tensor_reduce(TR[:, 0, :], EXCt, AX.X, ALU.add)
            ve.tensor_scalar(TR[:, 1, :], valid[:, :], -FAR, FAR, ALU.mult, ALU.add)
            ve.drain()
            ve.tensor_tensor(TR[:, 1, :], TR[:, 1, :], TR[:, 0, :], ALU.add)
            ve.tensor_copy(rowof_t[:, :], TR[:, 0, :])
            ve.tensor_tensor(TCM[0:1], TB[0:1, 1, :].unsqueeze(1).to_broadcast([1, TT, T1]),
                             iotaz[0:1, 0:TT].unsqueeze(2).to_broadcast([1, TT, T1]), ALU.is_le)
            ve.drain()
            ve.tensor_copy(slot_t[:, :], TR[:, 1, :])
            ve.tensor_reduce(TTF[0:1], TCM[0:1], AX.X, ALU.add)
            ve.drain()
            ve.tensor_scalar(ttype[:, :], TTF[0:1], float(T1 - 1), None, ALU.min
                             ).then_inc(sem("slot_t"), 1)
            ve.drain()

        def types_pool(pool):
            pool.wait_ge(sem("slot_t"), 1)
            pool.wait_ge(sem("xn"), 3 * NT)
            for t in range(25):
                pool.indirect_dma_start(typ_x, bass.IndirectOffsetOnAxis(ap=slot_t[:, t:t + 1].bitcast(U32), axis=0),
                                        XN[:, t, :], None, bounds_check=TT * P - 1, oob_is_err=False
                                        ).then_inc(sem("typ_x"), 16)

        NTY2 = TT // 2
        TW = [ar(1152 * s, 2, 3 * PROJ) for s in range(2)]
        TBR = [ar(2304 + 576 * s, 3 * PROJ) for s in range(2)]
        TX = [ar(3456 + 256 * s, D) for s in range(2)]
        TXT = [ar(3968 + 256 * s, 2, P) for s in range(2)]
        TROW = [ar(4480 + 440 * s, KV + DK) for s in range(2)]

        def kvq_sync(sp):
            sp.wait_ge(sem("typ_x"), 16 * 25)
            sp.wait_ge(sem("x2"), 1)
            ws = [A["L1_gnn_W" + c].rearrange("t (k p) n -> p (t k) n", p=P) for c in "kvq"]
            bs = [A["L1_gnn_b" + c] for c in "kvq"]
            xin = typ_x.rearrange("(b p) d -> b p d", p=P)

            def body(i, first):
                for s in range(2):
                    it = 2 * i + s
                    ty = loads_of(sp, ttype[0:1, ds(it, 1)], T1 - 1, ET.SP)[0]
                    if not first:
                        sp.wait_ge(sem("kvq_mm"), 2 * i + s - 1)
                        sp.nop(nofuse=True)
                    for c in range(3):
                        sp.dma_start(TW[s][:, :, c * PROJ:(c + 1) * PROJ], ws[c][:, ds(ty * 2, 2), :]).then_inc(sem(f"kvq_in{s}"), 16)
                        sp.dma_start(TBR[s][0:1, c * PROJ:(c + 1) * PROJ], bs[c][ds(ty, 1), :]).then_inc(sem(f"kvq_in{s}"), 16)
                    sp.dma_start(TX[s], xin[ds(it, 1), :, :].rearrange("b p d -> (b p) d")).then_inc(sem(f"kvq_in{s}"), 16)

            run(sp, NTY2, body)

        def kvq_tensor(pe):
            def body(i, first):
                for s in range(2):
                    pe.wait_ge(sem(f"kvq_in{s}"), 112 * (i + 1))
                    if not first:
                        pe.wait_ge(sem("kvq_xt"), 2 * i + s - 1)
                    for k in range(2):
                        ins = pe.transpose(PS[s][:, k * P:(k + 1) * P], TX[s][:, k * P:(k + 1) * P], ident[:, :])
                    ins.then_inc(sem("kvq_tp"), 1)
                for s in range(2):
                    pe.wait_ge(sem("kvq_xt"), 2 * i + s + 1)
                    if not first:
                        pe.wait_ge(sem("kvq_row"), 2 * (2 * i + s - 1))
                    kv, q = PS[2 + s][:, 0:KV], PS[4 + s]
                    for k in range(2):
                        pe.matmul(kv, TXT[s][:, k, :], TW[s][:, k, 0:KV], start=(k == 0), stop=False)
                    pe.matmul(kv, ones[0:1, :], TBR[s][0:1, 0:KV], start=False, stop=True)
                    for h in range(4):
                        wd = DK if h < 3 else PROJ - 3 * DK
                        c0 = KV + h * DK
                        for k in range(2):
                            pe.matmul(q[:, 0:wd], TXT[s][:, k, :], TW[s][:, k, c0:c0 + wd], start=(h == 0 and k == 0), stop=False,
                                      skip_group_check=True)
                        ins = pe.matmul(q[:, 0:wd], ones[0:1, :], TBR[s][0:1, c0:c0 + wd], start=False, stop=(h == 3),
                                        skip_group_check=True)
                    ins.then_inc(sem("kvq_mm"), 1)

            run(pe, NTY2, body)

        def kvq_scalar(act):
            rows = typ_kvq.rearrange("(b p) d -> b p d", p=P)

            def body(i, first):
                for s in range(2):
                    act.wait_ge(sem("kvq_tp"), 2 * i + s + 1)
                    if not first:
                        act.wait_ge(sem("kvq_mm"), 2 * i + s - 1)
                    act.activation(TXT[s].rearrange("p k n -> p (k n)"), PS[s][:, 0:D], ACT.Copy).then_inc(sem("kvq_xt"), 1)
                for s in range(2):
                    it = 2 * i + s
                    act.wait_ge(sem("kvq_mm"), 2 * i + s + 1)
                    if not first:
                        act.wait_ge(sem(f"kvq_out{s}"), 16 * i)
                    act.activation(TROW[s][:, 0:KV], PS[2 + s][:, 0:KV], ACT.Copy).then_inc(sem("kvq_row"), 1)
                    act.activation(TROW[s][:, KV:], PS[4 + s][:, 0:DK], ACT.Copy).then_inc(sem("kvq_row"), 1)
                    act.wait_ge(sem("kvq_row"), 2 * (2 * i + s + 1))
                    act.dma_start(rows[ds(it, 1), :, :].rearrange("b p d -> (b p) d"), TROW[s]).then_inc(sem(f"kvq_out{s}"), 16)

            run(act, NTY2, body)

        KVG = BIGR[:, 0:NT * (KV + DK)].rearrange("p (t d) -> p t d", d=KV + DK)

        def kvq_rows_pool(pool):
            for s in range(2):
                pool.wait_ge(sem(f"kvq_out{s}"), 16 * NTY2)
            for t in range(NT):
                pool.indirect_dma_start(KVG[:, t, :], None, typ_kvq,
                                        bass.IndirectOffsetOnAxis(ap=rowof_t[:, t:t + 1].bitcast(U32), axis=0)
                                        ).then_inc(sem("kvg"), 16)

        def kvq_rows_sync(sp):
            sp.wait_ge(sem("kvg"), 16 * NT)
            sp.dma_start(kv_tab.rearrange("(t p) d -> p t d", p=P), KVG[:, :, 0:KV]).then_inc(sem("kv_tab"), 16)

        def kvq_rows_vector(ve):
            ve.wait_ge(sem("kvg"), 16 * NT)
            ve.tensor_copy(QS[:, :, :], KVG[:, :, KV:])
            ve.drain()

        KVR = [ar(1792 * s, U, ROW) for s in range(2)]
        EQB = [ar(3584 + 128 * s, U, TD) for s in range(2)]
        OH = [ar(3840 + 512 * s, U, P) for s in range(2)]
        OT = [ar(4864 + 512 * s, U, P) for s in range(2)]
        NEG = [ar(5888 + 256 * s, U, P, dt=BF16) for s in range(2)]
        PRD = [ar(6400 + 896 * s, U, H1 * DK) for s in range(2)]
        ATS = [ar(8192 + 16 * s, U * H1) for s in range(2)]
        BM = [ar(8224 + 16 * s, U * H1) for s in range(2)]
        ATT = ar(8300, NB, H1)
        VB = [ar(10000 + 1040 * s, U, SROW) for s in range(2)]
        ARG = [ar(12100 + 16 * s, U * H1) for s in range(2)]
        RCP = ar(12200, NT, H1)

        def score_sync(sp, o):
            rec = rec_tab[o].rearrange("(b p) c -> p b c", p=P)
            vt = v_tab[o].rearrange("(b p) c -> p b c", p=P)

            def body(i, first):
                j = o * NIT + i
                for s in range(2):
                    b = (2 * i + s) * U
                    if not first:
                        sp.wait_ge(sem("prod"), 2 * j + s - 1)
                        sp.nop(nofuse=True)
                        sp.wait_ge(sem(f"v_out{s}"), 16 * j)
                        sp.nop(nofuse=True)
                    sp.dma_start(KVR[s][:, :, KV:ROW], rec[:, ds(b, U), 0:2 * TD]).then_inc(sem(f"rec{s}"), 16)
                    sp.dma_start(EQB[s], rec[:, ds(b, U), R_EQ:R_EQ + TD]).then_inc(sem(f"rec{s}"), 16)
                for s in range(2):
                    b = (2 * i + s) * U
                    sp.wait_ge(sem(f"rec{s}"), 32 * (j + 1))
                    sp.nop(nofuse=True)
                    sp.wait_ge(sem(f"rows{s}"), 64 * (j + 1))
                    sp.nop(nofuse=True)
                    sp.dma_start(vt[:, ds(b, U), :], KVR[s][:, :, PROJ:ROW]).then_inc(sem(f"v_out{s}"), 16)

            run(sp, NIT, body)

        def score_pool(pool, o):
            pool.wait_ge(sem("kv_tab"), 16)
            if o:
                pool.wait_ge(sem("prod"), 2 * NIT)
                for s in range(2):
                    pool.wait_ge(sem(f"v_out{s}"), 16 * NIT)

            def body(i, first):
                j = o * NIT + i
                for s in range(2):
                    b = (2 * i + s) * U
                    if not first:
                        pool.wait_ge(sem("prod"), 2 * j + s - 1)
                        pool.wait_ge(sem(f"v_out{s}"), 16 * j)
                    pool.tensor_copy(IST[s][:, :], META[o][:, ds(b, U), 0].bitcast(I32)).then_inc(sem("ist"), 1)
                    pool.wait_ge(sem("ist"), 2 * NIT + 2 * j + s + 1)
                    pool.nop(nofuse=True)
                    for u in range(U):
                        pool.indirect_dma_start(KVR[s][:, u, 0:KV], None, kv_tab,
                                                bass.IndirectOffsetOnAxis(ap=IST[s][:, u:u + 1].bitcast(U32), axis=0)
                                                ).then_inc(sem(f"rows{s}"), 16)

            run(pool, NIT, body)

        def onehots(ve, o, b, s, free, n, done):
            if free is not None:
                ve.wait_ge(sem(free), n)
            ve.tensor_copy(MST[s][:, :, :], META[o][:, ds(b, U), :])
            ve.drain()
            for u in range(U):
                ins = ve.tensor_scalar(OH[s][:, u, :], iota1[:, :], MST[s][:, u, 1:2], None, ALU.is_equal)
            ins.then_inc(sem(done), 1)

        def score_vector(ve, o):
            ve.wait_ge(sem("kv_tab"), 16)
            ve.memset(BIGR[:, 0:NT * SROW], 0.0)
            ve.memset(M[:, :, :], -1.0e30)
            ve.drain()

            def body(i, first):
                j = o * NIT + i
                for s in range(2):
                    onehots(ve, o, (2 * i + s) * U, s, None if first else "ohT", 2 * j + s - 1, "oh")
                for s in range(2):
                    b = (2 * i + s) * U
                    ve.wait_ge(sem("q"), 2 * j + s + 1)
                    ve.wait_ge(sem(f"rows{s}"), 64 * (j + 1))
                    ve.wait_ge(sem(f"rec{s}"), 32 * (j + 1))
                    q = PS[2 + s][:, 0:U * 64].rearrange("p (u c) -> p u c", c=64)
                    for h in range(3):
                        ve.tensor_tensor(PRD[s][:, :, h * DK:(h + 1) * DK], KVR[s][:, :, h * DK:(h + 1) * DK], q[:, :, 0:DK], ALU.mult)
                    ve.tensor_tensor(PRD[s][:, :, 3 * DK:PROJ], KVR[s][:, :, 3 * DK:PROJ], q[:, :, 0:PROJ - 3 * DK], ALU.mult)
                    ve.tensor_tensor(PRD[s][:, :, PROJ:], KVR[s][:, :, KV:KV + TD], q[:, :, DK - TD:DK], ALU.mult).then_inc(sem("prod"), 1)
                    ve.drain()
                    if not first:
                        ve.wait_ge(sem("bm"), 4 * (2 * j + s - 1))
                    ve.tensor_reduce(ATS[s], PRD[s].rearrange("p u (h d) -> p (u h) d", d=DK), AX.X, ALU.add).then_inc(sem("att"), 1)
                    ve.drain()
                    ve.tensor_copy(ATT[:, ds(b, U), :].rearrange("p u h -> p (u h)"), ATS[s])
                for s in range(2):
                    b = (2 * i + s) * U
                    ws = loads_of(ve, win[o][0:1, ds(b, U)], W - 1, ET.DVE)
                    for u in range(U):
                        ve.wait_ge(sem("bm"), 4 * (2 * j + s) + u + 1)
                        ve.tensor_reduce(BM[s][:, u * H1:(u + 1) * H1], PS[4 + u][:, :].rearrange("p (h e) -> p h e", e=P),
                                         AX.X, ALU.max).then_inc(sem("bmr"), 1)
                    for u in range(U):
                        ve.drain()
                        m = M[:, ds(ws[u], 1), :].rearrange("p t h -> p (t h)")
                        ve.tensor_tensor(m, m, BM[s][:, u * H1:(u + 1) * H1], ALU.max)

            run(ve, NIT, body)
            ve.drain()
            ve.tensor_copy(RCP[:, 0, :], iotaz[:, 0:H1]).then_inc(sem("max"), 1)

        def transposes(pe, o, s, wait, n, done):
            pe.wait_ge(sem(wait), n)
            for u in range(U):
                ins = pe.transpose(PS[s][:, u * P:(u + 1) * P], OH[s][:, u, :], ident[:, :])
            ins.then_inc(sem(done), 1)

        def score_tensor(pe, o):
            def body(i, first):
                j = o * NIT + i
                for s in range(2):
                    if not first:
                        pe.wait_ge(sem("ot"), 2 * (2 * j + s - 1))
                    transposes(pe, o, s, "oh", 2 * j + s + 1, "ohT")
                for s in range(2):
                    b = (2 * i + s) * U
                    ws = loads_of(pe, win[o][0:1, ds(b, U)], W - 1, ET.PE)
                    pe.wait_ge(sem("ot"), 2 * (2 * j + s + 1))
                    pe.wait_ge(sem(f"rec{s}"), 32 * (j + 1))
                    if not first:
                        pe.wait_ge(sem("prod"), 2 * j + s - 1)
                    for u in range(U):
                        q = PS[2 + s][:, u * 64:u * 64 + DK]
                        pe.matmul(q, OT[s][:, u, :], QS[:, ds(ws[u], 1), :].rearrange("p t d -> p (t d)"), start=True, stop=False,
                                  skip_group_check=True)
                        ins = pe.matmul(PS[2 + s][:, u * 64 + DK - TD:u * 64 + DK], ident[:, :], EQB[s][:, u, :], start=False, stop=True,
                                        skip_group_check=True)
                    ins.then_inc(sem("q"), 1)
                for s in range(2):
                    pe.wait_ge(sem("att"), 2 * j + s + 1)
                    for u in range(U):
                        if s or not first:
                            pe.wait_ge(sem("bmr"), 8 * j + 4 * s + u - 3)
                        pe.matmul(PS[4 + u][:, :], identb[:, :], NEG[s][:, u, :].unsqueeze(1).to_broadcast([P, H1, P]),
                                  start=True, stop=False, skip_group_check=True)
                        for h in range(H1):
                            ins = pe.matmul(PS[4 + u][:, h * P:(h + 1) * P], ATS[s][:, u * H1 + h:u * H1 + h + 1].to_broadcast([P, P]),
                                            ident[:, :], start=False, stop=(h == 3), skip_group_check=True)
                        ins.then_inc(sem("bm"), 1)

            run(pe, NIT, body)

        def score_scalar(act, o):
            def body(i, first):
                j = o * NIT + i
                for s in range(2):
                    act.wait_ge(sem("ohT"), 2 * j + s + 1)
                    if not first:
                        act.wait_ge(sem("q"), 2 * j + s - 1)
                        act.wait_ge(sem("bm"), 4 * (2 * j + s - 1))
                    act.activation(OT[s].rearrange("p u n -> p (u n)"), PS[s][:, :], ACT.Copy).then_inc(sem("ot"), 1)
                    act.activation(NEG[s].rearrange("p u n -> p (u n)"), PS[s][:, :], ACT.Copy, scale=BIG, bias=-BIG).then_inc(sem("ot"), 1)

            run(act, NIT, body)

        def sum_sync(sp, o):
            for s in range(2):
                sp.wait_ge(sem(f"v_out{s}"), 16 * NIT * (o + 1))
            vt = v_tab[o].rearrange("(b p) c -> p b c", p=P)

            def body(i, first):
                j = o * NIT + i
                for s in range(2):
                    b = (2 * i + s) * U
                    if not first:
                        sp.wait_ge(sem("sum"), 2 * j + s - 1)
                        sp.nop(nofuse=True)
                    sp.dma_start(VB[s][:, :, 0:VROW], vt[:, ds(b, U), :]).then_inc(sem(f"vb{s}"), 16)

            run(sp, NIT, body)

        def sum_vector(ve, o):
            def body(i, first):
                j = o * NIT + i
                for s in range(2):
                    onehots(ve, o, (2 * i + s) * U, s, None if first else "sum", 2 * j + s - 1, "oh2")
                for s in range(2):
                    b = (2 * i + s) * U
                    ve.wait_ge(sem("m"), 2 * j + s + 1)
                    if not first:
                        ve.wait_ge(sem("exp"), 2 * j + s - 1)
                    ve.tensor_tensor(ARG[s], ATT[:, ds(b, U), :].rearrange("p u h -> p (u h)"), PS[2 + s][:, 0:U * H1],
                                     ALU.subtract).then_inc(sem("arg"), 1)
                for s in range(2):
                    ve.wait_ge(sem(f"vb{s}"), 16 * (j + 1))
                    ve.wait_ge(sem("exp"), 2 * j + s + 1)
                    for u in range(U):
                        v = VB[s][:, u, 0:H1 * DK].rearrange("p (h d) -> p h d", d=DK)
                        ins = ve.tensor_tensor(v, v, VB[s][:, u, D:SROW].unsqueeze(2).to_broadcast([P, H1, DK]), ALU.mult)
                    ins.then_inc(sem("pv"), 1)
                for s in range(2):
                    b = (2 * i + s) * U
                    ws = loads_of(ve, win[o][0:1, ds(b, U)], W - 1, ET.DVE)
                    for u in range(U):
                        if u == 0:
                            ve.wait_ge(sem("sum"), 2 * j + s + 1)
                        a = ACC[:, ds(ws[u], 1), :].rearrange("p t d -> p (t d)")
                        ve.tensor_tensor(a, a, PS[4 + u][:, 0:SROW], ALU.add).then_inc(sem("add"), 1)
                        ve.drain()

            run(ve, NIT, body)
            ve.tensor_scalar(RCP, ACC[:, :, D:SROW], 1.0e-16, None, ALU.add)
            ve.drain()
            ve.reciprocal(RCP, RCP)
            ve.drain()
            for h in range(H1):
                a = ACC[:, :, h * DK:(h + 1) * DK]
                ve.tensor_tensor(a, a, RCP[:, :, h].unsqueeze(2).to_broadcast([P, NT, DK]), ALU.mult)
            ve.drain()
            if o == 0:
                ve.tensor_copy(AGG, ACC[:, :, 0:D])
            else:
                ve.tensor_tensor(AGG, AGG, ACC[:, :, 0:D], ALU.add).then_inc(sem("agg"), 1)
            ve.drain()

        def sum_tensor(pe, o):
            pe.wait_ge(sem("max"), o + 1)

            def body(i, first):
                j = o * NIT + i
                for s in range(2):
                    if not first:
                        pe.wait_ge(sem("ot2"), 2 * j + s - 1)
                    transposes(pe, o, s, "oh2", 2 * j + s + 1, "oh2T")
                for s in range(2):
                    b = (2 * i + s) * U
                    ws = loads_of(pe, win[o][0:1, ds(b, U)], W - 1, ET.PE)
                    pe.wait_ge(sem("ot2"), 2 * j + s + 1)
                    if not first:
                        pe.wait_ge(sem("arg"), 2 * j + s - 1)
                    for u in range(U):
                        ins = pe.matmul(PS[2 + s][:, u * H1:(u + 1) * H1], OT[s][:, u, :],
                                        M[:, ds(ws[u], 1), :].rearrange("p t h -> p (t h)"), start=True, stop=True,
                                        skip_group_check=True)
                    ins.then_inc(sem("m"), 1)
                for s in range(2):
                    pe.wait_ge(sem("pv"), 2 * j + s + 1)
                    for u in range(U):
                        if s or not first:
                            pe.wait_ge(sem("add"), 8 * j + 4 * s + u - 3)
                        ins = pe.matmul(PS[4 + u][:, 0:SROW], OH[s][:, u, :], VB[s][:, u, :], start=True, stop=True)
                    ins.then_inc(sem("sum"), 1)

            run(pe, NIT, body)

        def sum_scalar(act, o):
            def body(i, first):
                j = o * NIT + i
                for s in range(2):
                    act.wait_ge(sem("oh2T"), 2 * j + s + 1)
                    if not first:
                        act.wait_ge(sem("m"), 2 * j + s - 1)
                    act.activation(OT[s].rearrange("p u n -> p (u n)"), PS[s][:, :], ACT.Copy).then_inc(sem("ot2"), 1)
                for s in range(2):
                    act.wait_ge(sem("arg"), 2 * j + s + 1)
                    if not first:
                        act.wait_ge(sem("sum"), 2 * j + s - 1)
                    act.activation(VB[s][:, :, D:SROW], ARG[s].rearrange("p (u h) -> p u h", h=H1), ACT.Exp,
                                   scale=float(DK) ** -0.5).then_inc(sem("exp"), 1)

            run(act, NIT, body)


        WA = [ar(1024 * s, 4, D) for s in range(2)]
        WS = [ar(2048 + 512 * s, 2, D) for s in range(2)]
        AX2 = [ar(3072 + 512 * s, 2, D) for s in range(2)]
        AT2 = [ar(4096 + 256 * s, 2, P) for s in range(2)]
        ROWS3 = [ar(4608 + 768 * s, 3 * D) for s in range(2)]
        YT = [ar(6144 + 256 * s, D) for s in range(2)]
        YST = [sb(f"yst{s}", [P, 6]) for s in range(2)]
        YMV = [sb(f"ymv{s}", [P, 2]) for s in range(2)]
        YRS = [sb(f"yrs{s}", [P, 4, 1]) for s in range(2)]

        def agg_pool(pool):
            pool.wait_ge(sem("agg"), 1)
            for t in range(25):
                pool.indirect_dma_start(typ_agg, bass.IndirectOffsetOnAxis(ap=slot_t[:, t:t + 1].bitcast(U32), axis=0),
                                        AGG[:, t, :], None, bounds_check=TT * P - 1, oob_is_err=False
                                        ).then_inc(sem("typ_agg"), 16)

        def proj_sync(sp):
            sp.wait_ge(sem("typ_agg"), 16 * 25)
            wa = A["L1_gnn_Wa"].rearrange("t (k p) n -> p (t k) n", p=P)
            ain = typ_agg.rearrange("(b p) d -> b p d", p=P)
            xin = typ_x.rearrange("(b p) d -> b p d", p=P)
            yout = typ_y.rearrange("(b p) d -> b p d", p=P)

            def body(i, first):
                for s in range(2):
                    it = 2 * i + s
                    ty = loads_of(sp, ttype[0:1, ds(it, 1)], T1 - 1, ET.SP)[0]
                    if not first:
                        sp.wait_ge(sem(f"pj_out{s}"), 16 * i)
                        sp.nop(nofuse=True)
                    sp.dma_start(WA[s], wa[:, ds(ty * 4, 4), :]).then_inc(sem(f"pj_in{s}"), 16)
                    for c, name in enumerate(("L1_gnn_ba", "L1_gnn_gamma", "L1_gnn_beta")):
                        sp.dma_start(ROWS3[s][0:1, c * D:(c + 1) * D], A[name][ds(ty, 1), :]).then_inc(sem(f"pj_in{s}"), 16)
                    for c, src in enumerate((ain, xin)):
                        sp.dma_start(AX2[s][:, c, :], src[ds(it, 1), :, :].rearrange("b p d -> (b p) d")).then_inc(sem(f"pj_in{s}"), 16)
                for s in range(2):
                    it = 2 * i + s
                    sp.wait_ge(sem("pj_y"), 2 * i + s + 1)
                    sp.nop(nofuse=True)
                    sp.dma_start(yout[ds(it, 1), :, :].rearrange("b p d -> (b p) d"), YT[s]).then_inc(sem(f"pj_out{s}"), 16)

            run(sp, NTY2, body)

        def proj_tensor(pe):
            def body(i, first):
                for s in range(2):
                    pe.wait_ge(sem(f"pj_in{s}"), 96 * (i + 1))
                    if not first:
                        pe.wait_ge(sem("pj_y"), 2 * i + s - 1)
                    for k in range(2):
                        ins = pe.transpose(PS[s][:, k * P:(k + 1) * P], AX2[s][:, 0, k * P:(k + 1) * P], ident[:, :])
                    ins.then_inc(sem("pj_t"), 1)
                    pe.matmul(PS[4 + s][:, :], ones[0:1, :], ROWS3[s][0:1, D:3 * D], start=True, stop=True).then_inc(sem("pj_gb"), 1)
                for s in range(2):
                    pe.wait_ge(sem("pj_ts"), 2 * i + s + 1)
                    pe.wait_ge(sem("pj_ws"), 2 * i + s + 1)
                    y = PS[2 + s][:, 0:D]
                    for k in range(2):
                        pe.matmul(y, AT2[s][:, k, :], WS[s][:, k, :], start=(k == 0), stop=False)
                    pe.matmul(y, ones[0:1, :], ROWS3[s][0:1, 0:D], start=False, stop=True).then_inc(sem("pj_mm"), 1)

            run(pe, NTY2, body)

        def proj_scalar(act):
            def body(i, first):
                for s in range(2):
                    act.wait_ge(sem("pj_t"), 2 * i + s + 1)
                    if not first:
                        act.wait_ge(sem("pj_mm"), 2 * i + s - 1)
                    act.activation(AT2[s].rearrange("p k n -> p (k n)"), PS[s][:, 0:D], ACT.Copy).then_inc(sem("pj_ts"), 1)
                for s in range(2):
                    act.wait_ge(sem("pj_v"), 2 * i + s + 1)
                    act.activation(YRS[s][:, 1, :], YRS[s][:, 0, :], ACT.Sqrt).then_inc(sem("pj_sd"), 1)

            run(act, NTY2, body)

        def proj_vector(ve):
            def body(i, first):
                for s in range(2):
                    ve.wait_ge(sem(f"pj_in{s}"), 96 * (i + 1))
                    if not first:
                        ve.wait_ge(sem("pj_mm"), 2 * i + s - 1)
                    ve.tensor_tensor(WS[s], WA[s][:, 0:2, :], WA[s][:, 2:4, :], ALU.add).then_inc(sem("pj_ws"), 1)
                for s in range(2):
                    ve.wait_ge(sem("pj_mm"), 2 * i + s + 1)
                    if not first:
                        ve.wait_ge(sem(f"pj_out{s}"), 16 * i)
                    ve.tensor_tensor(YT[s], PS[2 + s][:, 0:D], AX2[s][:, 1, :], ALU.add)
                    ve.drain()
                    ve.bn_stats(YST[s][:, :], YT[s])
                    ve.drain()
                    ve.bn_aggr(YMV[s][:, :], YST[s][:, :])
                    ve.drain()
                    ve.tensor_scalar(YRS[s][:, 0, :], YMV[s][:, 1:2], LN_EPS, None, ALU.add).then_inc(sem("pj_v"), 1)
                for s in range(2):
                    ve.wait_ge(sem("pj_sd"), 2 * i + s + 1)
                    newton(ve, YRS[s], slice(0, 1))
                    ve.tensor_scalar(YT[s], YT[s], YMV[s][:, 0:1], YRS[s][:, 3, :], ALU.subtract, ALU.mult)
                    ve.drain()
                    ve.wait_ge(sem("pj_gb"), 2 * i + s + 1)
                    ve.tensor_tensor(YT[s], YT[s], PS[4 + s][:, 0:D], ALU.mult)
                    ve.drain()
                    ve.tensor_tensor(YT[s], YT[s], PS[4 + s][:, D:2 * D], ALU.add).then_inc(sem("pj_y"), 1)

            run(ve, NTY2, body)
            ve.drain()

        def proj_rows_pool(pool):
            for s in range(2):
                pool.wait_ge(sem(f"pj_out{s}"), 16 * NTY2)
            pool.wait_ge(sem("typ_agg"), 16 * 25)
            for t in range(25):
                pool.indirect_dma_start(YG[:, t, :], None, typ_y,
                                        bass.IndirectOffsetOnAxis(ap=rowof_t[:, t:t + 1].bitcast(U32), axis=0)
                                        ).then_inc(sem("y_rows"), 16)

        def proj_rows_vector(ve):
            ve.wait_ge(sem("y_rows"), 16 * 25)
            for t in range(25):
                ins = ve.tensor_tensor(X[:, t, :], X[:, t, :], YG[:, t, :], ALU.add)
            ins.then_inc(sem("x3"), 1)
            ve.drain()

        HP = H2 // 2
        SWT = BIGR[:, 0:HP * NT * P].rearrange("p (t h n) -> p t h n", h=HP, n=P)
        WFX = ar(0, 2, H2 * G)
        WL = ar(1024, 2, H2 * G)
        WXT = ar(2048, HP, D)
        WOUT = ar(3072, HP, D)
        WX = ar(4096, 2, H2 * G)
        BDS = ar(5120, 4, P)
        BDM = ar(5632, P)
        RBF = ar(5760, H2 * G)
        RBL = ar(6272, H2 * G)
        RBS = ar(6784, P)
        RBO = ar(6912, D)
        BXC = ar(7168, HP)
        TMP = ar(7172, 2, H2)
        FX = [ar(7200 + 520 * s, H2, G + 1) for s in range(2)]
        SW = [ar(8240 + 512 * s, H2, G) for s in range(2)]
        XT4 = [ar(9264 + 256 * s, 2, P) for s in range(2)]
        SM = [ar(9776 + 24 * s, 3, H2) for s in range(2)]
        TOK = ar(9830, P)
        TOKT, QT, KT, VV, PP, PPT, OTT = (ar(9960 + 128 * k, P) for k in range(7))
        SA = ar(10860, 8)
        MO = ar(10880, HP, D)
        ZC = ar(11910, P + 2)
        OB = [ar(12050 + 256 * s, D) for s in range(2)]
        b1row = ar(12600, 1)

        def slice_sync(sp):
            sp.wait_ge(sem("x3"), 1)
            sp.wait_ge(sem("bd_zero"), 1)

            def ld(dst, src):
                sp.dma_start(dst, src).then_inc(sem("sl_in"), 16)

            ld(WFX, A["L1_ffn_W_fx"].rearrange("(k p) n -> p k n", p=P))
            ld(WX, A["L1_ffn_W_x"].rearrange("(k p) n -> p k n", p=P))
            ld(WOUT, A["L1_ffn_W_out"].rearrange("(k p) n -> p k n", p=P))
            for c, name in enumerate(("slice", "q", "k", "v")):
                for h in range(2):
                    ld(BDS[h * G:(h + 1) * G, c, h * G:(h + 1) * G], A["L1_ffn_W_" + name])
            ld(RBF[0:1, :], A["L1_ffn_b_fx"].rearrange("(a n) -> a n", a=1))
            ld(RBO[0:1, :], A["L1_ffn_b_out"].rearrange("(a n) -> a n", a=1))
            for h in range(2):
                ld(RBS[0:1, h * G:(h + 1) * G], A["L1_ffn_b_slice"].rearrange("(a n) -> a n", a=1))
            ld(BXC, A["L1_ffn_b_x"].rearrange("(k p) -> p k", p=P))
            ld(TMP[:, 0, :], A["L1_ffn_temperature"].rearrange("a h b c -> (a b c) h").to_broadcast([P, H2]))

        N_SL = 16 * 17

        def slice_prep_vector(ve):
            ve.memset(BDS, 0.0)
            ve.memset(BDM, 0.0)
            ve.memset(ZC, 0.0)
            for s in range(2):
                ve.memset(FX[s], 1.0)
            ve.drain()
            ve.memset(BDM[0:G, 0:G], 1.0)
            ve.memset(BDM[G:P, G:P], 1.0).then_inc(sem("bd_zero"), 1)
            ve.wait_ge(sem("sl_in"), N_SL)
            ve.tensor_scalar(TMP[:, 1, :], TMP[:, 0, :], 0.1, 5.0, ALU.max, ALU.min)
            ve.drain()
            ve.reciprocal(TMP[:, 1, :], TMP[:, 1, :])
            ve.drain()
            tmp = TMP[:, 1, :].unsqueeze(2).to_broadcast([P, H2, G])
            ve.wait_ge(sem("wxt_ps"), 1)
            for k in range(2):
                ve.tensor_copy(WXT[:, :, k * P:(k + 1) * P], PS[k][:, :].rearrange("p (h n) -> p h n", n=P))
            ve.drain()
            ve.tensor_scalar(WXT[0:1, 0, 0:1], WXT[0:1, 0, 0:1], 1.0, None, ALU.mult).then_inc(sem("wxt"), 1)
            ve.wait_ge(sem("wl_ps"), 1)
            for k in range(2):
                ve.tensor_tensor(WL[:, k, :].rearrange("p (h g) -> p h g", g=G), PS[2 + k][:, :].rearrange("p (h g) -> p h g", g=G), tmp, ALU.mult)
            ve.tensor_tensor(RBL[0:1, :].rearrange("p (h g) -> p h g", g=G), PS[4][0:1, :].rearrange("p (h g) -> p h g", g=G),
                             tmp[0:1], ALU.mult).then_inc(sem("wl"), 1)
            ve.drain()

        def slice_prep_tensor(pe):
            pe.wait_ge(sem("sl_in"), N_SL)
            pe.wait_ge(sem("bd_zero"), 1)
            for k in range(2):
                for h in range(HP):
                    ins = pe.transpose(PS[k][:, h * P:(h + 1) * P], WX[:, k, h * P:(h + 1) * P], ident[:, :])
            ins.then_inc(sem("wxt_ps"), 1)
            pe.wait_ge(sem("wxt"), 1)
            for k in range(2):
                for h in range(HP):
                    pe.matmul(PS[2 + k][:, h * P:(h + 1) * P], WXT[:, h, k * P:(k + 1) * P], BDS[:, 0, :], start=True, stop=True)
            for h in range(HP):
                pe.matmul(PS[4][0:1, h * P:(h + 1) * P], BXC[:, h:h + 1], BDS[:, 0, :], start=True, stop=False, skip_group_check=True)
                ins = pe.matmul(PS[4][0:1, h * P:(h + 1) * P], ones[0:1, 0:1], RBS[0:1, :], start=False, stop=True, skip_group_check=True)
            ins.then_inc(sem("wl_ps"), 1)
            pe.wait_ge(sem("wl"), 1)
            for h in range(HP):
                pe.matmul(tok_ps(h), ZC[:, 0:P], ZC[:, 0:2 * (G + 1)], start=True, stop=False, skip_group_check=True)

        def tok_ps(h):
            return PS[6 + h // 2][:, (h % 2) * 256:(h % 2) * 256 + 2 * (G + 1)]

        def slices_tensor(pe):
            for t in range(NT):
                s = t % 2
                pe.wait_ge(sem("xn"), 3 * NT + t + 1)
                if t >= 1:
                    pe.wait_ge(sem("x4ts"), t)
                for k in range(2):
                    ins = pe.transpose(PS[0][:, k * P:(k + 1) * P], XN[:, t, k * P:(k + 1) * P], ident[:, :])
                ins.then_inc(sem("x4t"), 1)
                pe.wait_ge(sem("x4ts"), t + 1)
                if t >= 2:
                    pe.wait_ge(sem("fxs"), t - 1)
                    pe.wait_ge(sem("lgs"), t - 1)
                for c, (w, b) in enumerate(((WFX, RBF), (WL, RBL))):
                    o_ = PS[2 + c + 2 * s][:, :]
                    for k in range(2):
                        pe.matmul(o_, XT4[s][:, k, :], w[:, k, :], start=(k == 0), stop=False)
                    pe.matmul(o_, ones[0:1, :], b[0:1, :], start=False, stop=True).then_inc(sem("fxl"), 1)
                if t >= 1:
                    slice_tail(pe, t - 1)
            slice_tail(pe, NT - 1)

        def slice_tail(pe, t):
            s = t % 2
            pe.wait_ge(sem("sw"), t + 1)
            pe.wait_ge(sem("fxs"), t + 1)
            if t >= 1:
                pe.wait_ge(sem("sw_t2"), t)
            for h in range(HP):
                pe.transpose(PS[1][:, h * P:(h + 1) * P], SW[s][:, 2 * h:2 * h + 2, :].rearrange("p h g -> p (h g)"), ident[:, :])
                ins = pe.matmul(tok_ps(h), SW[s][:, 2 * h:2 * h + 2, :].rearrange("p h g -> p (h g)"),
                                FX[s][:, 2 * h:2 * h + 2, :].rearrange("p h g -> p (h g)"), start=False, stop=(t == NT - 1),
                                skip_group_check=True)
            ins.then_inc(sem("sl_mm"), 1)

        def slices_scalar(act):
            for t in range(NT):
                s = t % 2
                act.wait_ge(sem("x4t"), t + 1)
                if t >= 2:
                    act.wait_ge(sem("fxl"), 2 * (t - 1))
                act.activation(XT4[s].rearrange("p k n -> p (k n)"), PS[0][:, 0:D], ACT.Copy).then_inc(sem("x4ts"), 1)
                act.wait_ge(sem("fxl"), 2 * t + 2)
                if t >= 2:
                    act.wait_ge(sem("sl_mm"), t - 1)
                act.activation(FX[s][:, :, 0:G], PS[2 + 2 * s][:, :].rearrange("p (h c) -> p h c", c=G), ACT.Copy).then_inc(sem("fxs"), 1)
                act.wait_ge(sem("sw_sub"), t + 1)
                act.activation(SW[s], SW[s], ACT.Exp).then_inc(sem("sw_exp"), 1)
                if t >= 1:
                    slice_turned(act, t - 1)
            slice_turned(act, NT - 1)

        def slice_turned(act, t):
            act.wait_ge(sem("sl_mm"), t + 1)
            act.activation(SWT[:, t, :, :].rearrange("p h n -> p (h n)"), PS[1][:, :], ACT.Copy).then_inc(sem("sw_t2"), 1)

        def slices_vector(ve):
            for t in range(NT):
                s = t % 2
                lg = PS[3 + 2 * s][:, :].rearrange("p (h g) -> p h g", g=G)
                ve.wait_ge(sem("fxl"), 2 * t + 2)
                if t >= 2:
                    ve.wait_ge(sem("sl_mm"), t - 1)
                ve.tensor_reduce(SM[s][:, 0, :], lg, AX.X, ALU.max)
                ve.drain()
                ve.tensor_tensor(SW[s], lg, SM[s][:, 0, :].unsqueeze(2).to_broadcast([P, H2, G]), ALU.subtract).then_inc(sem("lgs"), 1)
                ve.drain()
                ve.tensor_copy(SM[s][:, 1, 0:1], SM[s][:, 0, 0:1]).then_inc(sem("sw_sub"), 1)
                ve.wait_ge(sem("sw_exp"), t + 1)
                ve.tensor_reduce(SM[s][:, 1, :], SW[s], AX.X, ALU.add)
                ve.drain()
                ve.reciprocal(SM[s][:, 2, :], SM[s][:, 1, :])
                ve.drain()
                ve.tensor_scalar(SM[s][:, 2, :], SM[s][:, 2, :], valid[:, t:t + 1], None, ALU.mult)
                ve.drain()
                ve.tensor_tensor(SW[s], SW[s], SM[s][:, 2, :].unsqueeze(2).to_broadcast([P, H2, G]), ALU.mult).then_inc(sem("sw"), 1)

        def tokens_vector(ve):
            ve.wait_ge(sem("sl_mm"), NT)
            for h in range(HP):
                tp = tok_ps(h)
                if h:
                    ve.wait_ge(sem("tk_m"), h)
                ve.memset(TOK, 0.0)
                for j in range(2):
                    r, c0 = slice(j * G, (j + 1) * G), j * (G + 1)
                    ve.tensor_scalar(SA[r, 0:1], tp[r, c0 + G:c0 + G + 1], 1.0e-5, None, ALU.add)
                ve.drain()
                ve.reciprocal(SA[:, 1:2], SA[:, 0:1])
                ve.drain()
                for j in range(2):
                    r, c0 = slice(j * G, (j + 1) * G), j * (G + 1)
                    ins = ve.tensor_scalar(TOK[r, j * G:(j + 1) * G], tp[r, c0:c0 + G], SA[r, 1:2], None, ALU.mult)
                ins.then_inc(sem("tk"), 1)
                ve.wait_ge(sem("tkt_ps"), h + 1)
                ve.tensor_copy(TOKT, PS[0][:, 0:P]).then_inc(sem("tkt"), 1)
                ve.wait_ge(sem("qkv_ps"), h + 1)
                ve.tensor_copy(QT, PS[1][:, 0:P])
                ve.tensor_copy(KT, PS[1][:, P:2 * P])
                ve.tensor_copy(VV, PS[1][:, 2 * P:3 * P]).then_inc(sem("qkv"), 1)
                ve.wait_ge(sem("sc_ps"), h + 1)
                ve.tensor_scalar(PP, BDM, BIG, -BIG, ALU.mult, ALU.add)
                ve.drain()
                ve.scalar_tensor_tensor(out=PP, in0=PS[0][:, P:2 * P], scalar=float(G) ** -0.5, in1=PP, op0=ALU.mult, op1=ALU.add)
                ve.drain()
                ve.tensor_reduce(SA[:, 2:3], PP, AX.X, ALU.max)
                ve.drain()
                ve.tensor_scalar(PP, PP, SA[:, 2:3], None, ALU.subtract).then_inc(sem("sc"), 1)
                ve.wait_ge(sem("sc_exp"), h + 1)
                ve.tensor_reduce(SA[:, 3:4], PP, AX.X, ALU.add)
                ve.drain()
                ve.reciprocal(SA[:, 4:5], SA[:, 3:4])
                ve.drain()
                ve.tensor_scalar(PP, PP, SA[:, 4:5], None, ALU.mult).then_inc(sem("pp"), 1)
                ve.wait_ge(sem("ppt_ps"), h + 1)
                ve.tensor_copy(PPT, PS[2][:, 0:P]).then_inc(sem("ppt"), 1)
                ve.wait_ge(sem("ott_ps"), h + 1)
                ve.tensor_copy(OTT, PS[2][:, P:2 * P]).then_inc(sem("ott"), 1)
                ve.wait_ge(sem("tk_m"), h + 1)
                ve.tensor_copy(MO[:, h, :], PS[3][:, 0:D]).then_inc(sem("mo"), 1)
                ve.drain()

        def tokens_scalar(act):
            for h in range(HP):
                act.wait_ge(sem("sc"), h + 1)
                act.activation(PP, PP, ACT.Exp).then_inc(sem("sc_exp"), 1)

        def tokens_tensor(pe):
            pe.wait_ge(sem("sw_t2"), NT)
            for h in range(HP):
                pe.wait_ge(sem("tk"), h + 1)
                pe.transpose(PS[0][:, 0:P], TOK, ident[:, :]).then_inc(sem("tkt_ps"), 1)
                pe.wait_ge(sem("tkt"), h + 1)
                pe.matmul(PS[1][:, 0:P], BDS[:, 1, :], TOKT, start=True, stop=True)
                pe.matmul(PS[1][:, P:2 * P], BDS[:, 2, :], TOKT, start=True, stop=True)
                pe.matmul(PS[1][:, 2 * P:3 * P], TOKT, BDS[:, 3, :], start=True, stop=True).then_inc(sem("qkv_ps"), 1)
                pe.wait_ge(sem("qkv"), h + 1)
                pe.matmul(PS[0][:, P:2 * P], QT, KT, start=True, stop=True).then_inc(sem("sc_ps"), 1)
                pe.wait_ge(sem("pp"), h + 1)
                pe.transpose(PS[2][:, 0:P], PP, ident[:, :]).then_inc(sem("ppt_ps"), 1)
                pe.wait_ge(sem("ppt"), h + 1)
                pe.matmul(PS[2][:, P:2 * P], VV, PPT, start=True, stop=True).then_inc(sem("ott_ps"), 1)
                pe.wait_ge(sem("ott"), h + 1)
                if h:
                    pe.wait_ge(sem("mo"), h)
                pe.matmul(PS[3][:, 0:D], OTT, WOUT[:, h, :], start=True, stop=True).then_inc(sem("tk_m"), 1)

        def final_tensor(pe):
            pe.wait_ge(sem("mo"), HP)
            for t in range(25):
                if t >= 4:
                    pe.wait_ge(sem("fin"), t - 3)
                y = PS[4 + t % 4][:, 0:D]
                for h in range(HP):
                    pe.matmul(y, SWT[:, t, h, :], MO[:, h, :], start=(h == 0), stop=False)
                pe.matmul(y, ones[0:1, :], RBO[0:1, :], start=False, stop=True).then_inc(sem("fin_ps"), 1)

        def final_vector(ve):
            for t in range(25):
                ve.wait_ge(sem("fin_ps"), t + 1)
                ve.tensor_tensor(X[:, t, :], X[:, t, :], PS[4 + t % 4][:, 0:D], ALU.add).then_inc(sem("fin"), 1)

        def final_sync(sp):
            for g in range(4):
                sp.wait_ge(sem("fin"), 6 * g + 6)
                sp.dma_start(out[768 * g:768 * g + 768, :].rearrange("(t p) d -> p t d", p=P), X[:, 6 * g:6 * g + 6, :]
                             ).then_inc(sem("out"), 16)
            sp.wait_ge(sem("fin"), 25)
            sp.dma_start(out[24 * P:N, :], X[0:TAIL, 24, :]).then_inc(sem("out"), 16)
            sp.wait_ge(sem("out"), 80)

        @block.sync
        def _(sp):
            loads_sync(sp)
            meta_sync(sp)
            mlp_sync(sp)
            route_sync(sp)
            experts_sync(sp)
            types_sync(sp)
            kvq_sync(sp)
            kvq_rows_sync(sp)
            for o in range(2):
                score_sync(sp, o)
                sum_sync(sp, o)
            proj_sync(sp)
            slice_sync(sp)
            final_sync(sp)

        @block.gpsimd
        def _(pool):
            consts_pool(pool)
            scatter_pool(pool)
            l0_pool(pool)
            route_pool(pool)
            expert_rows_pool(pool)
            types_pool(pool)
            kvq_rows_pool(pool)
            for o in range(2):
                score_pool(pool, o)
            agg_pool(pool)
            proj_rows_pool(pool)

        @block.scalar
        def _(act):
            ln_scalar(act, 1)
            embed_scalar(act)
            mlp_scalar(act)
            ln_scalar(act, 2)
            route_scalar(act)
            experts_scalar(act)
            ln_scalar(act, 3)
            kvq_scalar(act)
            for o in range(2):
                score_scalar(act, o)
                sum_scalar(act, o)
            proj_scalar(act)
            ln_scalar(act, 4)
            slices_scalar(act)
            tokens_scalar(act)

        @block.tensor
        def _(pe):
            rank_tensor(pe, 0)
            rank_tensor(pe, 1)
            l0_tensor(pe)
            mlp_tensor(pe)
            route_tensor(pe)
            experts_tensor(pe)
            place_tensor(pe, "t", OHt.rearrange("p t g -> p (t g)"), T1)
            kvq_tensor(pe)
            for o in range(2):
                score_tensor(pe, o)
                sum_tensor(pe, o)
            proj_tensor(pe)
            slice_prep_tensor(pe)
            slices_tensor(pe)
            tokens_tensor(pe)
            final_tensor(pe)

        @block.vector
        def _(ve):
            ve.memset(ZR, 0.0).then_inc(sem("zeros"), 1)
            ve.memset(X[:, 24:NT, :], 0.0).then_inc(sem("xpad"), 1)
            ve.memset(slot_e[0][:, :], 1 << 20)
            ve.memset(slot_e[1][:, :], 1 << 20)
            ve.wait_ge(sem("ids"), 32)
            ve.wait_ge(sem("consts"), 1)
            rank_vector(ve, 0)
            rank_vector(ve, 1)
            ve.wait_ge(sem("x_in"), 32)
            ln_vector(ve, 1)
            embed_vector(ve)
            l0_vector(ve)
            ve.drain()
            mlp_vector(ve)
            ln_vector(ve, 2)
            route_vector(ve)
            experts_vector(ve)
            expert_rows_vector(ve)
            ln_vector(ve, 3)
            types_vector(ve)
            kvq_rows_vector(ve)
            for o in range(2):
                score_vector(ve, o)
                sum_vector(ve, o)
            proj_vector(ve)
            proj_rows_vector(ve)
            ln_vector(ve, 4)
            slice_prep_vector(ve)
            slices_vector(ve)
            tokens_vector(ve)
            final_vector(ve)


_INS = ["x", "src", "dst", "edge_attr_5", "edge_weight", "node_type_19", "L0_gnn_eps", "L0_gnn_w1", "L0_gnn_b1",
        "L0_gnn_w2", "L0_gnn_b2", "L0_ffn_gate_w", "L0_ffn_gate_b", "L0_ffn_w1", "L0_ffn_b1", "L0_ffn_w2", "L0_ffn_b2",
        "L1_gnn_Wk", "L1_gnn_bk", "L1_gnn_Wq", "L1_gnn_bq", "L1_gnn_Wv", "L1_gnn_bv", "L1_gnn_Wa", "L1_gnn_ba",
        "L1_gnn_gamma", "L1_gnn_beta", "L1_gnn_w_time", "L1_gnn_b_time", "L1_ffn_W_fx", "L1_ffn_b_fx", "L1_ffn_W_x",
        "L1_ffn_b_x", "L1_ffn_W_slice", "L1_ffn_b_slice", "L1_ffn_W_q", "L1_ffn_W_k", "L1_ffn_W_v", "L1_ffn_W_out",
        "L1_ffn_b_out", "L1_ffn_temperature"]


def kernel(**inputs):
    import numpy as _np
    import concourse.bacc as _bacc
    from concourse import mybir as _mybir
    from concourse.bass_utils import run_bass_kernel_spmd as _run

    nc = _bacc.Bacc("TRN2", target_bir_lowering=False, num_devices=1)
    arrays, aps = {}, {}
    for name in _INS:
        a = _np.ascontiguousarray(inputs[name])
        arrays[f"in_{name}"] = a
        aps[name] = nc.dram_tensor(f"in_{name}", a.shape, _mybir.dt.from_np(a.dtype), kind="ExternalInput").ap()
    out = nc.dram_tensor("out_0", (N, D), _mybir.dt.float32, kind="ExternalOutput").ap()
    build(nc, aps, out)
    r = _run(nc, [arrays], core_ids=[0])
    return r.results[0]["out_0"]
```

```python
from contextlib import ExitStack

import concourse.bass as bass
from concourse import mybir

ALU = mybir.AluOpType
ACT = mybir.ActivationFunctionType
AX = mybir.AxisListType
F32 = mybir.dt.float32
BF16 = mybir.dt.bfloat16
I32 = mybir.dt.int32
U32 = mybir.dt.uint32
ds = bass.ds

P = 128
N, D = 3125, 256
NT = 26
TAIL = N - 24 * P
E = 50000
EP, EC = 125, 400
W = 25
NB = 416
U = 4
SL = 4
NG = NB // U
REC = 128
R_EQ, R_META = 64, 96
CC = 10
PROJ, TD, H1, DK = 192, 32, 4, 56
KV = 2 * PROJ
ROW = KV + 3 * TD
SROW = D + H1
T1 = 19
TT = 44
EX, F = 8, 1024
CAP = 489
CAPP = 512
H2, G = 8, 64
LN_EPS = 1e-5
BIG = 2.0 ** 100
TWO_PI = 6.283185307179586
MAGIC = 12582912.0
FAR = float(1 << 20)


def build(nc, A, out):
    ctx = ExitStack()
    with ctx:
        ctx.enter_context(nc.allow_non_contiguous_dma(reason="small tables of biases and types"))
        sems = {}

        def sem(name):
            if name not in sems:
                sems[name] = ctx.enter_context(nc.semaphore(name))
            return sems[name]

        def sb(name, shape, dt=F32):
            return ctx.enter_context(nc.sbuf_tensor(name, shape, dt))

        def dram(name, rows, cols):
            return nc.dram_tensor(name, (rows, cols), F32).ap()

        xn_tab = dram("xn_tab", NT * P, D)
        kv_tab = dram("kv_tab", NT * P, KV)
        rec_tab = [dram("rec_dst", NB * P, REC), dram("rec_src", NB * P, REC)]
        v_tab = [dram("v_dst", NB * P, PROJ), dram("v_src", NB * P, PROJ)]
        moe_in = dram("moe_in", EX * CAPP, D)
        moe_out = dram("moe_out", EX * CAPP, D)
        typ_x = dram("typ_x", TT * P, D)
        typ_agg = dram("typ_agg", TT * P, D)
        typ_kvq = dram("typ_kvq", TT * P, KV + DK)
        typ_y = dram("typ_y", TT * P, D)

        X = sb("X", [P, NT, D])
        XN = sb("XN", [P, NT, D])
        BIGR = sb("BIGR", [P, NT * (SROW + D)])
        ACC = BIGR[:, 0:NT * SROW].rearrange("p (t c) -> p t c", c=SROW)
        AGG = BIGR[:, NT * SROW:].rearrange("p (t c) -> p t c", c=D)
        AR = sb("AR", [P, 15600])
        QS = sb("QS", [P, NT, DK])
        M = sb("M", [P, NT, H1])
        META = [sb("META0", [P, NB, 4]), sb("META1", [P, NB, 4])]
        ident = sb("ident", [P, P])
        identb = sb("identb", [P, P], BF16)
        tri = sb("tri", [P, P])
        ones = sb("ones", [P, P])
        iota1 = sb("iota1", [P, P])
        iotaz = sb("iotaz", [P, P])
        pcol = sb("pcol", [P, 1])
        valid = sb("valid", [P, NT])
        win = [sb("win0", [1, NB], I32), sb("win1", [1, NB], I32)]
        slot_e = [sb("slot_e0", [P, EC], I32), sb("slot_e1", [P, EC], I32)]
        mv = sb("mv", [P, NT, 2])
        rs = sb("rs", [P, 4, NT])
        bst = sb("bst", [P, 2, 6])
        slot_m = sb("slot_m", [P, NT], I32)
        rowof_m = sb("rowof_m", [P, NT], I32)
        gate_p = sb("gate_p", [P, NT])
        slot_t = sb("slot_t", [P, NT], I32)
        rowof_t = sb("rowof_t", [P, NT], I32)
        ttype = sb("ttype", [1, TT], I32)

        def ar(off, *shape, dt=F32):
            n = 1
            for k in shape:
                n *= k
            v = AR[:, off:off + n]
            if dt is not F32:
                v = AR[:, off:off + (n // 2 if dt is BF16 else n)].bitcast(dt)
            if len(shape) == 2:
                v = v.rearrange("p (a b) -> p a b", b=shape[1])
            if len(shape) == 3:
                v = v.rearrange("p (a b c) -> p a b c", b=shape[1], c=shape[2])
            return v

        PS = [ctx.enter_context(nc.psum_tensor(f"ps{k}", [P, 512], F32)) for k in range(8)]

        ids = [ar(0, EC, dt=I32), ar(400, EC, dt=I32)]
        wgt = ar(800, EC)
        lo1 = [ar(1200, EC), ar(1600, EC)]
        attr = ar(2000, EC, 5)
        logt = ar(4000, EC * 3)
        SCAN = ar(5200, W, EC)
        MASK = BIGR[:, 0:W * EC].rearrange("p (a b) -> p a b", b=EC)
        hi_i = ar(15200, EC, dt=I32)
        rk = sb("rk", [P, 5, 32])
        rk_i = sb("rk_i", [P, 32], I32)
        tmpf = BIGR[:, 10400:10816]
        jrow = BIGR[0:1, 12000:12416]
        wt_row = sb("wt_row", [P, 2, TD])
        Z0, Z1 = ar(5200, CC * 3, TD), ar(6160, CC * 3, TD)
        RD = [[ar(7200 + 2560 * s + 1280 * o, CC, REC) for o in range(2)] for s in range(2)]
        scst = [[sb(f"scst{s}{o}", [P, CC], I32) for o in range(2)] for s in range(2)]

        def loads_of(eng, ap_row, maxv, etype):
            _, vals = nc.values_load_multi_w_load_instructions(
                ap_row, engines=[etype], min_val=0, max_val=maxv,
                skip_runtime_bounds_check_because="clamped when the table was computed")
            return vals

        ET = mybir.EngineType
        block = ctx.enter_context(nc.Block())

        def bc(ap, shape):
            return ap.to_broadcast(shape)

        def ln_vector(ve, tag):
            for t in range(NT):
                ve.bn_stats(bst[:, t % 2, :], X[:, t, :])
                ve.drain()
                ve.bn_aggr(mv[:, t, :], bst[:, t % 2, :])
            ve.drain()
            ve.tensor_scalar(rs[:, 0, :], mv[:, :, 1], LN_EPS, None, ALU.add).then_inc(sem("var"), 1)
            ve.wait_ge(sem("sd"), tag)
            newton(ve, rs, slice(0, NT))
            for t in range(NT):
                ve.tensor_scalar(XN[:, t, :], X[:, t, :], mv[:, t, 0:1], rs[:, 3, t:t + 1],
                                 ALU.subtract, ALU.mult).then_inc(sem("xn"), 1)
            ve.drain()

        def newton(ve, r, sl):
            ve.reciprocal(r[:, 2, sl], r[:, 1, sl])
            ve.drain()
            ve.tensor_tensor(r[:, 2, sl], r[:, 2, sl], r[:, 0, sl], ALU.mult)
            ve.drain()
            ve.tensor_tensor(r[:, 2, sl], r[:, 2, sl], r[:, 1, sl], ALU.add)
            ve.drain()
            ve.tensor_scalar(r[:, 2, sl], r[:, 2, sl], 0.5, None, ALU.mult)
            ve.drain()
            ve.reciprocal(r[:, 3, sl], r[:, 2, sl])
            ve.drain()

        def ln_scalar(act, tag):
            act.wait_ge(sem("var"), tag)
            act.activation(rs[:, 1, :], rs[:, 0, :], ACT.Sqrt).then_inc(sem("sd"), 1)

        def consts_pool(pool):
            pool.memset(ident[:, :], 0.0)
            pool.memset(tri[:, :], 1.0)
            pool.memset(ones[:, :], 1.0)
            pool.iota(iota1[:, :], [[1, P]], base=1, channel_multiplier=0, allow_small_or_imprecise_dtypes=True)
            pool.iota(iotaz[:, :], [[1, P]], base=0, channel_multiplier=0, allow_small_or_imprecise_dtypes=True)
            pool.iota(pcol[:, :], [[0, 1]], base=0, channel_multiplier=1, allow_small_or_imprecise_dtypes=True)
            pool.iota(jrow, [[1, NB]], base=0, channel_multiplier=0, allow_small_or_imprecise_dtypes=True)
            pool.drain()
            pool.affine_select(out=ident[:, :], in_=ident[:, :], compare_op=ALU.not_equal, fill=1.0, base=0,
                               pattern=[[-1, P]], channel_multiplier=1)
            pool.affine_select(out=tri[:, :], in_=tri[:, :], compare_op=ALU.is_gt, fill=0.0, base=0,
                               pattern=[[1, P]], channel_multiplier=-1)
            pool.drain()
            pool.tensor_copy(identb[:, :], ident[:, :]).then_inc(sem("consts"), 1)

        ZR = BIGR[:, 10900:11924]

        def zero_view(tab, rows, cols):
            return tab.rearrange("(p c) w -> p (c w)", p=P).rearrange("p (k n) -> p k n", n=1024)

        def loads_sync(sp):
            sp.dma_start(ids[0][0:EP], A["dst"].rearrange("(p c) -> p c", p=EP)).then_inc(sem("ids"), 16)
            sp.dma_start(ids[1][0:EP], A["src"].rearrange("(p c) -> p c", p=EP)).then_inc(sem("ids"), 16)
            sp.wait_ge(sem("xpad"), 1)
            sp.dma_start(X[:, 0:24, :], A["x"][0:24 * P, :].rearrange("(t p) d -> p t d", p=P)).then_inc(sem("x_in"), 16)
            sp.dma_start(X[0:TAIL, 24, :], A["x"][24 * P:N, :]).then_inc(sem("x_in"), 16)
            sp.dma_start(attr[0:EP], A["edge_attr_5"].rearrange("(p c) k -> p c k", p=EP)).then_inc(sem("edges_in"), 16)
            sp.dma_start(wgt[0:EP], A["edge_weight"].rearrange("(p c) -> p c", p=EP)).then_inc(sem("edges_in"), 16)
            for k, name in enumerate(("L1_gnn_w_time", "L1_gnn_b_time")):
                sp.dma_start(wt_row[:, k, :], A[name].rearrange("(a n) -> a n", a=1).to_broadcast([P, TD])).then_inc(sem("edges_in"), 16)
            sp.wait_ge(sem("zeros"), 1)
            for tab, rows, cols in ((rec_tab[0], NB * P, REC), (rec_tab[1], NB * P, REC), (moe_in, EX * CAPP, D),
                                    (typ_x, TT * P, D), (typ_agg, TT * P, D)):
                v = zero_view(tab, rows, cols)
                sp.dma_start(v, ZR.unsqueeze(1).to_broadcast([P, v.shape[1], 1024])).then_inc(sem("zeroed"), 16)
            for t in range(NT):
                sp.wait_ge(sem("xn"), t + 1)
            sp.dma_start(xn_tab.rearrange("(t p) d -> p t d", p=P), XN[:, :, :]).then_inc(sem("xn_tab"), 16)

        def rank_vector(ve, o):
            ve.tensor_scalar(hi_i[0:EP], ids[o][0:EP], 7, None, ALU.arith_shift_right)
            ve.drain()
            ve.tensor_copy(tmpf[0:EP, 0:EC], hi_i[0:EP])
            ve.drain()
            ve.tensor_scalar(hi_i[0:EP], ids[o][0:EP], 127, None, ALU.bitwise_and)
            ve.tensor_tensor(MASK[0:EP], tmpf[0:EP, 0:EC].unsqueeze(1).to_broadcast([EP, W, EC]),
                             iotaz[0:EP, 0:W].unsqueeze(2).to_broadcast([EP, W, EC]), ALU.is_equal)
            ve.drain()
            ve.tensor_scalar(lo1[o][0:EP], hi_i[0:EP], 1.0, None, ALU.add)
            ve.tensor_reduce(rk[0:EP, 0, 0:W], MASK[0:EP], AX.X, ALU.add).then_inc(sem("tot_e"), 1)
            ve.wait_ge(sem("cross_e"), o + 1)
            ve.tensor_scalar(rk_i[:, 0:W], PS[0][:, 32:32 + W], 127.0, None, ALU.add)
            ve.drain()
            ve.tensor_scalar(rk_i[:, 0:W], rk_i[:, 0:W], 7, None, ALU.arith_shift_right)
            ve.drain()
            ve.tensor_copy(rk[:, 1, 0:W], rk_i[:, 0:W])
            ve.drain()
            ve.tensor_tensor_scan(rk[:, 2, 0:W], ones[:, 0:W], rk[:, 1, 0:W], 0.0, ALU.mult, ALU.add)
            ve.drain()
            ve.tensor_tensor(rk[:, 3, 0:W], rk[:, 2, 0:W], rk[:, 1, 0:W], ALU.subtract)
            ve.drain()
            ve.scalar_tensor_tensor(out=rk[0:EP, 4, 0:W], in0=rk[0:EP, 3, 0:W], scalar=128.0, in1=PS[0][0:EP, 0:W],
                                    op0=ALU.mult, op1=ALU.add)
            ve.drain()
            for w in range(W):
                ve.tensor_tensor_scan(SCAN[0:EP, w, :], bc(ones[0:EP, 0:1], [EP, EC]), MASK[0:EP, w, :],
                                      rk[0:EP, 4, w:w + 1], ALU.mult, ALU.add)
            ve.drain()
            ve.tensor_tensor(MASK[0:EP], MASK[0:EP], SCAN[0:EP], ALU.mult)
            ve.drain()
            ve.tensor_reduce(tmpf[0:EP, 0:EC], MASK[0:EP].rearrange("p w j -> p j w"), AX.X, ALU.add)
            ve.drain()
            ve.tensor_scalar(slot_e[o][0:EP], tmpf[0:EP, 0:EC], -1.0, None, ALU.add)
            cmp = MASK[0:1].rearrange("p a b -> p (a b)")[:, 0:208 * W].rearrange("p (j w) -> p j w", w=W)
            for half in range(2):
                js = slice(208 * half, 208 * half + 208)
                ve.drain()
                ve.tensor_tensor(cmp, rk[0:1, 2, 0:W].unsqueeze(1).to_broadcast([1, 208, W]),
                                 jrow[:, js].unsqueeze(2).to_broadcast([1, 208, W]), ALU.is_le)
                ve.drain()
                ve.tensor_reduce(tmpf[0:1, js], cmp, AX.X, ALU.add)
            ve.drain()
            ve.tensor_scalar(win[o][:, :], tmpf[0:1, 0:NB], float(W - 1), None, ALU.min).then_inc(sem("win"), 1)
            ve.drain()

        def rank_tensor(pe, o):
            pe.wait_ge(sem("consts"), 1)
            pe.wait_ge(sem("tot_e"), o + 1)
            pe.matmul(PS[0][0:EP, 0:W], tri[0:EP, 0:EP], rk[0:EP, 0, 0:W], start=True, stop=True)
            pe.matmul(PS[0][:, 32:32 + W], ones[0:EP, :], rk[0:EP, 0, 0:W], start=True, stop=True).then_inc(sem("cross_e"), 1)


        def run(eng, n, body):
            body(0, True)
            with eng.Fori(1, n) as i:
                body(i, False)

        NCH = EC // CC // 2

        def embed_vector(ve):
            ve.wait_ge(sem("edges_in"), 64)
            ve.tensor_scalar(wt_row[:, 1, :], wt_row[:, 1, :], TWO_PI / 4, None, ALU.add)
            for s in range(2):
                for o in range(2):
                    ve.memset(RD[s][o], 0.0)
            ve.drain()
            ve.wait_ge(sem("logt"), 1)

            def body(i, first):
                for s in range(2):
                    c = 2 * i + s
                    if not first:
                        ve.wait_ge(sem(f"rd_sent{s}"), 16 * 2 * CC * i)
                        ve.wait_ge(sem("sin_done"), 2 * i + s)
                    elif s:
                        ve.wait_ge(sem("sin_done"), 1)
                    ve.tensor_tensor(Z0[0:EP], logt[0:EP, ds(c * 3 * CC, 3 * CC)].unsqueeze(2).to_broadcast([EP, 3 * CC, TD]),
                                     wt_row[0:EP, 0, :].unsqueeze(1).to_broadcast([EP, 3 * CC, TD]), ALU.mult)
                    ve.drain()
                    ve.tensor_tensor(Z0[0:EP], Z0[0:EP], wt_row[0:EP, 1, :].unsqueeze(1).to_broadcast([EP, 3 * CC, TD]), ALU.add)
                    ve.drain()
                    ve.tensor_scalar(Z1[0:EP], Z0[0:EP], 1.0 / TWO_PI, MAGIC, ALU.mult, ALU.add)
                    ve.drain()
                    ve.tensor_scalar(Z1[0:EP], Z1[0:EP], MAGIC, -TWO_PI, ALU.subtract, ALU.mult)
                    ve.drain()
                    ve.tensor_tensor(Z0[0:EP], Z0[0:EP], Z1[0:EP], ALU.add)
                    ve.drain()
                    ve.tensor_scalar(Z0[0:EP], Z0[0:EP], 3.1415925, -3.1415925, ALU.min, ALU.max).then_inc(sem("z_ready"), 1)
                    for o in range(2):
                        r = RD[s][o]
                        ve.tensor_copy(r[0:EP, :, R_META].bitcast(I32), ids[1 - o][0:EP, ds(c * CC, CC)])
                        ve.tensor_copy(r[0:EP, :, R_META + 1], lo1[o][0:EP, ds(c * CC, CC)])
                        ve.tensor_copy(r[0:EP, :, R_META + 2], wgt[0:EP, ds(c * CC, CC)]).then_inc(sem("rd_meta"), 1)

            run(ve, NCH, body)
            ve.drain()

        def embed_scalar(act):
            act.wait_ge(sem("edges_in"), 64)
            act.activation(logt[0:EP].rearrange("p (j k) -> p j k", k=3), attr[0:EP, :, 0:3], ACT.Ln, bias=1.0).then_inc(sem("logt"), 1)

            def body(i, first):
                for s in range(2):
                    act.wait_ge(sem("z_ready"), 2 * i + s + 1)
                    z = Z0.rearrange("p (j k) n -> p j k n", k=3)
                    for o, order in enumerate(((1, 0, 2), (2, 0, 1))):
                        for q, k in enumerate(order):
                            ins = act.activation(RD[s][o][0:EP, :, q * TD:(q + 1) * TD], z[0:EP, :, k, :], ACT.Sin)
                    ins.then_inc(sem("sin_done"), 1)

            run(act, NCH, body)

        def scatter_pool(pool):
            pool.wait_ge(sem("win"), 2)
            pool.wait_ge(sem("zeroed"), 16 * 5)

            def body(i, first):
                for s in range(2):
                    c = 2 * i + s
                    if not first:
                        pool.wait_ge(sem(f"rd_sent{s}"), 16 * 2 * CC * i)
                    for o in range(2):
                        pool.tensor_copy(scst[s][o][:, :], slot_e[o][:, ds(c * CC, CC)]).then_inc(sem("scst"), 1)
                    pool.wait_ge(sem("scst"), 4 * i + 2 * s + 2)
                    pool.wait_ge(sem("sin_done"), 2 * i + s + 1)
                    pool.wait_ge(sem("rd_meta"), 4 * i + 2 * s + 2)
                    pool.nop(nofuse=True)
                    for o in range(2):
                        for k in range(CC):
                            pool.indirect_dma_start(
                                rec_tab[o], bass.IndirectOffsetOnAxis(ap=scst[s][o][:, k:k + 1].bitcast(U32), axis=0),
                                RD[s][o][:, k, :], None, bounds_check=NB * P - 1, oob_is_err=False,
                            ).then_inc(sem(f"rd_sent{s}"), 16)

            run(pool, NCH, body)

        def meta_sync(sp):
            for s in range(2):
                sp.wait_ge(sem(f"rd_sent{s}"), 16 * 2 * CC * NCH)
            for o in range(2):
                v = rec_tab[o].rearrange("(b p) c -> p b c", p=P)
                for q in range(4):
                    bs = slice(104 * q, 104 * q + 104)
                    sp.dma_start(META[o][:, bs, :], v[:, bs, R_META:R_META + 4]).then_inc(sem(f"meta{o}"), 16)

        def pipe(eng, stages):
            lead = max(ahead for ahead, _ in stages)

            def step(i, s):
                for ahead, f in stages:
                    q = s + ahead
                    f(i + q // SL, q % SL)

            def edge(k):
                for ahead, f in stages:
                    if 0 <= k + ahead < NG:
                        f((k + ahead) // SL, (k + ahead) % SL)

            for k in range(-lead, SL):
                edge(k)
            last = (NG - lead) // SL
            with eng.Fori(1, last) as i:
                for s in range(SL):
                    step(i, s)
            for k in range(last * SL, NG):
                edge(k)

        def later(i, least=1):
            return not (isinstance(i, int) and i < least)

        GA = [ar(7200 + 1024 * s, U, D) for s in range(SL)]
        OW = [ar(11296 + 512 * s, U, P) for s in range(SL)]
        MST = [sb(f"mst{s}", [P, U, 4]) for s in range(SL)]
        IST = [sb(f"ist{s}", [P, U], I32) for s in range(SL)]

        def l0_ps(s, u):
            return PS[2 * s + u // 2][:, (u % 2) * D:(u % 2) * D + D]

        def l0_pool(pool):
            pool.wait_ge(sem("meta0"), 64)
            pool.wait_ge(sem("xn_tab"), 16)

            def gather(i, s):
                g = SL * i + s
                if later(i):
                    pool.wait_ge(sem("l0_mm"), g - SL + 1)
                pool.tensor_copy(IST[s][:, :], META[0][:, ds(g * U, U), 0].bitcast(I32)).then_inc(sem("ist"), 1)
                pool.wait_ge(sem("ist"), g + 1)
                pool.nop(nofuse=True)
                for u in range(U):
                    pool.indirect_dma_start(GA[s][:, u, :], None, xn_tab,
                                            bass.IndirectOffsetOnAxis(ap=IST[s][:, u:u + 1].bitcast(U32), axis=0)
                                            ).then_inc(sem(f"rows{s}"), 16)

            pipe(pool, [(0, gather)])

        def l0_vector(ve):
            ve.wait_ge(sem("meta0"), 64)
            ve.wait_ge(sem("zeroed"), 80)
            ve.memset(BIGR[:, 0:NT * SROW], 0.0)
            ve.drain()

            def weights(i, s):
                g = SL * i + s
                if later(i):
                    ve.wait_ge(sem("l0_mm"), g - SL + 1)
                ve.tensor_copy(MST[s][:, :, :], META[0][:, ds(g * U, U), :])
                ve.drain()
                for u in range(U):
                    ins = ve.tensor_scalar(OW[s][:, u, :], iota1[:, :], MST[s][:, u, 1:2], MST[s][:, u, 2:3],
                                           ALU.is_equal, ALU.mult)
                ins.then_inc(sem("l0_ow"), 1)

            def add(i, s):
                g = SL * i + s
                ws = loads_of(ve, win[0][0:1, ds(g * U, U)], W - 1, ET.DVE)
                ve.wait_ge(sem("l0_mm"), g + 1)
                for u in range(U):
                    a = ACC[:, ds(ws[u], 1), 0:D].rearrange("p t d -> p (t d)")
                    ins = ve.tensor_tensor(a, a, l0_ps(s, u), ALU.add)
                    if u == U - 1:
                        ins.then_inc(sem("l0_add"), 1)
                    ve.drain()

            pipe(ve, [(2, weights), (0, add)])

        def l0_tensor(pe):
            def mm(i, s):
                g = SL * i + s
                pe.wait_ge(sem("l0_ow"), g + 1)
                pe.wait_ge(sem(f"rows{s}"), 64 * (i + 1))
                if later(i):
                    pe.wait_ge(sem("l0_add"), g - SL + 1)
                for u in range(U):
                    ins = pe.matmul(l0_ps(s, u), OW[s][:, u, :], GA[s][:, u, :], start=True, stop=True)
                ins.then_inc(sem("l0_mm"), 1)

            pipe(pe, [(0, mm)])


        NH = NT // 2
        w1_sb, w2_sb = ar(3100, 2, D), ar(3612, 2, D)
        b1c, b2r, epsc = ar(4124, 2), ar(4126, 1, D), ar(4382, 1)
        HS = [ar(4400 + 256 * s, D) for s in range(2)]
        HTS = [ar(4912 + 256 * s, 2, P) for s in range(2)]
        ZTS = [ar(5424 + 256 * s, 2, P) for s in range(2)]

        def mlp_sync(sp):
            for s in range(2):
                sp.wait_ge(sem(f"rd_sent{s}"), 16 * 2 * CC * NCH)
            sp.dma_start(w1_sb, A["L0_gnn_w1"].rearrange("(k p) n -> p k n", p=P)).then_inc(sem("mlp_w"), 16)
            sp.dma_start(w2_sb, A["L0_gnn_w2"].rearrange("(k p) n -> p k n", p=P)).then_inc(sem("mlp_w"), 16)
            sp.dma_start(b1c, A["L0_gnn_b1"].rearrange("(k p) -> p k", p=P)).then_inc(sem("mlp_w"), 16)
            sp.dma_start(b2r[0:1, 0, :], A["L0_gnn_b2"].rearrange("(a n) -> a n", a=1)).then_inc(sem("mlp_w"), 16)
            sp.dma_start(epsc, A["L0_gnn_eps"].rearrange("(a n) -> a n", a=1).to_broadcast([P, 1])).then_inc(sem("mlp_w"), 16)

        def mlp_vector(ve):
            ve.wait_ge(sem("mlp_w"), 80)
            ve.tensor_scalar(epsc, epsc, 1.0, None, ALU.add)
            ve.drain()

            def body(i, first):
                for s in range(2):
                    t = 2 * i + s
                    if not first:
                        ve.wait_ge(sem("mlp_ht"), 2 * i + s - 1)
                    ve.scalar_tensor_tensor(out=HS[s], in0=XN[:, ds(t, 1), :].rearrange("p t d -> p (t d)"), scalar=epsc,
                                            in1=ACC[:, ds(t, 1), 0:D].rearrange("p t d -> p (t d)"),
                                            op0=ALU.mult, op1=ALU.add).then_inc(sem("mlp_h"), 1)
                for s in range(2):
                    t = 2 * i + s
                    ve.wait_ge(sem("mlp_y"), 2 * i + s + 1)
                    x = X[:, ds(t, 1), :].rearrange("p t d -> p (t d)")
                    ve.tensor_tensor(x, x, PS[4 + s][:, 0:D], ALU.add).then_inc(sem("mlp_x"), 1)

            run(ve, NH, body)
            ve.drain()

        def mlp_tensor(pe):
            pe.wait_ge(sem("mlp_w"), 80)

            def body(i, first):
                for s in range(2):
                    pe.wait_ge(sem("mlp_h"), 2 * i + s + 1)
                    for k in range(2):
                        ins = pe.transpose(PS[s][:, k * P:(k + 1) * P], HS[s][:, k * P:(k + 1) * P], ident[:, :])
                    ins.then_inc(sem("mlp_ht"), 1)
                for s in range(2):
                    pe.wait_ge(sem("mlp_hts"), 2 * i + s + 1)
                    for f in range(2):
                        for k in range(2):
                            ins = pe.matmul(PS[2 + s][:, f * P:(f + 1) * P], w1_sb[:, k, f * P:(f + 1) * P], HTS[s][:, k, :],
                                            start=(k == 0), stop=(k == 1))
                    ins.then_inc(sem("mlp_z"), 1)
                for s in range(2):
                    pe.wait_ge(sem("mlp_zs"), 2 * (2 * i + s + 1))
                    if not first:
                        pe.wait_ge(sem("mlp_x"), 2 * i + s - 1)
                    for k in range(2):
                        pe.matmul(PS[4 + s][:, 0:D], ZTS[s][:, k, :], w2_sb[:, k, :], start=(k == 0), stop=False)
                    pe.matmul(PS[4 + s][:, 0:D], ones[0:1, :], b2r[0:1, 0, :], start=False, stop=True).then_inc(sem("mlp_y"), 1)

            run(pe, NH, body)

        def mlp_scalar(act):
            act.wait_ge(sem("mlp_w"), 80)

            def body(i, first):
                for s in range(2):
                    act.wait_ge(sem("mlp_ht"), 2 * i + s + 1)
                    act.activation(HTS[s].rearrange("p k n -> p (k n)"), PS[s][:, 0:D], ACT.Copy).then_inc(sem("mlp_hts"), 1)
                for s in range(2):
                    act.wait_ge(sem("mlp_z"), 2 * i + s + 1)
                    for f in range(2):
                        act.activation(ZTS[s][:, f, :], PS[2 + s][:, f * P:(f + 1) * P], ACT.Relu,
                                       bias=b1c[:, f:f + 1]).then_inc(sem("mlp_zs"), 1)

            run(act, NH, body)

        def place_tensor(pe, tag, OH, n):
            pe.wait_ge(sem(f"oh_{tag}"), 1)
            pe.matmul(PS[0][:, 0:NT * n], tri[:, :], OH, start=True, stop=True)
            pe.matmul(PS[1][:, 0:NT * n], ones[:, :], OH, start=True, stop=True).then_inc(sem(f"cnt_{tag}"), 1)

        def place_vector(ve, tag, OH, n, TOT, INC, EXC):
            ve.wait_ge(sem(f"cnt_{tag}"), 1)
            ve.tensor_copy(TOT, PS[1][:, 0:NT * n].rearrange("p (t g) -> p t g", g=n))
            ve.drain()
            for g in range(n):
                ve.tensor_tensor_scan(INC[:, :, g], ones[:, 0:NT], TOT[:, :, g], 0.0, ALU.mult, ALU.add)
            ve.drain()
            ve.tensor_tensor(EXC, INC, TOT, ALU.subtract)
            ve.drain()
            ve.tensor_tensor(EXC, EXC, PS[0][:, 0:NT * n].rearrange("p (t g) -> p t g", g=n), ALU.add)
            ve.drain()

        gw_sb, gb_row = ar(0, 2, EX), ar(16, 1, EX)
        XTG = [ar(32 + 256 * s, 2, P) for s in range(2)]
        LG, OHm, T8a, T8b, T8c = (ar(600 + 208 * k, NT, EX) for k in range(5))
        R26 = ar(1700, 8, NT)
        b1T = ar(2000, EX * F // P)
        b2e = ar(2064, EX * D)
        b1raw = ar(4112, P)
        ME = 4300
        XE = [ar(ME + 1024 * s, 4, D) for s in range(2)]
        XET = ar(ME + 2048, 2, 4 * P)
        YB = ar(ME + 3072, 4, D)
        MW = [[BIGR[:, 4096 * s:4096 * s + 2048].rearrange("p (k n) -> p k n", k=2),
               BIGR[:, 4096 * s + 2048:4096 * s + 4096].rearrange("p (k n) -> p k n", k=8)] for s in range(2)]
        HM = BIGR[:, 8192:12288].rearrange("p (f n) -> p f n", f=8)
        b1s = [sb(f"b1s{s}", [P, 8]) for s in range(2)]

        def route_sync(sp):
            sp.wait_ge(sem("mlp_x"), NT)
            sp.dma_start(gw_sb, A["L0_ffn_gate_w"].rearrange("(k p) n -> p k n", p=P)).then_inc(sem("gw"), 16)
            sp.dma_start(gb_row[0:1, 0, :], A["L0_ffn_gate_b"].rearrange("(a n) -> a n", a=1)).then_inc(sem("gw"), 16)
            sp.dma_start(b1raw[0:64, :], A["L0_ffn_b1"].rearrange("e (f p) -> (e f) p", p=P)).then_inc(sem("gw"), 16)
            sp.dma_start(b2e[0:1, :], A["L0_ffn_b2"].rearrange("(a e) n -> a (e n)", a=1)).then_inc(sem("gw"), 16)

        def route_tensor(pe):
            pe.wait_ge(sem("gw"), 64)
            pe.transpose(PS[7][:, 0:64], b1raw[0:64, :], ident[0:64, 0:64]).then_inc(sem("b1T"), 1)
            for t in range(NT):
                pe.wait_ge(sem("xn"), NT + t + 1)
                if t >= 2:
                    pe.wait_ge(sem("xtg"), t - 1)
                for k in range(2):
                    ins = pe.transpose(PS[t % 2][:, k * P:(k + 1) * P], XN[:, t, k * P:(k + 1) * P], ident[:, :])
                ins.then_inc(sem("xtg_ps"), 1)
                pe.wait_ge(sem("xtg"), t + 1)
                lg = PS[6][:, t * EX:(t + 1) * EX]
                for k in range(2):
                    pe.matmul(lg, XTG[t % 2][:, k, :], gw_sb[:, k, :], start=(k == 0), stop=False)
                ins = pe.matmul(lg, ones[0:1, :], gb_row[0:1, 0, :], start=False, stop=True)
                if t == NT - 1:
                    ins.then_inc(sem("gate_lg"), 1)
                else:
                    ins.then_inc(sem("gate_mm"), 1)
            place_tensor(pe, "m", OHm.rearrange("p t g -> p (t g)"), EX)

        def route_scalar(act):
            act.wait_ge(sem("b1T"), 1)
            act.activation(b1T, PS[7][:, 0:64], ACT.Copy).then_inc(sem("b1T_sb"), 1)
            for t in range(NT):
                act.wait_ge(sem("xtg_ps"), t + 1)
                if t >= 2:
                    act.wait_ge(sem("gate_mm"), t - 1)
                act.activation(XTG[t % 2].rearrange("p k n -> p (k n)"), PS[t % 2][:, 0:D], ACT.Copy).then_inc(sem("xtg"), 1)
            act.wait_ge(sem("gate_sub"), 1)
            act.activation(T8a, T8a, ACT.Exp).then_inc(sem("gate_exp"), 1)

        def route_vector(ve):
            e_row = iotaz[:, 0:EX].unsqueeze(1).to_broadcast([P, NT, EX])
            ve.tensor_scalar(valid[:, 24:25], pcol[:, :], float(TAIL), None, ALU.is_lt)
            ve.memset(valid[:, 0:24], 1.0)
            ve.memset(valid[:, 25:26], 0.0)
            ve.wait_ge(sem("gate_lg"), 1)
            ve.tensor_copy(LG, PS[6][:, 0:NT * EX].rearrange("p (t g) -> p t g", g=EX))
            ve.drain()
            ve.tensor_reduce(R26[:, 0, :], LG, AX.X, ALU.max)
            ve.drain()
            ve.tensor_tensor(T8a, LG, R26[:, 0, :].unsqueeze(2).to_broadcast([P, NT, EX]), ALU.subtract).then_inc(sem("gate_sub"), 1)
            ve.tensor_tensor(T8b, LG, R26[:, 0, :].unsqueeze(2).to_broadcast([P, NT, EX]), ALU.is_equal)
            ve.tensor_scalar(T8c, e_row, -100.0, None, ALU.add)
            ve.drain()
            ve.tensor_tensor(T8b, T8b, T8c, ALU.mult)
            ve.drain()
            ve.tensor_reduce(R26[:, 1, :], T8b, AX.X, ALU.min)
            ve.drain()
            ve.tensor_scalar(R26[:, 1, :], R26[:, 1, :], 100.0, None, ALU.add)
            ve.drain()
            ve.tensor_tensor(OHm, e_row, R26[:, 1, :].unsqueeze(2).to_broadcast([P, NT, EX]), ALU.is_equal)
            ve.drain()
            ve.tensor_tensor(OHm, OHm, valid[:, :].unsqueeze(2).to_broadcast([P, NT, EX]), ALU.mult).then_inc(sem("oh_m"), 1)
            ve.wait_ge(sem("gate_exp"), 1)
            ve.tensor_reduce(R26[:, 2, :], T8a, AX.X, ALU.add)
            ve.drain()
            ve.reciprocal(R26[:, 3, :], R26[:, 2, :])
            place_vector(ve, "m", OHm, EX, T8b, T8c, T8a)
            ve.tensor_tensor(T8b, T8a, OHm, ALU.mult)
            ve.drain()
            ve.tensor_reduce(R26[:, 4, :], T8b, AX.X, ALU.add)
            ve.drain()
            ve.tensor_scalar(R26[:, 5, :], R26[:, 4, :], float(CAP), None, ALU.is_lt)
            ve.drain()
            ve.tensor_tensor(R26[:, 5, :], R26[:, 5, :], valid[:, :], ALU.mult)
            ve.scalar_tensor_tensor(out=R26[:, 4, :], in0=R26[:, 1, :], scalar=float(CAPP), in1=R26[:, 4, :],
                                    op0=ALU.mult, op1=ALU.add)
            ve.drain()
            ve.tensor_tensor(gate_p[:, :], R26[:, 3, :], R26[:, 5, :], ALU.mult)
            ve.tensor_tensor(R26[:, 6, :], R26[:, 4, :], R26[:, 5, :], ALU.mult)
            ve.tensor_scalar(R26[:, 7, :], R26[:, 5, :], -FAR, FAR, ALU.mult, ALU.add)
            ve.drain()
            ve.tensor_copy(rowof_m[:, :], R26[:, 6, :])
            ve.tensor_tensor(R26[:, 7, :], R26[:, 7, :], R26[:, 6, :], ALU.add)
            ve.drain()
            ve.tensor_copy(slot_m[:, :], R26[:, 7, :]).then_inc(sem("slot_m"), 1)
            ve.drain()

        def route_pool(pool):
            pool.wait_ge(sem("slot_m"), 1)
            for t in range(25):
                pool.indirect_dma_start(moe_in, bass.IndirectOffsetOnAxis(ap=slot_m[:, t:t + 1].bitcast(U32), axis=0),
                                        XN[:, t, :], None, bounds_check=EX * CAPP - 1, oob_is_err=False
                                        ).then_inc(sem("moe_in"), 16)

        def experts_sync(sp):
            sp.wait_ge(sem("moe_in"), 16 * 25)
            w1 = A["L0_ffn_w1"].rearrange("e (k p) n -> p (e k) n", p=P)
            w2 = A["L0_ffn_w2"].rearrange("e (k p) n -> p (e k) n", p=P)
            xin = moe_in.rearrange("(b p) d -> p b d", p=P)
            yout = moe_out.rearrange("(b p) d -> p b d", p=P)

            def body(i, first):
                for s in range(2):
                    e = 2 * i + s
                    if not first:
                        sp.wait_ge(sem("ex_y"), 4 * (2 * i + s - 1))
                        sp.nop(nofuse=True)
                    sp.dma_start(XE[s], xin[:, ds(4 * e, 4), :]).then_inc(sem(f"ex_in{s}"), 16)
                    sp.dma_start(MW[s][0], w1[:, ds(2 * e, 2), :]).then_inc(sem(f"ex_in{s}"), 16)
                    sp.dma_start(MW[s][1], w2[:, ds(8 * e, 8), :]).then_inc(sem(f"ex_in{s}"), 16)
                for s in range(2):
                    e = 2 * i + s
                    sp.wait_ge(sem("ex_ys"), 4 * (e + 1))
                    sp.nop(nofuse=True)
                    sp.dma_start(yout[:, ds(4 * e, 4), :], YB).then_inc(sem("ex_out"), 16)

            run(sp, EX // 2, body)

        def experts_tensor(pe):
            def body(i, first):
                for s in range(2):
                    e = 2 * i + s
                    pe.wait_ge(sem(f"ex_in{s}"), 48 * (i + 1))
                    for k in range(2):
                        for t in range(4):
                            ins = pe.transpose(PS[k][:, t * P:(t + 1) * P], XE[s][:, t, k * P:(k + 1) * P], ident[:, :])
                        ins.then_inc(sem("ex_xt"), 1)
                    pe.wait_ge(sem("ex_xts"), e + 1)
                    pe.wait_ge(sem("ex_xts2"), e + 1)
                    for f in range(8):
                        if f >= 2 or s or not first:
                            pe.wait_ge(sem("ex_hs"), 8 * e + f - 1)
                        for k in range(2):
                            ins = pe.matmul(PS[2 + f % 2][:, :], MW[s][0][:, k, f * P:(f + 1) * P], XET[:, k, :],
                                            start=(k == 0), stop=(k == 1))
                        ins.then_inc(sem("ex_h"), 1)
                    pe.wait_ge(sem("ex_hs"), 8 * (e + 1))
                    if s or not first:
                        pe.wait_ge(sem("ex_ys"), 4 * e)
                    for t in range(4):
                        y = PS[4 + t][:, 0:D]
                        for f in range(8):
                            pe.matmul(y, HM[:, f, t * P:(t + 1) * P], MW[s][1][:, f, :], start=(f == 0), stop=False)
                        pe.matmul(y, ones[0:1, :], b2e[0:1, ds(e * D, D)], start=False, stop=True).then_inc(sem("ex_y"), 1)

            run(pe, EX // 2, body)

        def experts_scalar(act):
            act.wait_ge(sem("b1T_sb"), 1)

            def body(i, first):
                for s in range(2):
                    e = 2 * i + s
                    act.activation(b1s[s][:, :], b1T[:, ds(8 * e, 8)], ACT.Copy)
                    act.wait_ge(sem("ex_xt"), 2 * e + 1)
                    if s or not first:
                        act.wait_ge(sem("ex_h"), 8 * e)
                    act.activation(XET[:, 0, :], PS[0][:, :], ACT.Copy).then_inc(sem("ex_xts"), 1)
                    act.drain()
                    for f in range(8):
                        act.wait_ge(sem("ex_h"), 8 * e + f + 1)
                        if f == 0 and (s or not first):
                            act.wait_ge(sem("ex_y"), 4 * e)
                        act.activation(HM[:, f, :], PS[2 + f % 2][:, :], ACT.Relu, bias=b1s[s][:, f:f + 1]).then_inc(sem("ex_hs"), 1)

            run(act, EX // 2, body)

        def experts_vector(ve):
            def body(i, first):
                for s in range(2):
                    e = 2 * i + s
                    ve.wait_ge(sem("ex_xt"), 2 * e + 2)
                    if s or not first:
                        ve.wait_ge(sem("ex_h"), 8 * e)
                    ve.tensor_copy(XET[:, 1, :], PS[1][:, :]).then_inc(sem("ex_xts2"), 1)
                    if s or not first:
                        ve.wait_ge(sem("ex_out"), 16 * e)
                    for t in range(4):
                        ve.wait_ge(sem("ex_y"), 4 * e + t + 1)
                        ve.tensor_copy(YB[:, t, :], PS[4 + t][:, 0:D]).then_inc(sem("ex_ys"), 1)

            run(ve, EX // 2, body)

        YG = BIGR[:, 0:NT * D].rearrange("p (t d) -> p t d", d=D)
        OFF = ar(0, NT * D, dt=I32)
        TENK = ar(NT * D, 2)

        def expert_rows_pool(pool):
            pool.wait_ge(sem("ex_out"), 16 * EX)
            for t in range(NT):
                pool.indirect_dma_start(YG[:, t, :], None, moe_out,
                                        bass.IndirectOffsetOnAxis(ap=rowof_m[:, t:t + 1].bitcast(U32), axis=0)
                                        ).then_inc(sem("moe_rows"), 16)

        def expert_rows_vector(ve):
            ve.wait_ge(sem("ex_out"), 16 * EX)
            ve.memset(TENK[:, 0:1], 10000.0)
            ve.memset(TENK[:, 1:2], -10000.0)
            ve.wait_ge(sem("moe_rows"), 16 * NT)
            for t in range(NT):
                ve.tensor_scalar(YG[:, t, :], YG[:, t, :], gate_p[:, t:t + 1], None, ALU.mult)
            ve.drain()
            y = BIGR[:, 0:NT * D]
            for q, (op, lim) in enumerate(((ALU.is_gt, 3.4028234663852886e38), (ALU.is_lt, -3.4028234663852886e38))):
                ve.tensor_scalar(OFF, y, lim, None, op)
                ve.drain()
                ve.copy_predicated(y, OFF, TENK[:, q:q + 1].to_broadcast([P, NT * D]))
                ve.drain()
            ve.tensor_tensor(OFF, y, y, ALU.not_equal)
            ve.drain()
            ve.copy_predicated(y, OFF, valid[:, 25:26].to_broadcast([P, NT * D]))
            ve.drain()
            for t in range(25):
                ins = ve.tensor_tensor(X[:, t, :], X[:, t, :], YG[:, t, :], ALU.add)
            ins.then_inc(sem("x2"), 1)
            ve.drain()


        NTY = ar(6000, NT, dt=I32)
        NTF = ar(6040, NT)
        OHt, TOTt, INCt, EXCt = (ar(6100 + 500 * k, NT, T1) for k in range(4))
        TB = ar(8200, 8, T1)
        TBI = ar(8400, T1, dt=I32)
        TCM = ar(8500, TT, T1)
        TR = ar(9400, 3, NT)
        TTF = ar(9500, TT)

        def types_sync(sp):
            sp.wait_ge(sem("types_pad"), 1)
            nt = A["node_type_19"]
            sp.dma_start(NTY[:, 0:24], nt[0:24 * P].rearrange("(t p) -> p t", p=P)).then_inc(sem("types_in"), 16)
            sp.dma_start(NTY[0:TAIL, 24:25], nt[24 * P:N].rearrange("(p t) -> p t", t=1)).then_inc(sem("types_in"), 16)

        def types_vector(ve):
            t_row = iotaz[:, 0:T1]
            ve.memset(NTY[:, 24:26], 0).then_inc(sem("types_pad"), 1)
            ve.wait_ge(sem("types_in"), 32)
            ve.tensor_copy(NTF, NTY)
            ve.drain()
            ve.tensor_tensor(OHt, t_row.unsqueeze(1).to_broadcast([P, NT, T1]), NTF.unsqueeze(2).to_broadcast([P, NT, T1]), ALU.is_equal)
            ve.drain()
            ve.tensor_tensor(OHt, OHt, valid[:, :].unsqueeze(2).to_broadcast([P, NT, T1]), ALU.mult).then_inc(sem("oh_t"), 1)
            place_vector(ve, "t", OHt, T1, TOTt, INCt, EXCt)
            ve.tensor_scalar(TBI, INCt[:, NT - 1, :], 127.0, None, ALU.add)
            ve.drain()
            ve.tensor_scalar(TBI, TBI, 7, None, ALU.arith_shift_right)
            ve.drain()
            ve.tensor_copy(TB[:, 0, :], TBI)
            ve.drain()
            ve.tensor_tensor_scan(TB[:, 1, :], ones[:, 0:T1], TB[:, 0, :], 0.0, ALU.mult, ALU.add)
            ve.drain()
            ve.tensor_tensor(TB[:, 2, :], TB[:, 1, :], TB[:, 0, :], ALU.subtract)
            ve.drain()
            ve.tensor_scalar(TB[:, 2, :], TB[:, 2, :], 128.0, None, ALU.mult)
            ve.drain()
            ve.tensor_tensor(EXCt, EXCt, TB[:, 2, :].unsqueeze(1).to_broadcast([P, NT, T1]), ALU.add)
            ve.drain()
            ve.tensor_tensor(EXCt, EXCt, OHt, ALU.mult)
            ve.drain()
            ve.tensor_reduce(TR[:, 0, :], EXCt, AX.X, ALU.add)
            ve.tensor_scalar(TR[:, 1, :], valid[:, :], -FAR, FAR, ALU.mult, ALU.add)
            ve.drain()
            ve.tensor_tensor(TR[:, 1, :], TR[:, 1, :], TR[:, 0, :], ALU.add)
            ve.tensor_copy(rowof_t[:, :], TR[:, 0, :])
            ve.tensor_tensor(TCM[0:1], TB[0:1, 1, :].unsqueeze(1).to_broadcast([1, TT, T1]),
                             iotaz[0:1, 0:TT].unsqueeze(2).to_broadcast([1, TT, T1]), ALU.is_le)
            ve.drain()
            ve.tensor_copy(slot_t[:, :], TR[:, 1, :])
            ve.tensor_reduce(TTF[0:1], TCM[0:1], AX.X, ALU.add)
            ve.drain()
            ve.tensor_scalar(ttype[:, :], TTF[0:1], float(T1 - 1), None, ALU.min
                             ).then_inc(sem("slot_t"), 1)
            ve.drain()

        def types_pool(pool):
            pool.wait_ge(sem("slot_t"), 1)
            pool.wait_ge(sem("xn"), 3 * NT)
            for t in range(25):
                pool.indirect_dma_start(typ_x, bass.IndirectOffsetOnAxis(ap=slot_t[:, t:t + 1].bitcast(U32), axis=0),
                                        XN[:, t, :], None, bounds_check=TT * P - 1, oob_is_err=False
                                        ).then_inc(sem("typ_x"), 16)

        NTY2 = TT // 2
        TW = [ar(1152 * s, 2, 3 * PROJ) for s in range(2)]
        TBR = [ar(2304 + 576 * s, 3 * PROJ) for s in range(2)]
        TX = [ar(3456 + 256 * s, D) for s in range(2)]
        TXT = [ar(3968 + 256 * s, 2, P) for s in range(2)]
        TROW = [ar(4480 + 440 * s, KV + DK) for s in range(2)]

        def kvq_sync(sp):
            sp.wait_ge(sem("typ_x"), 16 * 25)
            sp.wait_ge(sem("x2"), 1)
            ws = [A["L1_gnn_W" + c].rearrange("t (k p) n -> p (t k) n", p=P) for c in "kvq"]
            bs = [A["L1_gnn_b" + c] for c in "kvq"]
            xin = typ_x.rearrange("(b p) d -> b p d", p=P)

            def body(i, first):
                for s in range(2):
                    it = 2 * i + s
                    ty = loads_of(sp, ttype[0:1, ds(it, 1)], T1 - 1, ET.SP)[0]
                    if not first:
                        sp.wait_ge(sem("kvq_mm"), 2 * i + s - 1)
                        sp.nop(nofuse=True)
                    for c in range(3):
                        sp.dma_start(TW[s][:, :, c * PROJ:(c + 1) * PROJ], ws[c][:, ds(ty * 2, 2), :]).then_inc(sem(f"kvq_in{s}"), 16)
                        sp.dma_start(TBR[s][0:1, c * PROJ:(c + 1) * PROJ], bs[c][ds(ty, 1), :]).then_inc(sem(f"kvq_in{s}"), 16)
                    sp.dma_start(TX[s], xin[ds(it, 1), :, :].rearrange("b p d -> (b p) d")).then_inc(sem(f"kvq_in{s}"), 16)

            run(sp, NTY2, body)

        def kvq_tensor(pe):
            def body(i, first):
                for s in range(2):
                    pe.wait_ge(sem(f"kvq_in{s}"), 112 * (i + 1))
                    if not first:
                        pe.wait_ge(sem("kvq_xt"), 2 * i + s - 1)
                    for k in range(2):
                        ins = pe.transpose(PS[s][:, k * P:(k + 1) * P], TX[s][:, k * P:(k + 1) * P], ident[:, :])
                    ins.then_inc(sem("kvq_tp"), 1)
                for s in range(2):
                    pe.wait_ge(sem("kvq_xt"), 2 * i + s + 1)
                    if not first:
                        pe.wait_ge(sem("kvq_row"), 2 * (2 * i + s - 1))
                    kv, q = PS[2 + s][:, 0:KV], PS[4 + s]
                    for k in range(2):
                        pe.matmul(kv, TXT[s][:, k, :], TW[s][:, k, 0:KV], start=(k == 0), stop=False)
                    pe.matmul(kv, ones[0:1, :], TBR[s][0:1, 0:KV], start=False, stop=True)
                    for h in range(4):
                        wd = DK if h < 3 else PROJ - 3 * DK
                        c0 = KV + h * DK
                        for k in range(2):
                            pe.matmul(q[:, 0:wd], TXT[s][:, k, :], TW[s][:, k, c0:c0 + wd], start=(h == 0 and k == 0), stop=False,
                                      skip_group_check=True)
                        ins = pe.matmul(q[:, 0:wd], ones[0:1, :], TBR[s][0:1, c0:c0 + wd], start=False, stop=(h == 3),
                                        skip_group_check=True)
                    ins.then_inc(sem("kvq_mm"), 1)

            run(pe, NTY2, body)

        def kvq_scalar(act):
            rows = typ_kvq.rearrange("(b p) d -> b p d", p=P)

            def body(i, first):
                for s in range(2):
                    act.wait_ge(sem("kvq_tp"), 2 * i + s + 1)
                    if not first:
                        act.wait_ge(sem("kvq_mm"), 2 * i + s - 1)
                    act.activation(TXT[s].rearrange("p k n -> p (k n)"), PS[s][:, 0:D], ACT.Copy).then_inc(sem("kvq_xt"), 1)
                for s in range(2):
                    it = 2 * i + s
                    act.wait_ge(sem("kvq_mm"), 2 * i + s + 1)
                    if not first:
                        act.wait_ge(sem(f"kvq_out{s}"), 16 * i)
                    act.activation(TROW[s][:, 0:KV], PS[2 + s][:, 0:KV], ACT.Copy).then_inc(sem("kvq_row"), 1)
                    act.activation(TROW[s][:, KV:], PS[4 + s][:, 0:DK], ACT.Copy).then_inc(sem("kvq_row"), 1)
                    act.wait_ge(sem("kvq_row"), 2 * (2 * i + s + 1))
                    act.dma_start(rows[ds(it, 1), :, :].rearrange("b p d -> (b p) d"), TROW[s]).then_inc(sem(f"kvq_out{s}"), 16)

            run(act, NTY2, body)

        KVG = BIGR[:, 0:NT * (KV + DK)].rearrange("p (t d) -> p t d", d=KV + DK)

        def kvq_rows_pool(pool):
            for s in range(2):
                pool.wait_ge(sem(f"kvq_out{s}"), 16 * NTY2)
            for t in range(NT):
                pool.indirect_dma_start(KVG[:, t, :], None, typ_kvq,
                                        bass.IndirectOffsetOnAxis(ap=rowof_t[:, t:t + 1].bitcast(U32), axis=0)
                                        ).then_inc(sem("kvg"), 16)

        def kvq_rows_sync(sp):
            sp.wait_ge(sem("kvg"), 16 * NT)
            kv = kv_tab.rearrange("(t p) d -> p t d", p=P)
            for half in range(2):
                sp.dma_start(kv[:, :, (1 - half) * PROJ:(2 - half) * PROJ], KVG[:, :, half * PROJ:(half + 1) * PROJ]
                             ).then_inc(sem("kv_tab"), 16)

        def kvq_rows_vector(ve):
            ve.wait_ge(sem("kvg"), 16 * NT)
            ve.tensor_copy(QS[:, :, :], KVG[:, :, KV:])
            ve.drain()

        KVR = [ar(U * ROW * s, U, ROW) for s in range(SL)]
        OH = [ar(7680 + 512 * s, U, P) for s in range(SL)]
        OT = [ar(9728 + 512 * s, U, P) for s in range(2)]
        NEG = [ar(14092 + 256 * s, U, P, dt=BF16) for s in range(SL)]
        LO = [ar(10752 + 16 * s, U) for s in range(SL)]
        DIST = ar(10816, U, P)
        PRD = ar(11330, U, H1 * DK)
        ATS = [ar(12226 + 16 * s, U * H1) for s in range(2)]
        BM = [ar(12258 + 16 * s, U * H1) for s in range(2)]
        ARG = [ar(12290 + 16 * s, U * H1) for s in range(2)]
        RCP = ar(12322, NT, H1)
        ATT = ar(12428, NB, H1)
        VB = [ar(U * SROW * s, U, SROW) for s in range(SL)]

        def score_sync(sp, o):
            rec = rec_tab[o].rearrange("(b p) c -> p b c", p=P)
            vt = v_tab[o].rearrange("(b p) c -> p b c", p=P)
            if o:
                sp.wait_ge(sem("sum"), U * NG)
                sp.nop(nofuse=True)

            def load(i, s):
                g = o * NG + SL * i + s
                if later(i):
                    sp.wait_ge(sem("prod"), g - SL + 1)
                    sp.nop(nofuse=True)
                    sp.wait_ge(sem(f"v_out{s}"), 16 * (o * (NG // SL) + i))
                    sp.nop(nofuse=True)
                sp.dma_start(KVR[s][:, :, KV:ROW], rec[:, ds((SL * i + s) * U, U), 0:3 * TD]).then_inc(sem(f"edges{s}"), 16)

            def store(i, s):
                sp.wait_ge(sem(f"rows{s}"), ROWS0 + 64 * (o * (NG // SL) + i + 1))
                sp.nop(nofuse=True)
                sp.dma_start(vt[:, ds((SL * i + s) * U, U), :], KVR[s][:, :, 0:PROJ]).then_inc(sem(f"v_out{s}"), 16)

            pipe(sp, [(0, store), (3, load)])

        ROWS0 = 64 * (NG // SL)

        def score_pool(pool, o):
            pool.wait_ge(sem("kv_tab"), 32)
            if o:
                pool.wait_ge(sem("sum"), U * NG)

            def gather(i, s):
                g = o * NG + SL * i + s
                if later(i):
                    pool.wait_ge(sem("prod"), g - SL + 1)
                    pool.wait_ge(sem(f"v_out{s}"), 16 * (o * (NG // SL) + i))
                pool.tensor_copy(IST[s][:, :], META[o][:, ds((SL * i + s) * U, U), 0].bitcast(I32)).then_inc(sem("ist"), 1)
                pool.wait_ge(sem("ist"), NG + g + 1)
                pool.nop(nofuse=True)
                for u in range(U):
                    pool.indirect_dma_start(KVR[s][:, u, 0:KV], None, kv_tab,
                                            bass.IndirectOffsetOnAxis(ap=IST[s][:, u:u + 1].bitcast(U32), axis=0)
                                            ).then_inc(sem(f"rows{s}"), 16)

            pipe(pool, [(0, gather)])

        def onehots(act, o, i, s, done):
            act.activation(LO[s], META[o][:, ds((SL * i + s) * U, U), 1], ACT.Copy)
            act.drain()
            for u in range(U):
                act.activation(DIST[:, u, :], iota1[:, :], ACT.Abs, scale=-1.0, bias=LO[s][:, u:u + 1])
            act.drain()
            act.activation(OH[s].rearrange("p u n -> p (u n)"), DIST.rearrange("p u n -> p (u n)"), ACT.Relu,
                           scale=-1.0, bias=1.0).then_inc(sem(done), 1)

        def score_vector(ve, o):
            ve.wait_ge(sem("kv_tab"), 32)
            ve.memset(BIGR[:, 0:NT * SROW], 0.0)
            ve.memset(M[:, :, :], -1.0e30)
            ve.drain()
            ve.tensor_copy(RCP[:, 0, :], iotaz[:, 0:H1]).then_inc(sem("pass_set"), 1)

            def products(i, s):
                g = o * NG + SL * i + s
                b = (SL * i + s) * U
                ve.wait_ge(sem("q"), g + 1)
                ve.wait_ge(sem(f"rows{s}"), ROWS0 + 64 * (o * (NG // SL) + i + 1))
                ve.wait_ge(sem(f"edges{s}"), 16 * (3 * o * (NG // SL) + i + 1))
                q = PS[2 + s % 2][:, 0:U * 64].rearrange("p (u c) -> p u c", c=64)
                if isinstance(i, int):
                    ve.drain()
                ve.tensor_tensor(PRD.rearrange("p u (h d) -> p u h d", d=DK),
                                 KVR[s][:, :, PROJ:KV + TD].rearrange("p u (h d) -> p u h d", d=DK),
                                 q[:, :, 0:DK].unsqueeze(2).to_broadcast([P, U, H1, DK]), ALU.mult).then_inc(sem("prod"), 1)
                ve.drain()
                if later(i) or s >= 2:
                    ve.wait_ge(sem("bm"), U * (g - 1))
                ve.tensor_reduce(ATS[s % 2], PRD.rearrange("p u (h d) -> p (u h) d", d=DK), AX.X, ALU.add).then_inc(sem("att"), 1)

            def maxima(i, s):
                g = o * NG + SL * i + s
                b = (SL * i + s) * U
                ws = loads_of(ve, win[o][0:1, ds(b, U)], W - 1, ET.DVE)
                ve.tensor_copy(ATT[:, ds(b, U), :].rearrange("p u h -> p (u h)"), ATS[s % 2])
                bm = BM[s % 2]
                for u in range(U):
                    ve.wait_ge(sem("bm"), U * g + u + 1)
                    ve.tensor_reduce(bm[:, u * H1:(u + 1) * H1], PS[4 + u][:, :].rearrange("p (h e) -> p h e", e=P),
                                     AX.X, ALU.max).then_inc(sem("bmr"), 1)
                for u in range(U):
                    ve.drain()
                    m = M[:, ds(ws[u], 1), :].rearrange("p t h -> p (t h)")
                    ve.tensor_tensor(m, m, bm[:, u * H1:(u + 1) * H1], ALU.max)

            pipe(ve, [(1, products), (0, maxima)])
            ve.drain()
            ve.tensor_copy(RCP[:, 0, :], iotaz[:, 0:H1]).then_inc(sem("pass_set"), 1)

        def transposes(pe, s):
            for u in range(U):
                ins = pe.transpose(PS[s % 2][:, u * P:(u + 1) * P], OH[s][:, u, :], ident[:, :])
            return ins

        def score_tensor(pe, o):
            def turn(i, s):
                g = o * NG + SL * i + s
                pe.wait_ge(sem("oh"), g + 1)
                if later(i) or s >= 2:
                    pe.wait_ge(sem("ot"), 2 * (g - 1))
                transposes(pe, s).then_inc(sem("ohT"), 1)

            def queries(i, s):
                g = o * NG + SL * i + s
                ws = loads_of(pe, win[o][0:1, ds((SL * i + s) * U, U)], W - 1, ET.PE)
                pe.wait_ge(sem("ot"), 2 * (g + 1))
                pe.wait_ge(sem(f"edges{s}"), 16 * (3 * o * (NG // SL) + i + 1))
                if later(i) or s >= 2:
                    pe.wait_ge(sem("prod"), g - 1)
                for u in range(U):
                    q = PS[2 + s % 2][:, u * 64:u * 64 + DK]
                    pe.matmul(q, OT[s % 2][:, u, :], QS[:, ds(ws[u], 1), :].rearrange("p t d -> p (t d)"), start=True, stop=False,
                              skip_group_check=True)
                    ins = pe.matmul(PS[2 + s % 2][:, u * 64 + DK - TD:u * 64 + DK], ident[:, :], KVR[s][:, u, KV + 2 * TD:ROW],
                                    start=False, stop=True, skip_group_check=True)
                ins.then_inc(sem("q"), 1)

            def spread(i, s):
                g = o * NG + SL * i + s
                pe.wait_ge(sem("att"), g + 1)
                for u in range(U):
                    if later(i) or s:
                        pe.wait_ge(sem("bmr"), U * g + u - U + 1)
                    pe.matmul(PS[4 + u][:, :], identb[:, :], NEG[s][:, u, :].unsqueeze(1).to_broadcast([P, H1, P]),
                              start=True, stop=False, skip_group_check=True)
                    for h in range(H1):
                        ins = pe.matmul(PS[4 + u][:, h * P:(h + 1) * P], ATS[s % 2][:, u * H1 + h:u * H1 + h + 1].to_broadcast([P, P]),
                                        ident[:, :], start=False, stop=(h == 3), skip_group_check=True)
                    ins.then_inc(sem("bm"), 1)

            pipe(pe, [(2, queries), (3, turn), (0, spread)])

        def score_scalar(act, o):
            def onehot(i, s):
                if later(i):
                    act.wait_ge(sem("ohT"), o * NG + SL * i + s - SL + 1)
                onehots(act, o, i, s, "oh")

            def copies(i, s):
                g = o * NG + SL * i + s
                act.wait_ge(sem("ohT"), g + 1)
                if later(i) or s >= 2:
                    act.wait_ge(sem("q"), g - 1)
                act.activation(OT[s % 2].rearrange("p u n -> p (u n)"), PS[s % 2][:, :], ACT.Copy).then_inc(sem("ot"), 1)
                if later(i):
                    act.wait_ge(sem("bm"), U * (g - SL + 1))
                act.activation(NEG[s].rearrange("p u n -> p (u n)"), PS[s % 2][:, :], ACT.Copy, scale=BIG, bias=-BIG).then_inc(sem("ot"), 1)

            act.wait_ge(sem("pass_set"), 2 * o + 1)
            pipe(act, [(0, copies), (1, onehot)])

        def sum_sync(sp, o):
            for s in range(SL):
                sp.wait_ge(sem(f"v_out{s}"), 16 * (NG // SL) * (o + 1))
            sp.wait_ge(sem("prod"), NG * (o + 1))
            sp.nop(nofuse=True)
            rec = rec_tab[o].rearrange("(b p) c -> p b c", p=P)
            vt = v_tab[o].rearrange("(b p) c -> p b c", p=P)

            def load(i, s):
                if later(i):
                    sp.wait_ge(sem("sum"), U * (o * NG + SL * i + s - SL + 1))
                    sp.nop(nofuse=True)
                sp.dma_start(VB[s][:, :, 0:PROJ], vt[:, ds((SL * i + s) * U, U), :]).then_inc(sem(f"edges{s}"), 16)
                sp.dma_start(VB[s][:, :, PROJ:D], rec[:, ds((SL * i + s) * U, U), 0:2 * TD]).then_inc(sem(f"edges{s}"), 16)

            pipe(sp, [(0, load)])

        def sum_vector(ve, o):
            def onehot(i, s):
                if later(i):
                    ve.wait_ge(sem("sum"), U * (o * NG + SL * i + s - SL + 1))
                ve.tensor_copy(MST[s][:, :, :], META[o][:, ds((SL * i + s) * U, U), :])
                ve.drain()
                for u in range(U):
                    ins = ve.tensor_scalar(OH[s][:, u, :], iota1[:, :], MST[s][:, u, 1:2], None, ALU.is_equal)
                ins.then_inc(sem("oh2"), 1)

            def argument(i, s):
                g = o * NG + SL * i + s
                ve.wait_ge(sem("m"), g + 1)
                if later(i) or s >= 2:
                    ve.wait_ge(sem("exp"), g - 1)
                ve.tensor_tensor(ARG[s % 2], ATT[:, ds((SL * i + s) * U, U), :].rearrange("p u h -> p (u h)"),
                                 PS[2 + s % 2][:, 0:U * H1], ALU.subtract).then_inc(sem("arg"), 1)

            def weigh(i, s):
                ve.wait_ge(sem("exp"), o * NG + SL * i + s + 1)
                for u in range(U):
                    v = VB[s][:, u, 0:H1 * DK].rearrange("p (h d) -> p h d", d=DK)
                    ins = ve.tensor_tensor(v, v, VB[s][:, u, D:SROW].unsqueeze(2).to_broadcast([P, H1, DK]), ALU.mult)
                ins.then_inc(sem("pv"), 1)

            def add(i, s):
                ws = loads_of(ve, win[o][0:1, ds((SL * i + s) * U, U)], W - 1, ET.DVE)
                for u in range(U):
                    ve.wait_ge(sem("sum"), U * (o * NG + SL * i + s) + u + 1)
                    a = ACC[:, ds(ws[u], 1), :].rearrange("p t d -> p (t d)")
                    ve.tensor_tensor(a, a, PS[4 + u][:, 0:SROW], ALU.add).then_inc(sem("add"), 1)
                    ve.drain()

            pipe(ve, [(1, weigh), (0, add), (2, argument), (4, onehot)])
            ve.tensor_scalar(RCP, ACC[:, :, D:SROW], 1.0e-16, None, ALU.add)
            ve.drain()
            ve.reciprocal(RCP, RCP)
            ve.drain()
            for h in range(H1):
                a = ACC[:, :, h * DK:(h + 1) * DK]
                ve.tensor_tensor(a, a, RCP[:, :, h].unsqueeze(2).to_broadcast([P, NT, DK]), ALU.mult)
            ve.drain()
            if o == 0:
                ve.tensor_copy(AGG, ACC[:, :, 0:D])
            else:
                ve.tensor_tensor(AGG, AGG, ACC[:, :, 0:D], ALU.add).then_inc(sem("agg"), 1)
            ve.drain()

        def sum_tensor(pe, o):
            pe.wait_ge(sem("pass_set"), 2 * o + 2)

            def turn(i, s):
                g = o * NG + SL * i + s
                pe.wait_ge(sem("oh2"), g + 1)
                if later(i) or s >= 2:
                    pe.wait_ge(sem("ot2"), g - 1)
                transposes(pe, s).then_inc(sem("oh2T"), 1)

            def lookup(i, s):
                g = o * NG + SL * i + s
                ws = loads_of(pe, win[o][0:1, ds((SL * i + s) * U, U)], W - 1, ET.PE)
                pe.wait_ge(sem("ot2"), g + 1)
                if later(i) or s >= 2:
                    pe.wait_ge(sem("arg"), g - 1)
                for u in range(U):
                    ins = pe.matmul(PS[2 + s % 2][:, u * H1:(u + 1) * H1], OT[s % 2][:, u, :],
                                    M[:, ds(ws[u], 1), :].rearrange("p t h -> p (t h)"), start=True, stop=True,
                                    skip_group_check=True)
                ins.then_inc(sem("m"), 1)

            def sums(i, s):
                g = o * NG + SL * i + s
                pe.wait_ge(sem("pv"), g + 1)
                for u in range(U):
                    if later(i) or s:
                        pe.wait_ge(sem("add"), U * g + u - U + 1)
                    pe.matmul(PS[4 + u][:, 0:SROW], OH[s][:, u, :], VB[s][:, u, :], start=True, stop=True).then_inc(sem("sum"), 1)

            pipe(pe, [(0, sums), (2, lookup), (3, turn)])

        def sum_scalar(act, o):
            def copies(i, s):
                g = o * NG + SL * i + s
                act.wait_ge(sem("oh2T"), g + 1)
                if later(i) or s >= 2:
                    act.wait_ge(sem("m"), g - 1)
                act.activation(OT[s % 2].rearrange("p u n -> p (u n)"), PS[s % 2][:, :], ACT.Copy).then_inc(sem("ot2"), 1)

            def exponentials(i, s):
                g = o * NG + SL * i + s
                act.wait_ge(sem("arg"), g + 1)
                act.wait_ge(sem(f"edges{s}"), 16 * ((3 * o + 1) * (NG // SL) + 2 * (i + 1)))
                act.activation(VB[s][:, :, D:SROW], ARG[s % 2].rearrange("p (u h) -> p u h", h=H1), ACT.Exp,
                               scale=float(DK) ** -0.5).then_inc(sem("exp"), 1)

            act.wait_ge(sem("pass_set"), 2 * o + 2)
            pipe(act, [(1, copies), (0, exponentials)])


        WA = [ar(1024 * s, 4, D) for s in range(2)]
        WS = [ar(2048 + 512 * s, 2, D) for s in range(2)]
        AX2 = [ar(3072 + 512 * s, 2, D) for s in range(2)]
        AT2 = [ar(4096 + 256 * s, 2, P) for s in range(2)]
        ROWS3 = [ar(4608 + 768 * s, 3 * D) for s in range(2)]
        YT = [ar(6144 + 256 * s, D) for s in range(2)]
        YST = [sb(f"yst{s}", [P, 6]) for s in range(2)]
        YMV = [sb(f"ymv{s}", [P, 2]) for s in range(2)]
        YRS = [sb(f"yrs{s}", [P, 4, 1]) for s in range(2)]

        def agg_pool(pool):
            pool.wait_ge(sem("agg"), 1)
            for t in range(25):
                pool.indirect_dma_start(typ_agg, bass.IndirectOffsetOnAxis(ap=slot_t[:, t:t + 1].bitcast(U32), axis=0),
                                        AGG[:, t, :], None, bounds_check=TT * P - 1, oob_is_err=False
                                        ).then_inc(sem("typ_agg"), 16)

        def proj_sync(sp):
            sp.wait_ge(sem("typ_agg"), 16 * 25)
            wa = A["L1_gnn_Wa"].rearrange("t (k p) n -> p (t k) n", p=P)
            ain = typ_agg.rearrange("(b p) d -> b p d", p=P)
            xin = typ_x.rearrange("(b p) d -> b p d", p=P)
            yout = typ_y.rearrange("(b p) d -> b p d", p=P)

            def body(i, first):
                for s in range(2):
                    it = 2 * i + s
                    ty = loads_of(sp, ttype[0:1, ds(it, 1)], T1 - 1, ET.SP)[0]
                    if not first:
                        sp.wait_ge(sem(f"pj_out{s}"), 16 * i)
                        sp.nop(nofuse=True)
                    sp.dma_start(WA[s], wa[:, ds(ty * 4, 4), :]).then_inc(sem(f"pj_in{s}"), 16)
                    for c, name in enumerate(("L1_gnn_ba", "L1_gnn_gamma", "L1_gnn_beta")):
                        sp.dma_start(ROWS3[s][0:1, c * D:(c + 1) * D], A[name][ds(ty, 1), :]).then_inc(sem(f"pj_in{s}"), 16)
                    for c, src in enumerate((ain, xin)):
                        sp.dma_start(AX2[s][:, c, :], src[ds(it, 1), :, :].rearrange("b p d -> (b p) d")).then_inc(sem(f"pj_in{s}"), 16)
                for s in range(2):
                    it = 2 * i + s
                    sp.wait_ge(sem("pj_y"), 2 * i + s + 1)
                    sp.nop(nofuse=True)
                    sp.dma_start(yout[ds(it, 1), :, :].rearrange("b p d -> (b p) d"), YT[s]).then_inc(sem(f"pj_out{s}"), 16)

            run(sp, NTY2, body)

        def proj_tensor(pe):
            def body(i, first):
                for s in range(2):
                    pe.wait_ge(sem(f"pj_in{s}"), 96 * (i + 1))
                    if not first:
                        pe.wait_ge(sem("pj_y"), 2 * i + s - 1)
                    for k in range(2):
                        ins = pe.transpose(PS[s][:, k * P:(k + 1) * P], AX2[s][:, 0, k * P:(k + 1) * P], ident[:, :])
                    ins.then_inc(sem("pj_t"), 1)
                    pe.matmul(PS[4 + s][:, :], ones[0:1, :], ROWS3[s][0:1, D:3 * D], start=True, stop=True).then_inc(sem("pj_gb"), 1)
                for s in range(2):
                    pe.wait_ge(sem("pj_ts"), 2 * i + s + 1)
                    pe.wait_ge(sem("pj_ws"), 2 * i + s + 1)
                    y = PS[2 + s][:, 0:D]
                    for k in range(2):
                        pe.matmul(y, AT2[s][:, k, :], WS[s][:, k, :], start=(k == 0), stop=False)
                    pe.matmul(y, ones[0:1, :], ROWS3[s][0:1, 0:D], start=False, stop=True).then_inc(sem("pj_mm"), 1)

            run(pe, NTY2, body)

        def proj_scalar(act):
            def body(i, first):
                for s in range(2):
                    act.wait_ge(sem("pj_t"), 2 * i + s + 1)
                    if not first:
                        act.wait_ge(sem("pj_mm"), 2 * i + s - 1)
                    act.activation(AT2[s].rearrange("p k n -> p (k n)"), PS[s][:, 0:D], ACT.Copy).then_inc(sem("pj_ts"), 1)
                for s in range(2):
                    act.wait_ge(sem("pj_v"), 2 * i + s + 1)
                    act.activation(YRS[s][:, 1, :], YRS[s][:, 0, :], ACT.Sqrt).then_inc(sem("pj_sd"), 1)

            run(act, NTY2, body)

        def proj_vector(ve):
            def body(i, first):
                for s in range(2):
                    ve.wait_ge(sem(f"pj_in{s}"), 96 * (i + 1))
                    if not first:
                        ve.wait_ge(sem("pj_mm"), 2 * i + s - 1)
                    ve.tensor_tensor(WS[s], WA[s][:, 0:2, :], WA[s][:, 2:4, :], ALU.add).then_inc(sem("pj_ws"), 1)
                for s in range(2):
                    ve.wait_ge(sem("pj_mm"), 2 * i + s + 1)
                    if not first:
                        ve.wait_ge(sem(f"pj_out{s}"), 16 * i)
                    ve.tensor_tensor(YT[s], PS[2 + s][:, 0:D], AX2[s][:, 1, :], ALU.add)
                    ve.drain()
                    ve.bn_stats(YST[s][:, :], YT[s])
                    ve.drain()
                    ve.bn_aggr(YMV[s][:, :], YST[s][:, :])
                    ve.drain()
                    ve.tensor_scalar(YRS[s][:, 0, :], YMV[s][:, 1:2], LN_EPS, None, ALU.add).then_inc(sem("pj_v"), 1)
                for s in range(2):
                    ve.wait_ge(sem("pj_sd"), 2 * i + s + 1)
                    newton(ve, YRS[s], slice(0, 1))
                    ve.tensor_scalar(YT[s], YT[s], YMV[s][:, 0:1], YRS[s][:, 3, :], ALU.subtract, ALU.mult)
                    ve.drain()
                    ve.wait_ge(sem("pj_gb"), 2 * i + s + 1)
                    ve.tensor_tensor(YT[s], YT[s], PS[4 + s][:, 0:D], ALU.mult)
                    ve.drain()
                    ve.tensor_tensor(YT[s], YT[s], PS[4 + s][:, D:2 * D], ALU.add).then_inc(sem("pj_y"), 1)

            run(ve, NTY2, body)
            ve.drain()

        def proj_rows_pool(pool):
            for s in range(2):
                pool.wait_ge(sem(f"pj_out{s}"), 16 * NTY2)
            pool.wait_ge(sem("typ_agg"), 16 * 25)
            for t in range(25):
                pool.indirect_dma_start(YG[:, t, :], None, typ_y,
                                        bass.IndirectOffsetOnAxis(ap=rowof_t[:, t:t + 1].bitcast(U32), axis=0)
                                        ).then_inc(sem("y_rows"), 16)

        def proj_rows_vector(ve):
            ve.wait_ge(sem("y_rows"), 16 * 25)
            for t in range(25):
                ins = ve.tensor_tensor(X[:, t, :], X[:, t, :], YG[:, t, :], ALU.add)
            ins.then_inc(sem("x3"), 1)
            ve.drain()

        HP = H2 // 2
        SWT = BIGR[:, 0:HP * NT * P].rearrange("p (t h n) -> p t h n", h=HP, n=P)
        WFX = ar(0, 2, H2 * G)
        WL = ar(1024, 2, H2 * G)
        WXT = ar(2048, HP, D)
        WOUT = ar(3072, HP, D)
        WX = ar(4096, 2, H2 * G)
        BDS = ar(5120, 4, P)
        BDM = ar(5632, P)
        RBF = ar(5760, H2 * G)
        RBL = ar(6272, H2 * G)
        RBS = ar(6784, P)
        RBO = ar(6912, D)
        BXC = ar(7168, HP)
        TMP = ar(7172, 2, H2)
        FX = [ar(7200 + 520 * s, H2, G + 1) for s in range(2)]
        SW = [ar(8240 + 512 * s, H2, G) for s in range(2)]
        XT4 = [ar(9264 + 256 * s, 2, P) for s in range(2)]
        SM = [ar(9776 + 24 * s, 3, H2) for s in range(2)]
        TOK = ar(9830, P)
        TOKT, QT, KT, VV, PP, PPT, OTT = (ar(9960 + 128 * k, P) for k in range(7))
        SA = ar(10860, 8)
        MO = ar(10880, HP, D)
        ZC = ar(11910, P + 2)
        OB = [ar(12050 + 256 * s, D) for s in range(2)]
        b1row = ar(12600, 1)

        def slice_sync(sp):
            sp.wait_ge(sem("x3"), 1)
            sp.wait_ge(sem("bd_zero"), 1)

            def ld(dst, src):
                sp.dma_start(dst, src).then_inc(sem("sl_in"), 16)

            ld(WFX, A["L1_ffn_W_fx"].rearrange("(k p) n -> p k n", p=P))
            ld(WX, A["L1_ffn_W_x"].rearrange("(k p) n -> p k n", p=P))
            ld(WOUT, A["L1_ffn_W_out"].rearrange("(k p) n -> p k n", p=P))
            for c, name in enumerate(("slice", "q", "k", "v")):
                for h in range(2):
                    ld(BDS[h * G:(h + 1) * G, c, h * G:(h + 1) * G], A["L1_ffn_W_" + name])
            ld(RBF[0:1, :], A["L1_ffn_b_fx"].rearrange("(a n) -> a n", a=1))
            ld(RBO[0:1, :], A["L1_ffn_b_out"].rearrange("(a n) -> a n", a=1))
            for h in range(2):
                ld(RBS[0:1, h * G:(h + 1) * G], A["L1_ffn_b_slice"].rearrange("(a n) -> a n", a=1))
            ld(BXC, A["L1_ffn_b_x"].rearrange("(k p) -> p k", p=P))
            ld(TMP[:, 0, :], A["L1_ffn_temperature"].rearrange("a h b c -> (a b c) h").to_broadcast([P, H2]))

        N_SL = 16 * 17

        def slice_prep_vector(ve):
            ve.memset(BDS, 0.0)
            ve.memset(BDM, 0.0)
            ve.memset(ZC, 0.0)
            for s in range(2):
                ve.memset(FX[s], 1.0)
            ve.drain()
            ve.memset(BDM[0:G, 0:G], 1.0)
            ve.memset(BDM[G:P, G:P], 1.0).then_inc(sem("bd_zero"), 1)
            ve.wait_ge(sem("sl_in"), N_SL)
            ve.tensor_scalar(TMP[:, 1, :], TMP[:, 0, :], 0.1, 5.0, ALU.max, ALU.min)
            ve.drain()
            ve.reciprocal(TMP[:, 1, :], TMP[:, 1, :])
            ve.drain()
            tmp = TMP[:, 1, :].unsqueeze(2).to_broadcast([P, H2, G])
            ve.wait_ge(sem("wxt_ps"), 1)
            for k in range(2):
                ve.tensor_copy(WXT[:, :, k * P:(k + 1) * P], PS[k][:, :].rearrange("p (h n) -> p h n", n=P))
            ve.drain()
            ve.tensor_scalar(WXT[0:1, 0, 0:1], WXT[0:1, 0, 0:1], 1.0, None, ALU.mult).then_inc(sem("wxt"), 1)
            ve.wait_ge(sem("wl_ps"), 1)
            for k in range(2):
                ve.tensor_tensor(WL[:, k, :].rearrange("p (h g) -> p h g", g=G), PS[2 + k][:, :].rearrange("p (h g) -> p h g", g=G), tmp, ALU.mult)
            ve.tensor_tensor(RBL[0:1, :].rearrange("p (h g) -> p h g", g=G), PS[4][0:1, :].rearrange("p (h g) -> p h g", g=G),
                             tmp[0:1], ALU.mult).then_inc(sem("wl"), 1)
            ve.drain()

        def slice_prep_tensor(pe):
            pe.wait_ge(sem("sl_in"), N_SL)
            pe.wait_ge(sem("bd_zero"), 1)
            for k in range(2):
                for h in range(HP):
                    ins = pe.transpose(PS[k][:, h * P:(h + 1) * P], WX[:, k, h * P:(h + 1) * P], ident[:, :])
            ins.then_inc(sem("wxt_ps"), 1)
            pe.wait_ge(sem("wxt"), 1)
            for k in range(2):
                for h in range(HP):
                    pe.matmul(PS[2 + k][:, h * P:(h + 1) * P], WXT[:, h, k * P:(k + 1) * P], BDS[:, 0, :], start=True, stop=True)
            for h in range(HP):
                pe.matmul(PS[4][0:1, h * P:(h + 1) * P], BXC[:, h:h + 1], BDS[:, 0, :], start=True, stop=False, skip_group_check=True)
                ins = pe.matmul(PS[4][0:1, h * P:(h + 1) * P], ones[0:1, 0:1], RBS[0:1, :], start=False, stop=True, skip_group_check=True)
            ins.then_inc(sem("wl_ps"), 1)
            pe.wait_ge(sem("wl"), 1)
            for h in range(HP):
                pe.matmul(tok_ps(h), ZC[:, 0:P], ZC[:, 0:2 * (G + 1)], start=True, stop=False, skip_group_check=True)

        def tok_ps(h):
            return PS[6 + h // 2][:, (h % 2) * 256:(h % 2) * 256 + 2 * (G + 1)]

        def slices_tensor(pe):
            for t in range(NT):
                s = t % 2
                pe.wait_ge(sem("xn"), 3 * NT + t + 1)
                if t >= 1:
                    pe.wait_ge(sem("x4ts"), t)
                for k in range(2):
                    ins = pe.transpose(PS[0][:, k * P:(k + 1) * P], XN[:, t, k * P:(k + 1) * P], ident[:, :])
                ins.then_inc(sem("x4t"), 1)
                pe.wait_ge(sem("x4ts"), t + 1)
                if t >= 2:
                    pe.wait_ge(sem("fxs"), t - 1)
                    pe.wait_ge(sem("lgs"), t - 1)
                for c, (w, b) in enumerate(((WFX, RBF), (WL, RBL))):
                    o_ = PS[2 + c + 2 * s][:, :]
                    for k in range(2):
                        pe.matmul(o_, XT4[s][:, k, :], w[:, k, :], start=(k == 0), stop=False)
                    pe.matmul(o_, ones[0:1, :], b[0:1, :], start=False, stop=True).then_inc(sem("fxl"), 1)
                if t >= 1:
                    slice_tail(pe, t - 1)
            slice_tail(pe, NT - 1)

        def slice_tail(pe, t):
            s = t % 2
            pe.wait_ge(sem("sw"), t + 1)
            pe.wait_ge(sem("fxs"), t + 1)
            if t >= 1:
                pe.wait_ge(sem("sw_t2"), t)
            for h in range(HP):
                pe.transpose(PS[1][:, h * P:(h + 1) * P], SW[s][:, 2 * h:2 * h + 2, :].rearrange("p h g -> p (h g)"), ident[:, :])
                ins = pe.matmul(tok_ps(h), SW[s][:, 2 * h:2 * h + 2, :].rearrange("p h g -> p (h g)"),
                                FX[s][:, 2 * h:2 * h + 2, :].rearrange("p h g -> p (h g)"), start=False, stop=(t == NT - 1),
                                skip_group_check=True)
            ins.then_inc(sem("sl_mm"), 1)

        def slices_scalar(act):
            for t in range(NT):
                s = t % 2
                act.wait_ge(sem("x4t"), t + 1)
                if t >= 2:
                    act.wait_ge(sem("fxl"), 2 * (t - 1))
                act.activation(XT4[s].rearrange("p k n -> p (k n)"), PS[0][:, 0:D], ACT.Copy).then_inc(sem("x4ts"), 1)
                act.wait_ge(sem("fxl"), 2 * t + 2)
                if t >= 2:
                    act.wait_ge(sem("sl_mm"), t - 1)
                act.activation(FX[s][:, :, 0:G], PS[2 + 2 * s][:, :].rearrange("p (h c) -> p h c", c=G), ACT.Copy).then_inc(sem("fxs"), 1)
                act.wait_ge(sem("sw_sub"), t + 1)
                act.activation(SW[s], SW[s], ACT.Exp).then_inc(sem("sw_exp"), 1)
                if t >= 1:
                    slice_turned(act, t - 1)
            slice_turned(act, NT - 1)

        def slice_turned(act, t):
            act.wait_ge(sem("sl_mm"), t + 1)
            act.activation(SWT[:, t, :, :].rearrange("p h n -> p (h n)"), PS[1][:, :], ACT.Copy).then_inc(sem("sw_t2"), 1)

        def slices_vector(ve):
            for t in range(NT):
                s = t % 2
                lg = PS[3 + 2 * s][:, :].rearrange("p (h g) -> p h g", g=G)
                ve.wait_ge(sem("fxl"), 2 * t + 2)
                if t >= 2:
                    ve.wait_ge(sem("sl_mm"), t - 1)
                ve.tensor_reduce(SM[s][:, 0, :], lg, AX.X, ALU.max)
                ve.drain()
                ve.tensor_tensor(SW[s], lg, SM[s][:, 0, :].unsqueeze(2).to_broadcast([P, H2, G]), ALU.subtract).then_inc(sem("lgs"), 1)
                ve.drain()
                ve.tensor_copy(SM[s][:, 1, 0:1], SM[s][:, 0, 0:1]).then_inc(sem("sw_sub"), 1)
                ve.wait_ge(sem("sw_exp"), t + 1)
                ve.tensor_reduce(SM[s][:, 1, :], SW[s], AX.X, ALU.add)
                ve.drain()
                ve.reciprocal(SM[s][:, 2, :], SM[s][:, 1, :])
                ve.drain()
                ve.tensor_scalar(SM[s][:, 2, :], SM[s][:, 2, :], valid[:, t:t + 1], None, ALU.mult)
                ve.drain()
                ve.tensor_tensor(SW[s], SW[s], SM[s][:, 2, :].unsqueeze(2).to_broadcast([P, H2, G]), ALU.mult).then_inc(sem("sw"), 1)

        def tokens_vector(ve):
            ve.wait_ge(sem("sl_mm"), NT)
            for h in range(HP):
                tp = tok_ps(h)
                if h:
                    ve.wait_ge(sem("tk_m"), h)
                ve.memset(TOK, 0.0)
                for j in range(2):
                    r, c0 = slice(j * G, (j + 1) * G), j * (G + 1)
                    ve.tensor_scalar(SA[r, 0:1], tp[r, c0 + G:c0 + G + 1], 1.0e-5, None, ALU.add)
                ve.drain()
                ve.reciprocal(SA[:, 1:2], SA[:, 0:1])
                ve.drain()
                for j in range(2):
                    r, c0 = slice(j * G, (j + 1) * G), j * (G + 1)
                    ins = ve.tensor_scalar(TOK[r, j * G:(j + 1) * G], tp[r, c0:c0 + G], SA[r, 1:2], None, ALU.mult)
                ins.then_inc(sem("tk"), 1)
                ve.wait_ge(sem("tkt_ps"), h + 1)
                ve.tensor_copy(TOKT, PS[0][:, 0:P]).then_inc(sem("tkt"), 1)
                ve.wait_ge(sem("qkv_ps"), h + 1)
                ve.tensor_copy(QT, PS[1][:, 0:P])
                ve.tensor_copy(KT, PS[1][:, P:2 * P])
                ve.tensor_copy(VV, PS[1][:, 2 * P:3 * P]).then_inc(sem("qkv"), 1)
                ve.wait_ge(sem("sc_ps"), h + 1)
                ve.tensor_scalar(PP, BDM, BIG, -BIG, ALU.mult, ALU.add)
                ve.drain()
                ve.scalar_tensor_tensor(out=PP, in0=PS[0][:, P:2 * P], scalar=float(G) ** -0.5, in1=PP, op0=ALU.mult, op1=ALU.add)
                ve.drain()
                ve.tensor_reduce(SA[:, 2:3], PP, AX.X, ALU.max)
                ve.drain()
                ve.tensor_scalar(PP, PP, SA[:, 2:3], None, ALU.subtract).then_inc(sem("sc"), 1)
                ve.wait_ge(sem("sc_exp"), h + 1)
                ve.tensor_reduce(SA[:, 3:4], PP, AX.X, ALU.add)
                ve.drain()
                ve.reciprocal(SA[:, 4:5], SA[:, 3:4])
                ve.drain()
                ve.tensor_scalar(PP, PP, SA[:, 4:5], None, ALU.mult).then_inc(sem("pp"), 1)
                ve.wait_ge(sem("ppt_ps"), h + 1)
                ve.tensor_copy(PPT, PS[2][:, 0:P]).then_inc(sem("ppt"), 1)
                ve.wait_ge(sem("ott_ps"), h + 1)
                ve.tensor_copy(OTT, PS[2][:, P:2 * P]).then_inc(sem("ott"), 1)
                ve.wait_ge(sem("tk_m"), h + 1)
                ve.tensor_copy(MO[:, h, :], PS[3][:, 0:D]).then_inc(sem("mo"), 1)
                ve.drain()

        def tokens_scalar(act):
            for h in range(HP):
                act.wait_ge(sem("sc"), h + 1)
                act.activation(PP, PP, ACT.Exp).then_inc(sem("sc_exp"), 1)

        def tokens_tensor(pe):
            pe.wait_ge(sem("sw_t2"), NT)
            for h in range(HP):
                pe.wait_ge(sem("tk"), h + 1)
                pe.transpose(PS[0][:, 0:P], TOK, ident[:, :]).then_inc(sem("tkt_ps"), 1)
                pe.wait_ge(sem("tkt"), h + 1)
                pe.matmul(PS[1][:, 0:P], BDS[:, 1, :], TOKT, start=True, stop=True)
                pe.matmul(PS[1][:, P:2 * P], BDS[:, 2, :], TOKT, start=True, stop=True)
                pe.matmul(PS[1][:, 2 * P:3 * P], TOKT, BDS[:, 3, :], start=True, stop=True).then_inc(sem("qkv_ps"), 1)
                pe.wait_ge(sem("qkv"), h + 1)
                pe.matmul(PS[0][:, P:2 * P], QT, KT, start=True, stop=True).then_inc(sem("sc_ps"), 1)
                pe.wait_ge(sem("pp"), h + 1)
                pe.transpose(PS[2][:, 0:P], PP, ident[:, :]).then_inc(sem("ppt_ps"), 1)
                pe.wait_ge(sem("ppt"), h + 1)
                pe.matmul(PS[2][:, P:2 * P], VV, PPT, start=True, stop=True).then_inc(sem("ott_ps"), 1)
                pe.wait_ge(sem("ott"), h + 1)
                if h:
                    pe.wait_ge(sem("mo"), h)
                pe.matmul(PS[3][:, 0:D], OTT, WOUT[:, h, :], start=True, stop=True).then_inc(sem("tk_m"), 1)

        def final_tensor(pe):
            pe.wait_ge(sem("mo"), HP)
            for t in range(25):
                if t >= 4:
                    pe.wait_ge(sem("fin"), t - 3)
                y = PS[4 + t % 4][:, 0:D]
                for h in range(HP):
                    pe.matmul(y, SWT[:, t, h, :], MO[:, h, :], start=(h == 0), stop=False)
                pe.matmul(y, ones[0:1, :], RBO[0:1, :], start=False, stop=True).then_inc(sem("fin_ps"), 1)

        def final_vector(ve):
            for t in range(25):
                ve.wait_ge(sem("fin_ps"), t + 1)
                ve.tensor_tensor(X[:, t, :], X[:, t, :], PS[4 + t % 4][:, 0:D], ALU.add).then_inc(sem("fin"), 1)

        def final_sync(sp):
            for g in range(4):
                sp.wait_ge(sem("fin"), 6 * g + 6)
                sp.dma_start(out[768 * g:768 * g + 768, :].rearrange("(t p) d -> p t d", p=P), X[:, 6 * g:6 * g + 6, :]
                             ).then_inc(sem("out"), 16)
            sp.wait_ge(sem("fin"), 25)
            sp.dma_start(out[24 * P:N, :], X[0:TAIL, 24, :]).then_inc(sem("out"), 16)
            sp.wait_ge(sem("out"), 80)

        @block.sync
        def _(sp):
            loads_sync(sp)
            meta_sync(sp)
            mlp_sync(sp)
            route_sync(sp)
            experts_sync(sp)
            types_sync(sp)
            kvq_sync(sp)
            kvq_rows_sync(sp)
            for o in range(2):
                score_sync(sp, o)
                sum_sync(sp, o)
            proj_sync(sp)
            slice_sync(sp)
            final_sync(sp)

        @block.gpsimd
        def _(pool):
            consts_pool(pool)
            scatter_pool(pool)
            l0_pool(pool)
            route_pool(pool)
            expert_rows_pool(pool)
            types_pool(pool)
            kvq_rows_pool(pool)
            for o in range(2):
                score_pool(pool, o)
            agg_pool(pool)
            proj_rows_pool(pool)

        @block.scalar
        def _(act):
            ln_scalar(act, 1)
            embed_scalar(act)
            mlp_scalar(act)
            ln_scalar(act, 2)
            route_scalar(act)
            experts_scalar(act)
            ln_scalar(act, 3)
            kvq_scalar(act)
            for o in range(2):
                score_scalar(act, o)
                sum_scalar(act, o)
            proj_scalar(act)
            ln_scalar(act, 4)
            slices_scalar(act)
            tokens_scalar(act)

        @block.tensor
        def _(pe):
            rank_tensor(pe, 0)
            rank_tensor(pe, 1)
            l0_tensor(pe)
            mlp_tensor(pe)
            route_tensor(pe)
            experts_tensor(pe)
            place_tensor(pe, "t", OHt.rearrange("p t g -> p (t g)"), T1)
            kvq_tensor(pe)
            for o in range(2):
                score_tensor(pe, o)
                sum_tensor(pe, o)
            proj_tensor(pe)
            slice_prep_tensor(pe)
            slices_tensor(pe)
            tokens_tensor(pe)
            final_tensor(pe)

        @block.vector
        def _(ve):
            ve.memset(ZR, 0.0).then_inc(sem("zeros"), 1)
            ve.memset(X[:, 24:NT, :], 0.0).then_inc(sem("xpad"), 1)
            ve.memset(slot_e[0][:, :], 1 << 20)
            ve.memset(slot_e[1][:, :], 1 << 20)
            ve.wait_ge(sem("ids"), 32)
            ve.wait_ge(sem("consts"), 1)
            rank_vector(ve, 0)
            rank_vector(ve, 1)
            ve.wait_ge(sem("x_in"), 32)
            ln_vector(ve, 1)
            embed_vector(ve)
            l0_vector(ve)
            ve.drain()
            mlp_vector(ve)
            ln_vector(ve, 2)
            route_vector(ve)
            experts_vector(ve)
            expert_rows_vector(ve)
            ln_vector(ve, 3)
            types_vector(ve)
            kvq_rows_vector(ve)
            for o in range(2):
                score_vector(ve, o)
                sum_vector(ve, o)
            proj_vector(ve)
            proj_rows_vector(ve)
            ln_vector(ve, 4)
            slice_prep_vector(ve)
            slices_vector(ve)
            tokens_vector(ve)
            final_vector(ve)


_INS = ["x", "src", "dst", "edge_attr_5", "edge_weight", "node_type_19", "L0_gnn_eps", "L0_gnn_w1", "L0_gnn_b1",
        "L0_gnn_w2", "L0_gnn_b2", "L0_ffn_gate_w", "L0_ffn_gate_b", "L0_ffn_w1", "L0_ffn_b1", "L0_ffn_w2", "L0_ffn_b2",
        "L1_gnn_Wk", "L1_gnn_bk", "L1_gnn_Wq", "L1_gnn_bq", "L1_gnn_Wv", "L1_gnn_bv", "L1_gnn_Wa", "L1_gnn_ba",
        "L1_gnn_gamma", "L1_gnn_beta", "L1_gnn_w_time", "L1_gnn_b_time", "L1_ffn_W_fx", "L1_ffn_b_fx", "L1_ffn_W_x",
        "L1_ffn_b_x", "L1_ffn_W_slice", "L1_ffn_b_slice", "L1_ffn_W_q", "L1_ffn_W_k", "L1_ffn_W_v", "L1_ffn_W_out",
        "L1_ffn_b_out", "L1_ffn_temperature"]


def kernel(**inputs):
    import numpy as _np
    import concourse.bacc as _bacc
    from concourse import mybir as _mybir
    from concourse.bass_utils import run_bass_kernel_spmd as _run

    nc = _bacc.Bacc("TRN2", target_bir_lowering=False, num_devices=1)
    arrays, aps = {}, {}
    for name in _INS:
        a = _np.ascontiguousarray(inputs[name])
        arrays[f"in_{name}"] = a
        aps[name] = nc.dram_tensor(f"in_{name}", a.shape, _mybir.dt.from_np(a.dtype), kind="ExternalInput").ap()
    out = nc.dram_tensor("out_0", (N, D), _mybir.dt.float32, kind="ExternalOutput").ap()
    build(nc, aps, out)
    r = _run(nc, [arrays], core_ids=[0])
    return r.results[0]["out_0"]
```
